# Optimizing a Trainium2 kernel written in Bass

```python
import numpy as np
import jax
import jax.numpy as jnp

def _softmax(x, axis=-1):
    return jax.nn.softmax(x, axis=axis)

def _gelu(x):
    return jax.nn.gelu(x, approximate=True)

def _silu(x):
    return jax.nn.silu(x)

def _sigmoid(x):
    return jax.nn.sigmoid(x)

def _layernorm(x, axis=-1, eps=1e-05):
    m = jnp.mean(x, axis=axis, keepdims=True)
    v = jnp.var(x, axis=axis, keepdims=True)
    return (x - m) / jnp.sqrt(v + eps)

def _scatter_add(tgt, idx, src, axis=0):
    return tgt.at[idx].add(src)

def _segment_sum(src, seg, n):
    return jax.ops.segment_sum(src, seg, n)
kernel_name = 'mk_decoder_preln_d1_seqx_r2_a2bd81'

def setup_inputs(seed: int=0):
    np.random.seed(seed)
    _w = jnp.asarray

    def _rec_inputs():
        import jax
        import jax.numpy as jnp
        _rk = jax.random.key(seed)
        x = -0.0002928 + 1 * jax.random.normal(jax.random.fold_in(_rk, 1), (16, 512, 1024), jnp.float32)
        _lenS = 512 - jax.random.randint(jax.random.fold_in(_rk, 7), (16,), 0, max(1, 512 // 4) + 1, jnp.int32)
        _lenS2 = 512 - jax.random.randint(jax.random.fold_in(_rk, 8), (16,), 0, max(1, 512 // 4) + 1, jnp.int32)
        fside_S2_0 = -0.00337071 + 1.01897 * jax.random.normal(jax.random.fold_in(_rk, 11), (512,), jnp.float32)
        _ctx_2048P = jax.random.normal(jax.random.fold_in(_rk, 12), (16, 16, 1024), jnp.float32)
        _ctx_2048c = jax.random.dirichlet(jax.random.fold_in(_rk, 512), 0.3 * jnp.ones((16,), jnp.float32), (16, 512))
        _ctx_2048t = jnp.einsum('bsk,bkd->bsd', _ctx_2048c, _ctx_2048P)
        _ctx_2048t = _ctx_2048t * jax.lax.rsqrt(jnp.mean(jnp.square(_ctx_2048t)) + 1e-12) * 0.953939
        ctx_2048 = 0.000675642 + 1.00031 * (_ctx_2048t + 0.3 * jax.random.normal(jax.random.fold_in(_rk, 612), (16, 512, 1024), jnp.float32))
        return (x, fside_S2_0, ctx_2048)
    x, fside_S2_0, ctx_2048 = _rec_inputs()

    def _L0_attn_setup():
        import jax, jax.numpy as jnp
        import numpy as np
        D_MODEL = 1024
        N_QUERY = 4
        N_HEAD = 8
        D_HEAD = D_MODEL // (N_QUERY * N_HEAD)
        D_KV = D_HEAD * N_HEAD
        BATCH, SEQ = (2, 1024)
        key = jax.random.key(seed)
        ks = jax.random.split(key, 5)
        w_scale = 1.0 / np.sqrt(D_MODEL).astype(np.float32)
        x = jax.random.normal(ks[0], (BATCH, SEQ, D_MODEL), jnp.float32)
        Wq = jax.random.normal(ks[1], (D_MODEL, D_MODEL), jnp.float32) * w_scale
        Wk = jax.random.normal(ks[2], (D_KV, D_MODEL), jnp.float32) * w_scale
        Wv = jax.random.normal(ks[3], (D_KV, D_MODEL), jnp.float32) * w_scale
        memory = jax.random.normal(ks[4], (D_KV, D_KV), jnp.float32) * 0.02
        memory_norm = jnp.ones((D_KV, 1), jnp.float32)
        memory_weight = jnp.ones((1,), jnp.float32)
        return dict(x=x, Wq=Wq, Wk=Wk, Wv=Wv, memory=memory, memory_norm=memory_norm, memory_weight=memory_weight)
    _L0_attn_all = _L0_attn_setup()
    _L0_attn_in = {k: v for k, v in _L0_attn_all.items() if k in ('Wq', 'Wk', 'Wv', 'memory', 'memory_norm', 'memory_weight')}
    del _L0_attn_all

    def _L0_xattn_setup():
        import jax, jax.numpy as jnp
        import numpy as np
        key = jax.random.key(seed)
        ks = jax.random.split(key, 5)
        B, D, L, NH = (2, 512, 1024, 8)
        H = D // NH
        return {'v': jax.random.normal(ks[0], (B, D, L), jnp.float32), 'k': jax.random.normal(ks[1], (H, L), jnp.float32) * 0.1, 'bias': jax.random.normal(ks[2], (D,), jnp.float32), 'x1': jax.random.normal(ks[3], (B, D, L), jnp.float32), 'x2': jax.random.normal(ks[4], (B, D, L), jnp.float32), 'num_heads': NH}
    _L0_xattn_all = _L0_xattn_setup()
    _L0_xattn_in = {k: v for k, v in _L0_xattn_all.items() if k in ('k',)}
    del _L0_xattn_all

    def _L0_ffn_setup():
        import jax, jax.numpy as jnp
        import numpy as np
        FP8_MAX = 448.0
        SCALE_EPS = 1e-07
        key = jax.random.key(seed)
        k1, k2, k3 = jax.random.split(key, 3)
        in_f, out_f = (1024, 1024)
        x = jax.random.normal(k1, (4, 2048, in_f), dtype=jnp.float32)
        w_fp32 = jax.random.normal(k2, (out_f, in_f), dtype=jnp.float32) * (1.0 / np.sqrt(in_f))
        weight = w_fp32.astype(jnp.float8_e4m3fn).astype(jnp.float32)
        weight_scale = jnp.ones((), dtype=jnp.float32)
        bound = 1.0 / np.sqrt(in_f)
        bias = jax.random.uniform(k3, (out_f,), dtype=jnp.float32, minval=-bound, maxval=bound)
        return {'x': x, 'weight': weight, 'weight_scale': weight_scale, 'bias': bias}
    _L0_ffn_all = _L0_ffn_setup()
    _L0_ffn_in = {k: v for k, v in _L0_ffn_all.items() if k in ('weight', 'weight_scale', 'bias')}
    del _L0_ffn_all
    return {'x': x, 'fside_S2_0': fside_S2_0, 'ctx_2048': ctx_2048, 'L0_attn_Wq': _L0_attn_in['Wq'], 'L0_attn_Wk': _L0_attn_in['Wk'], 'L0_attn_Wv': _L0_attn_in['Wv'], 'L0_attn_memory': _L0_attn_in['memory'], 'L0_attn_memory_norm': _L0_attn_in['memory_norm'], 'L0_attn_memory_weight': _L0_attn_in['memory_weight'], 'L0_xattn_k': _L0_xattn_in['k'], 'L0_ffn_weight': _L0_ffn_in['weight'], 'L0_ffn_weight_scale': _L0_ffn_in['weight_scale'], 'L0_ffn_bias': _L0_ffn_in['bias']}

def reference(x, fside_S2_0, ctx_2048, L0_attn_Wq, L0_attn_Wk, L0_attn_Wv, L0_attn_memory, L0_attn_memory_norm, L0_attn_memory_weight, L0_xattn_k, L0_ffn_weight, L0_ffn_weight_scale, L0_ffn_bias):
    import jax
    import jax.numpy as jnp

    def _L0_attn_ref(x, Wq, Wk, Wv, memory, memory_norm, memory_weight):
        import jax, jax.numpy as jnp
        import numpy as np
        D_MODEL = 1024
        N_QUERY = 4
        N_HEAD = 8
        D_HEAD = D_MODEL // (N_QUERY * N_HEAD)
        D_KV = D_HEAD * N_HEAD
        BATCH, SEQ = (2, 1024)
        b, s, d = x.shape
        q = x @ Wq.T
        k = x @ Wk.T
        v = x @ Wv.T
        qh = q.reshape(b, s, N_QUERY, N_HEAD, D_HEAD)
        kh = k.reshape(b, s, N_HEAD, D_HEAD)
        vh = v.reshape(b, s, N_HEAD, D_HEAD)
        scale = np.float32(1.0 / np.sqrt(np.float32(D_HEAD)))
        scores = jnp.einsum('bsqhd,bthd->bqhst', qh, kh) * scale
        probs = jax.nn.softmax(scores, axis=-1)
        a_dot = jnp.einsum('bqhst,bthd->bsqhd', probs, vh)
        a_dot = a_dot.reshape(b, s, N_QUERY * N_HEAD, D_HEAD)
        sigma_q = jax.nn.elu(q.reshape(b, s, N_QUERY, D_KV))
        a_mem = sigma_q @ memory / (sigma_q @ memory_norm)
        a_mem = a_mem.reshape(b, s, N_QUERY * N_HEAD, D_HEAD)
        w = jax.nn.sigmoid(memory_weight)
        out = a_dot * (1.0 - w) + a_mem * w
        return out.reshape(b, s, D_MODEL)

    def _L0_xattn_ref(v, k, bias, x1, x2, num_heads):
        import jax, jax.numpy as jnp
        import numpy as np
        B, D, L = v.shape
        H = D // num_heads
        fft_size = 2 * L
        vr = v.reshape(B, H, num_heads, L)
        x1r = x1.reshape(B, H, num_heads, L)
        x2r = x2.reshape(B, H, num_heads, L)
        kv = vr[:, :, :, None, :] * x2r[:, :, None, :, :]
        k_f = jnp.fft.rfft(k.astype(jnp.float32), n=fft_size)
        y = jnp.fft.irfft(jnp.fft.rfft(kv, n=fft_size) * k_f[None, :, None, None, :], n=fft_size)[..., :L]
        skip = bias.astype(jnp.float32).reshape(H, num_heads)[None, :, :, None, None]
        y = y + kv * skip
        out = jnp.einsum('bhijl,bhil->bhjl', y, x1r)
        return out.reshape(B, D, L)

    def _L0_ffn_ref(x, weight, weight_scale, bias):
        import jax, jax.numpy as jnp
        import numpy as np
        FP8_MAX = 448.0
        SCALE_EPS = 1e-07
        scale = jnp.maximum(jnp.max(jnp.abs(x)) / FP8_MAX, SCALE_EPS)
        x_q = (x / scale).astype(jnp.float8_e4m3fn).astype(jnp.float32)
        w = weight * weight_scale
        out = jnp.einsum('bsi,oi->bso', x_q, w) + bias
        return out
    x = x + _L0_attn_ref(_layernorm(x, axis=-1), L0_attn_Wq, L0_attn_Wk, L0_attn_Wv, L0_attn_memory, L0_attn_memory_norm, L0_attn_memory_weight)
    x = x + _L0_xattn_ref(_layernorm(x, axis=-1), L0_xattn_k, fside_S2_0, ctx_2048, ctx_2048, 8)
    x = x + _L0_ffn_ref(_layernorm(x, axis=-1), L0_ffn_weight, L0_ffn_weight_scale, L0_ffn_bias)
    return x

_drawn_inputs = setup_inputs


def setup_inputs(seed=0):
    import zlib

    import numpy as np

    out = dict(_drawn_inputs(seed))
    spreads = {'L0_attn_memory_norm': (1.0, 0.6)}
    factors = {'L0_attn_memory': 3.144, 'L0_ffn_bias': 64.0}
    for name, (base, spread) in spreads.items():
        noise = np.random.default_rng([zlib.crc32(name.encode()), seed]).standard_normal(out[name].shape)
        drawn = base * np.exp(spread * noise) if base else spread * noise
        out[name] = jnp.asarray(drawn.astype(out[name].dtype))
    for name, factor in factors.items():
        out[name] = (out[name] * factor).astype(out[name].dtype)
    return out
```

```python
import concourse.bass as bass
from concourse import mybir
from contextlib import ExitStack

P = 128
F32 = mybir.dt.float32
F16 = mybir.dt.float16
U32 = mybir.dt.uint32
ALU = mybir.AluOpType
ACT = mybir.ActivationFunctionType
AX_X = mybir.AxisListType.X

B, S, D = 16, 512, 1024
NQ, NH, DH = 4, 8, 32
DKV = NH * DH
E_ALL = D + 2 * DKV
ND = D // P
NS = S // P
NG = NQ * NH // 4
HX = 8
NHC = S // HX
LN_EPS = 1e-5

XN_S = 16.0
W_S = 256.0
QK_S = 16.0
T_S = 256.0
U_S = 16.0


def wait(eng, sem, value):
    if not (isinstance(value, int) and value <= 0):
        eng.wait_ge(sem, value)


def wait_on_cell(nc, cell, eng, sem, value):
    wait(eng, sem, value)
    nc.vector.memset(cell, 0.0)


def loop_first_last(eng, n, first, body):
    for i in range(first):
        body(i, i > 0, True)
    if n - 1 > first:
        with eng.Fori(first, n - 1) as i:
            body(i, True, True)
    body(n - 1, True, False)


class Count:

    def __init__(self, base=0):
        self.base, self.n = base, 0

    def next(self):
        v = self.base + self.n
        self.n += 1
        return v

    def now(self):
        return self.base + self.n


def s1_chunk_after(stage):
    order = ["q2", "q3", "q4", "q5", "q6", "q7", "v0", "v1"]
    return order.index(stage) if stage in order else None


PROJ = ["k0", "k1", "q0", "q1", "q2", "q3", "am0", "q4", "q5", "am1", "q6", "q7", "am2", "v0", "v1"]
def fill_plan(has_next):
    n, at = 0, {}
    for stage in PROJ:
        n += 4 if stage[:2] == "am" else 1
        at[stage] = n
        n += 4 * (s1_chunk_after(stage) is not None)
    n += 1
    at["rows", 0] = n
    for g in range(NG):
        for t in range(NS):
            if t == 0 and g + 1 < NG:
                n += 1
                at["rows", g + 1] = n
            n += 4 * (g + 2 < NG)
            if has_next and (g, t) in XT_AT:
                n += 1
                at["xt"] = n
            n += t == 2 and g > 0
    n += 4
    at["am3"] = n
    at["all"] = n + 1
    return at


XT_AT = {(2, 1): 0, (3, 1): 1, (4, 1): 2, (5, 1): 3, (6, 1): 4, (6, 3): 5, (7, 1): 6, (7, 3): 7}


def attention_phase(nc, x, Wq, Wk, Wv, memory, memory_norm, memory_weight, ident_in, x1, nb):
    with ExitStack() as ctx:
        def sb(name, shape, dt=F32):
            return ctx.enter_context(nc.sbuf_tensor(name, shape, dt))

        def sem(name):
            return ctx.enter_context(nc.semaphore(name))

        ident = sb("a_ident", [P, P])
        w_hi = sb("a_w_hi", [P, ND, E_ALL], F16)
        w_lo = sb("a_w_lo", [P, ND, E_ALL], F16)
        xin = sb("a_xin", [P, NS, D])
        xres = sb("a_xres", [P, NS, D])
        xT_hi = sb("a_xT_hi", [P, ND, S], F16)
        xT_lo = sb("a_xT_lo", [P, ND, S], F16)
        qk_hi = sb("a_qk_hi", [P, 4, S], F16)
        qk_lo = sb("a_qk_lo", [P, 4, S], F16)
        qs = sb("a_qs", [P, NQ * NH, S], F16)
        ks = sb("a_ks", [P, NH, S], F16)
        v = sb("a_v", [P, NS, DKV])
        probs = sb("a_probs", [P, 2, 4, S])
        rsum = sb("a_rsum", [P, S])
        oT = sb("a_oT", [P, 2, S])
        sq = sb("a_sq", [P, 4, S])
        eq = sb("a_eq", [P, 2, S])
        rq = sb("a_rq", [P, 2, S])
        mem = sb("a_mem", [P, 2, DKV + 1])
        ones = sb("a_ones", [P, DH])
        maxima = sb("a_max", [P, 2, 4, NS])
        mrow = sb("a_mrow", [16, 2, P], F16)
        stats = sb("a_stats", [P, NS, 2, 6])
        mv = sb("a_mv", [P, NS, 2])
        veps = sb("a_veps", [P, NS])
        rstd = sb("a_rstd", [P, NS])
        cell = sb("a_cell", [P, 1])
        mhalf = sb("a_mhalf", [P, NS])
        mixw = sb("a_mixw", [P, 8])
        den = sb("a_den", [P, 2, 2])

        psum = [ctx.enter_context(nc.psum_tensor(f"a_ps{i}", [P, 512], F32)) for i in range(4)]
        misc, ps_av, ps_sum = psum[0:2], psum[2], psum[3]
        score = [ctx.enter_context(nc.psum_tensor(f"a_score{i}", [P, 2, S], F32)) for i in range(2)]

        const_in = sem("a_const_in")
        w_in = [sem(f"a_w_in{i}") for i in range(2)]
        w_done = sem("a_w_done")
        xin_in = sem("a_xin_in")
        xres_in = sem("a_xres_in")
        x1_out = sem("a_x1_out")
        ready = sem("a_ready")
        filled = sem("a_filled")
        freed = sem("a_freed")
        hi_done = sem("a_hi_done")
        eq_done = sem("a_eq_done")
        sq_done = sem("a_sq_done")
        stacked = [sem(f"a_stacked{i}") for i in range(4)]
        ms_in = [sem(f"a_ms_in{i}") for i in range(2)]
        s2_filled = sem("a_s2_filled")
        exp_done = sem("a_exp_done")
        av_tick = sem("a_av_tick")
        av_done = sem("a_av_done")
        oT_done = sem("a_oT_done")
        stats_done = sem("a_stats_done")
        rstd_done = sem("a_rstd_done")
        norm_done = sem("a_norm_done")
        dve_step = sem("a_dve_step")
        mix1 = sem("a_mix1")
        w_filled = sem("a_w_filled")
        w_hi_done = sem("a_w_hi_done")
        elu_step = sem("a_elu_step")
        bn_step = sem("a_bn_step")
        aggr_step = sem("a_aggr_step")
        mem_step = sem("a_mem_step")
        quot_step = sem("a_quot_step")

        AT = fill_plan(True)
        FILLS = AT["all"]
        TILES = [s for s in PROJ if s[0] in "kq"]
        HIS = 2 + 8 + 8
        N_W = E_ALL // P

        block = ctx.enter_context(nc.Block())

        def w_rows(n):
            if n < ND:
                return Wq[n * P:(n + 1) * P, :]
            if n < ND + 2:
                return Wk[(n - ND) * P:(n - ND + 1) * P, :]
            return Wv[(n - ND - 2) * P:(n - ND - 1) * P, :]

        @block.sync
        def _(sp):
            sp.dma_start(ident[:, :], ident_in).then_inc(const_in, 16)
            sp.dma_start(mixw[:, 0:1], memory_weight.rearrange("(a n) -> a n", a=1).to_broadcast([P, 1])).then_inc(const_in, 16)
            for c in range(2):
                sp.dma_start(mem[:, c, 0:DKV], memory[c * P:(c + 1) * P, :]).then_inc(const_in, 16)
                sp.dma_start(mem[:, c, DKV:DKV + 1], memory_norm[c * P:(c + 1) * P, :]).then_inc(const_in, 16)
            for n in range(N_W):
                wait(sp, w_done, 2 * (n - 1))
                sp.dma_start(xres[:, n % 2, :], w_rows(n)).then_inc(w_in[n % 2], 16)
            sp.dma_start(xin[:, :, :], x[0].rearrange("(t p) d -> p t d", p=P)).then_inc(xin_in, 16)
            sp.wait_ge(w_done, 2 * N_W)

            def batch(b, has_prev, has_next):
                if has_next:
                    sp.wait_ge(filled, b * FILLS + ND - (FILLS - AT["xt"]) if has_prev else ND)
                    sp.dma_start(xin[:, :, :], x[b + 1].rearrange("(t p) d -> p t d", p=P)).then_inc(xin_in, 16)
                if has_prev:
                    sp.wait_ge(x1_out, 16 * b)
                sp.dma_start(xres[:, :, :], x[b].rearrange("(t p) d -> p t d", p=P)).then_inc(xres_in, 16)
                for n in range(10):
                    sp.wait_ge(freed, b * FILLS + ND + AT[TILES[n]])
                    for j in range(4):
                        rows = slice(DH * j, DH * j + DH)
                        hi, lo = qk_hi[rows, n % 4, :], qk_lo[rows, n % 4, :]
                        if n < 2:
                            dst, mid, last = ks[:, 4 * n + j, :], hi, lo
                        else:
                            dst, mid, last = qs[:, 4 * (n - 2) + j, :], lo, hi
                        for at, half in ((0, hi), (DH, mid), (2 * DH, last)):
                            sp.dma_start(dst[at:at + DH], half).then_inc(stacked[n % 4], 16)
                for g in range(NG):
                    sp.wait_ge(freed, b * FILLS + ND + fill_plan(has_next)["rows", g])
                    sp.dma_start(qs[3 * DH:3 * DH + 1, 4 * g:4 * g + 4, :], mrow[:, g % 2, :]).then_inc(ms_in[g % 2], 16)
                sp.wait_ge(freed, b * FILLS + ND + FILLS - (0 if has_next else ND))
                sp.dma_start(x1[b].rearrange("(t p) d -> p t d", p=P), xres[:, :, :]).then_inc(x1_out, 16)

            loop_first_last(sp, nb, 1, batch)
            sp.wait_ge(x1_out, 16 * nb)


        @block.gpsimd
        def _(pool):
            nc.gpsimd.memset(ones[:, :], 1.0).then_inc(ready, 1)
            nc.gpsimd.memset(mhalf[:, :], -0.5).then_inc(ready, 1)
            pool.wait_ge(ready, 2)
            nc.gpsimd.memset(ks[3 * DH:3 * DH + 1, :, :], QK_S * QK_S).then_inc(ready, 1)
            pool.wait_ge(ready, 3)

            def norm_scale(n):
                pool.wait_ge(stats_done, n + 1)
                nc.gpsimd.tensor_tensor(rstd[:, :], veps[:, :], mhalf[:, :], ALU.pow).then_inc(rstd_done, 1)

            norm_scale(0)

            def batch(b, has_prev, has_next):
                for t in range(8):
                    n = b * 8 + t
                    pool.wait_ge(elu_step, n + 1)
                    if t >= 4:
                        pool.wait_ge(filled, b * FILLS + ND + AT[f"am{t // 2 - 2}"])
                    elif has_prev:
                        pool.wait_ge(filled, b * FILLS + ND - (FILLS - AT[f"am{t // 2 + 2}"]))
                    nc.gpsimd.tensor_tensor(sq[:, t % 4, :], eq[:, t % 2, :], rq[:, t % 2, :], ALU.add).then_inc(sq_done, 1)
                if has_next:
                    norm_scale(b + 1)

            loop_first_last(pool, nb, 1, batch)

        @block.tensor
        def _(pe):
            pe.wait_ge(const_in, 16 * 6)
            pe.wait_ge(ready, 3)
            for n in range(N_W):
                pe.wait_ge(w_in[n % 2], 16 * (n // 2 + 1))
                for c in range(2):
                    wait(pe, w_done, 2 * n + c - 1)
                    for k in range(4):
                        m = nc.tensor.transpose(misc[c][:, k * P:(k + 1) * P], xres[:, n % 2, (4 * c + k) * P:(4 * c + k + 1) * P], ident[:, :])
                    m.then_inc(w_filled, 1)
            pe.wait_ge(w_done, 2 * N_W)

            def fill(f):
                n = f.next()
                wait(pe, freed, n - 1)
                return misc[(f.n - 1) % 2]

            def xn_transposes(f, kk):
                bank = fill(f)
                for st in range(NS):
                    m = nc.tensor.transpose(bank[:, st * P:(st + 1) * P], xin[:, st, kk * P:(kk + 1) * P], ident[:, :])
                m.then_inc(filled, 1)

            def three(out, lhs_hi, lhs_lo, rhs_hi, rhs_lo, first, last):
                nc.tensor.matmul(out, lhs_hi, rhs_hi, start=first, stop=False)
                nc.tensor.matmul(out, lhs_hi, rhs_lo, start=False, stop=False)
                return nc.tensor.matmul(out, lhs_lo, rhs_hi, start=False, stop=last)

            f0 = Count()
            pe.wait_ge(norm_done, NS)
            for kk in range(ND):
                xn_transposes(f0, kk)

            def batch(b, has_prev, has_next):
                f = Count(b * FILLS + ND)
                scored = {}
                pe.wait_ge(hi_done, (b + 1) * 8 + b * 10)
                if not has_prev:
                    pe.wait_ge(freed, ND)

                def score_max(g, chunk):
                    if chunk == 0:
                        if g == 0:
                            for n in range(2):
                                pe.wait_ge(stacked[n], stack_count(b, n))
                        n = g + 2
                        pe.wait_ge(stacked[n % 4], stack_count(b, n))
                    for c in range(4):
                        j = chunk
                        bank = fill(f)
                        nc.tensor.matmul(bank[:, :], qs[0:3 * DH, 4 * g + j, c * P:(c + 1) * P], ks[0:3 * DH, (g % 2) * 4 + j, :],
                                         start=True, stop=True).then_inc(filled, 1)
                    scored[g] = f.n

                def mem_products(qq):
                    pe.wait_ge(sq_done, b * 8 + 2 * qq + 2)
                    for st in range(NS):
                        bank = fill(f)
                        for c in range(2):
                            m = nc.tensor.matmul(bank[:, 0:DKV + 1], sq[:, (2 * qq + c) % 4, st * P:(st + 1) * P], mem[:, c, :],
                                                 start=(c == 0), stop=(c == 1))
                        m.then_inc(filled, 1)

                def max_rows(g):
                    pe.wait_ge(freed, f.base + scored[g])
                    bank = fill(f)
                    nc.tensor.matmul(bank[0:16, 0:P], maxima[:, g % 2, :, :].rearrange("p j s -> p (j s)"), ident[:, :],
                                     start=True, stop=True).then_inc(filled, 1)

                for stage in PROJ:
                    if stage[:2] == "am":
                        mem_products(int(stage[2]))
                    elif stage[0] == "v":
                        bank = fill(f)
                        for s in range(2):
                            st = 2 * int(stage[1]) + s
                            for kk in range(ND):
                                m = three(bank[:, s * DKV:(s + 1) * DKV], xT_hi[:, kk, st * P:(st + 1) * P], xT_lo[:, kk, st * P:(st + 1) * P],
                                          w_hi[:, kk, D + DKV:E_ALL], w_lo[:, kk, D + DKV:E_ALL], kk == 0, kk == ND - 1)
                        m.then_inc(filled, 1)
                    else:
                        e0 = (D if stage[0] == "k" else 0) + int(stage[1]) * P
                        bank = fill(f)
                        for kk in range(ND):
                            m = three(bank[:, :], w_hi[:, kk, e0:e0 + P], w_lo[:, kk, e0:e0 + P], xT_hi[:, kk, :], xT_lo[:, kk, :],
                                      kk == 0, kk == ND - 1)
                        m.then_inc(filled, 1)
                    c = s1_chunk_after(stage)
                    if c is not None:
                        score_max(c // 4, c % 4)
                max_rows(0)

                def scores(g, t, pair):
                    n = b * 64 + (g * 4 + t) * 2 + pair
                    wait(pe, exp_done, n - 1)
                    if t == 0 and pair == 0:
                        pe.wait_ge(ms_in[g % 2], 16 * (b * 4 + g // 2 + 1))
                    for i in range(2):
                        j = 2 * pair + i
                        m = nc.tensor.matmul(score[pair][:, i, :], ks[0:3 * DH + 1, (g % 2) * 4 + j, t * P:(t + 1) * P],
                                             qs[0:3 * DH + 1, 4 * g + j, :], start=True, stop=True)
                    m.then_inc(s2_filled, 1)

                def weighted(g, t):
                    tick = g * 4 + t
                    pe.wait_ge(exp_done, b * 64 + 2 * tick + 2)
                    if t == 0:
                        wait(pe, oT_done, b * NG + g)
                    for j in range(4):
                        rows = slice(DH * j, DH * j + DH)
                        head = (g % 2) * 4 + j
                        nc.tensor.matmul(ps_av[rows, :], v[:, t, head * DH:(head + 1) * DH], probs[:, tick % 2, j, :], start=(t == 0), stop=(t == 3))
                    for j in range(4):
                        rows = slice(DH * j, DH * j + DH)
                        m = nc.tensor.matmul(ps_sum[rows, :], ones[:, :], probs[:, tick % 2, j, :], start=(t == 0), stop=(t == 3))
                    m.then_inc(av_done if t == 3 else av_tick, 1)

                def out_transposes(g):
                    pe.wait_ge(oT_done, b * NG + g + 1)
                    bank = fill(f)
                    for st in range(NS):
                        m = nc.tensor.transpose(bank[:, st * P:(st + 1) * P], oT[:, g % 2, st * P:(st + 1) * P], ident[:, :])
                    m.then_inc(filled, 1)

                for g in range(NG):
                    for t in range(NS):
                        scores(g, t, 0)
                        scores(g, t, 1)
                        if t == 0 and g + 1 < NG:
                            max_rows(g + 1)
                        if g + 2 < NG:
                            score_max(g + 2, t)
                        if (g, t) != (0, 0):
                            weighted(*((g, t - 1) if t else (g - 1, 3)))
                        if has_next and (g, t) in XT_AT:
                            kk = XT_AT[g, t]
                            if kk == 0:
                                pe.wait_ge(norm_done, (b + 2) * NS)
                            xn_transposes(f, kk)
                        if t == 2 and g > 0:
                            out_transposes(g - 1)
                weighted(NG - 1, 3)
                mem_products(3)
                out_transposes(NG - 1)

            def stack_count(b, n):
                uses = [3, 3, 2, 2]
                return 16 * 12 * (b * uses[n % 4] + n // 4 + 1)

            loop_first_last(pe, nb, 1, batch)

        @block.scalar
        def _(act):
            act.wait_ge(const_in, 16 * 6)
            nc.scalar.activation(mixw[:, 1:2], mixw[:, 0:1], ACT.Exp, scale=-1.0).then_inc(mix1, 1)
            for n in range(2 * N_W):
                act.wait_ge(w_filled, n + 1)
                dst = w_hi[:, 4 * (n % 2):4 * (n % 2) + 4, (n // 2) * P:(n // 2 + 1) * P]
                nc.scalar.activation(dst, misc[n % 2][:, :].rearrange("p (k e) -> p k e", k=4), ACT.Copy, scale=W_S).then_inc(w_hi_done, 1)

            def xn_hi(n_fill, slot, kk):
                act.wait_ge(filled, n_fill + 1)
                nc.scalar.activation(xT_hi[:, kk, :], misc[slot][:, :], ACT.Copy, scale=XN_S).then_inc(hi_done, 1)

            for kk in range(ND):
                xn_hi(kk, kk % 2, kk)

            def batch(b, has_prev, has_next):
                f = Count(b * FILLS + ND)
                for stage in PROJ:
                    if stage[0] in "kq":
                        n = f.next()
                        bank = misc[(f.n - 1) % 2]
                        tile = int(stage[1]) + (2 if stage[0] == "q" else 0)
                        act.wait_ge(filled, n + 1)
                        if tile >= 4:
                            act.wait_ge(stacked[tile % 4], stack_count(b, tile - 4))
                        elif has_prev:
                            act.wait_ge(stacked[tile % 4], prev_count(b, tile % 4))
                        nc.scalar.activation(qk_hi[:, tile % 4, :], bank[:, :], ACT.Copy, scale=QK_S / (XN_S * W_S)).then_inc(hi_done, 1)
                        if stage[0] == "q":
                            t = tile - 2
                            wait(act, sq_done, b * 8 + t - 1)
                            nc.scalar.activation(eq[:, t % 2, :], bank[:, :], ACT.Exp, scale=1.0 / (XN_S * W_S))
                            nc.scalar.activation(rq[:, t % 2, :], bank[:, :], ACT.Relu, scale=1.0 / (XN_S * W_S)).then_inc(eq_done, 1)
                    elif stage[0] == "v":
                        f.next()
                    else:
                        f.n += 4
                    if s1_chunk_after(stage) is not None:
                        f.n += 4
                f.n += 1
                for g in range(NG):
                    for t in range(NS):
                        tick = g * 4 + t
                        for pair in range(2):
                            n = b * 64 + 2 * tick + pair
                            act.wait_ge(s2_filled, n + 1)
                            if pair == 0:
                                if tick >= 2:
                                    back = tick - 2
                                    if back % 4 == 3:
                                        act.wait_ge(av_done, b * NG + back // 4 + 1)
                                    else:
                                        act.wait_ge(av_tick, b * NG * 3 + (back // 4) * 3 + back % 4 + 1)
                                elif has_prev:
                                    act.wait_ge(av_done, b * NG)
                            nc.scalar.activation(probs[:, tick % 2, 2 * pair:2 * pair + 2, :], score[pair][:, :, :], ACT.Exp,
                                                 scale=DH ** -0.5 / (QK_S * QK_S)).then_inc(exp_done, 1)
                        if t == 0 and g + 1 < NG:
                            f.n += 1
                        if g + 2 < NG:
                            f.n += 4
                        if has_next and (g, t) in XT_AT:
                            n = f.next()
                            xn_hi(n, (f.n - 1) % 2, XT_AT[g, t])
                        if t == 2 and g > 0:
                            f.n += 1

            def stack_count(b, n):
                uses = [3, 3, 2, 2]
                return 16 * 12 * (b * uses[n % 4] + n // 4 + 1)

            def prev_count(b, n):
                return 16 * 12 * b * [3, 3, 2, 2][n]

            loop_first_last(act, nb, 1, batch)

        @block.vector
        def _(dve):
            dve.wait_ge(mix1, 1)
            nc.vector.tensor_scalar(mixw[:, 2:3], mixw[:, 1:2], 1.0, None, ALU.add).then_inc(dve_step, 1)
            dve.wait_ge(dve_step, 1)
            nc.vector.reciprocal(mixw[:, 3:4], mixw[:, 2:3]).then_inc(dve_step, 1)
            dve.wait_ge(dve_step, 2)
            nc.vector.tensor_scalar(mixw[:, 4:5], mixw[:, 3:4], -1.0, 1.0, ALU.mult, ALU.add).then_inc(dve_step, 1)
            dve.wait_ge(dve_step, 3)
            for n in range(2 * N_W):
                dve.wait_ge(w_hi_done, n + 1)
                rows = (slice(None), slice(4 * (n % 2), 4 * (n % 2) + 4), slice((n // 2) * P, (n // 2 + 1) * P))
                nc.vector.scalar_tensor_tensor(out=w_lo[rows], in0=misc[n % 2][:, :].rearrange("p (k e) -> p k e", k=4), scalar=W_S,
                                               in1=w_hi[rows], op0=ALU.mult, op1=ALU.subtract).then_inc(w_done, 1)

            def bn(n, st):
                if st == 0:
                    dve.wait_ge(xin_in, 16 * (n + 1))
                for h in range(2):
                    nc.vector.bn_stats(out=stats[:, st, h, :], in_=xin[:, st, h * 512:(h + 1) * 512]).then_inc(bn_step, 1)
                wait_on_cell(nc, cell[:, :], dve, bn_step, n * 2 * NS + 2 * st + 2)
                nc.vector.bn_aggr(out=mv[:, st, :], in_=stats[:, st, :, :]).then_inc(aggr_step, 1)
                if st == NS - 1:
                    dve.wait_ge(aggr_step, n * NS + NS)
                    nc.vector.tensor_scalar(veps[:, :], mv[:, :, 1], LN_EPS, None, ALU.add).then_inc(stats_done, 1)

            def normalise(n, st):
                dve.wait_ge(rstd_done, n + 1)
                nc.vector.tensor_scalar(xin[:, st, :], xin[:, st, :], mv[:, st, 0:1], rstd[:, st:st + 1], ALU.subtract, ALU.mult).then_inc(norm_done, 1)

            def xn_lo(n_fill, n_hi, slot, kk):
                dve.wait_ge(hi_done, n_hi + 1)
                nc.vector.scalar_tensor_tensor(out=xT_lo[:, kk, :], in0=misc[slot][:, :], scalar=XN_S, in1=xT_hi[:, kk, :],
                                               op0=ALU.mult, op1=ALU.subtract).then_inc(freed, 1)

            for st in range(NS):
                bn(0, st)
            for st in range(NS):
                normalise(0, st)
            for kk in range(ND):
                xn_lo(kk, kk, kk % 2, kk)

            def batch(b, has_prev, has_next):
                f = Count(b * FILLS + ND)
                his = Count(b * HIS + ND)

                def bank_ready():
                    n = f.next()
                    dve.wait_ge(filled, n + 1)
                    return misc[(f.n - 1) % 2]

                def maxima_of(g, chunk):
                    for c in range(4):
                        bank = bank_ready()
                        nc.vector.reduce_max(maxima[:, g % 2, chunk, c:c + 1], bank[:, :], AX_X).then_inc(freed, 1)

                def mem_mix(qq):
                    for st in range(NS):
                        bank = bank_ready()
                        k = Count(b * 32 + (qq * 4 + st) * 2)
                        nc.vector.reciprocal(den[:, st % 2, 0:1], bank[:, DKV:DKV + 1]).then_inc(mem_step, 1)
                        dve.wait_ge(mem_step, k.next() + 1)
                        nc.vector.tensor_scalar(den[:, st % 2, 1:2], den[:, st % 2, 0:1], mixw[:, 3:4], None, ALU.mult).then_inc(mem_step, 1)
                        dve.wait_ge(mem_step, k.next() + 1)
                        part = xres[:, st, qq * DKV:(qq + 1) * DKV]
                        nc.vector.scalar_tensor_tensor(out=part, in0=bank[:, 0:DKV], scalar=den[:, st % 2, 1:2], in1=part,
                                                       op0=ALU.mult, op1=ALU.add).then_inc(freed, 1)

                def rows_out(g):
                    bank = bank_ready()
                    if g >= 2:
                        dve.wait_ge(ms_in[g % 2], 16 * (b * 4 + g // 2))
                    elif has_prev:
                        dve.wait_ge(ms_in[g % 2], 16 * (b * 4))
                    nc.vector.tensor_scalar(mrow[:, g % 2, :], bank[0:16, 0:P], -1.0 / (QK_S * QK_S), None, ALU.mult).then_inc(freed, 1)

                def quotient(g):
                    dve.wait_ge(av_done, b * NG + g + 1)
                    nc.vector.reciprocal(rsum[:, :], ps_sum[:, :]).then_inc(quot_step, 1)
                    dve.wait_ge(quot_step, b * NG + g + 1)
                    nc.vector.tensor_tensor(oT[:, g % 2, :], ps_av[:, :], rsum[:, :], ALU.mult).then_inc(oT_done, 1)

                def attn_mix(g):
                    bank = bank_ready()
                    part = xres[:, :, g * P:(g + 1) * P]
                    dve.wait_ge(freed, f.now() - 1)
                    nc.vector.scalar_tensor_tensor(out=part, in0=bank[:, :].rearrange("p (s e) -> p s e", s=NS), scalar=mixw[:, 4:5], in1=part,
                                                   op0=ALU.mult, op1=ALU.add).then_inc(freed, 1)

                for stage in PROJ:
                    if stage[0] in "kq":
                        bank = bank_ready()
                        tile = int(stage[1]) + (2 if stage[0] == "q" else 0)
                        dve.wait_ge(hi_done, his.next() + 1)
                        if stage[0] == "q":
                            dve.wait_ge(eq_done, b * 8 + tile - 1)
                        nc.vector.scalar_tensor_tensor(out=qk_lo[:, tile % 4, :], in0=bank[:, :], scalar=QK_S / (XN_S * W_S),
                                                       in1=qk_hi[:, tile % 4, :], op0=ALU.mult, op1=ALU.subtract).then_inc(freed, 1)
                        if stage[0] == "q":
                            e = eq[:, tile % 2, :]
                            nc.vector.tensor_scalar(e, e, 1.0, 0.0, ALU.subtract, ALU.min).then_inc(elu_step, 1)
                    elif stage[0] == "v":
                        bank = bank_ready()
                        i = int(stage[1])
                        nc.vector.tensor_scalar(v[:, 2 * i:2 * i + 2, :], bank[:, :].rearrange("p (s e) -> p s e", s=2),
                                                1.0 / (XN_S * W_S), None, ALU.mult).then_inc(freed, 1)
                    else:
                        if stage == "am0":
                            dve.wait_ge(xres_in, 16 * (b + 1))
                        mem_mix(int(stage[2]))
                    c = s1_chunk_after(stage)
                    if c is not None:
                        maxima_of(c // 4, c % 4)
                rows_out(0)

                for g in range(NG):
                    for t in range(NS):
                        if t == 0 and g + 1 < NG:
                            rows_out(g + 1)
                        if t == 1 and g > 0:
                            quotient(g - 1)
                        if g + 2 < NG:
                            maxima_of(g + 2, t)
                        if has_next and g == 0:
                            bn(b + 1, t)
                        if has_next and g == 1:
                            normalise(b + 1, t)
                        if has_next and (g, t) in XT_AT:
                            n = f.next()
                            xn_lo(n, his.next(), (f.n - 1) % 2, XT_AT[g, t])
                        if t == 2 and g > 0:
                            attn_mix(g - 1)
                quotient(NG - 1)
                mem_mix(3)
                attn_mix(NG - 1)
                assert f.n == FILLS - (0 if has_next else ND), f.n

            loop_first_last(dve, nb, 1, batch)


def filter_phase(nc, k, toeplitz, toe_done):
    k_pad = nc.dram_tensor("filter_halves", [2, NHC, P + D], F16).ap()
    with (
        nc.sbuf_tensor("f_k", [NHC, P + D], F32) as kf,
        nc.sbuf_tensor("f_hi", [NHC, P + D], F16) as k_hi,
        nc.sbuf_tensor("f_lo", [NHC, P + D], F16) as k_lo,
        nc.semaphore("f_zero") as zeroed,
        nc.semaphore("f_in") as k_in,
        nc.semaphore("f_split") as split,
        nc.semaphore("f_out") as k_out,
        nc.Block() as block,
    ):
        @block.vector
        def _(dve):
            nc.vector.memset(kf[:, 0:P], 0.0).then_inc(zeroed, 1)
            dve.wait_ge(zeroed, 1)
            dve.wait_ge(k_in, 16)
            nc.vector.tensor_scalar(k_hi[:, :], kf[:, :], T_S, None, ALU.mult).then_inc(split, 1)
            dve.wait_ge(split, 1)
            nc.vector.scalar_tensor_tensor(out=k_lo[:, :], in0=kf[:, :], scalar=T_S, in1=k_hi[:, :],
                                           op0=ALU.mult, op1=ALU.subtract).then_inc(split, 1)

        @block.sync
        def _(sp):
            sp.dma_start(kf[:, P:P + D], k).then_inc(k_in, 16)
            sp.wait_ge(split, 2)
            sp.dma_start(k_pad[0], k_hi[:, :]).then_inc(k_out, 16)
            sp.dma_start(k_pad[1], k_lo[:, :]).then_inc(k_out, 16)
            sp.wait_ge(k_out, 32)
            for half in range(2):
                rows = k_pad[half, 0, P:]
                shifted = bass.AP(rows.tensor, rows.offset, [[P + D, NHC], [-1, P], [1, D]])
                sp.dma_start(toeplitz[:, :, half, :], shifted).then_inc(toe_done, 16)


def conv_phase(nc, x1, ctx_in, toeplitz, toe_done, skip, ident_in, x2, absmax, moments, nh):
    NL = D // P
    NP = HX * P
    with ExitStack() as ctx:
        def sb(name, shape, dt=F32):
            return ctx.enter_context(nc.sbuf_tensor(name, shape, dt))

        def sem(name):
            return ctx.enter_context(nc.semaphore(name))

        ident = sb("c_ident", [P, P])
        xh = sb("c_xh", [P, 2, D])
        ch = sb("c_ch", [P, 2, D])
        xres = sb("c_xres", [P, 2, D])
        vh = sb("c_vh", [P, D])
        vT = sb("c_vT", [P, NL, P])
        uT = sb("c_uT", [P, 2, NL, P])
        gT = sb("c_gT", [P, 2, NL, P])
        toe = sb("c_toe", [P, 2, 2, D], F16)
        u = sb("c_u", [P, 3, NP])
        u_hi = sb("c_u_hi", [P, 2, NL, NP], F16)
        u_lo = sb("c_u_lo", [P, 2, NL, NP], F16)
        z = sb("c_z", [P, 2, NP])
        tree = sb("c_tree", [P, 2, NP // 2])
        skp = sb("c_skp", [P, NHC, HX])
        sterm = sb("c_sterm", [P, 2, NL, P])
        st1 = sb("c_st1", [P, NL, P])
        oT = sb("c_oT", [P, 2, NL, P])
        zn = sb("c_zn", [P, D])
        stats = sb("c_stats", [P, 2, 6])
        mv = sb("c_mv", [P, 2])
        rstd = sb("c_rstd", [P, 1])
        stats2 = sb("c_stats2", [P, 2, 6])
        veps = sb("c_veps", [P, 2])
        cell = sb("c_cell", [P, 1])
        mv2 = sb("c_mv2", [P, 2])
        mhalf = sb("c_mhalf", [P, 1])

        bankT = [ctx.enter_context(nc.psum_tensor(f"c_bt{i}", [P, 512], F32)) for i in range(4)]
        y = [ctx.enter_context(nc.psum_tensor(f"c_y{i}", [P, 2, 512], F32)) for i in range(2)]

        const_in = sem("c_const_in")
        ready = sem("c_ready")
        skp_done = sem("c_skp_done")
        x_in = [sem(f"c_x_in{i}") for i in range(2)]
        c_in = [sem(f"c_c_in{i}") for i in range(2)]
        t_in = [sem(f"c_t_in{i}") for i in range(2)]
        x2_out = [sem(f"c_x2_out{i}") for i in range(2)]
        bn_step = sem("c_bn_step")
        veps_done = sem("c_veps_done")
        rstd_done = sem("c_rstd_done")
        rstd2_done = sem("c_rstd2_done")
        vh_done = sem("c_vh_done")
        res_done = sem("c_res_done")
        tr_filled = sem("c_tr_filled")
        tr_read = sem("c_tr_read")
        bk_filled = sem("c_bk_filled")
        bk_read = sem("c_bk_read")
        u_done = sem("c_u_done")
        hi_done = sem("c_hi_done")
        lo_done = sem("c_lo_done")
        y_done = sem("c_y_done")
        z_done = sem("c_z_done")
        tree_step = sem("c_tree_step")
        o_done = sem("c_o_done")
        skip_step = sem("c_skip_step")
        bn2_step = sem("c_bn2_step")
        zn_done = sem("c_zn_done")
        veps2_done = sem("c_veps2_done")

        block = ctx.enter_context(nc.Block())

        rows_x1 = x1.rearrange("b (h i) d -> h b i d", i=HX)
        rows_c = ctx_in.rearrange("b (h i) d -> h b i d", i=HX)

        @block.sync
        def _(sp):
            sp.dma_start(ident[:, :], ident_in).then_inc(const_in, 16)
            sp.dma_start(skp[:, :, :], skip.rearrange("(a h i) -> a h i", a=1, i=HX).to_broadcast([P, NHC, HX])).then_inc(const_in, 16)

            def load(h, q):
                sp.dma_start(toe[:, q, :, :], toeplitz[h]).then_inc(t_in[q], 16)
                sp.dma_start(xh[:, q, :], rows_x1[h]).then_inc(x_in[q], 16)
                sp.dma_start(ch[:, q, :], rows_c[h]).then_inc(c_in[q], 16)

            sp.wait_ge(toe_done, 32)
            load(0, 0)

            def channel(h, pair, q, has_prev, has_next):
                if has_next:
                    if has_prev:
                        sp.wait_ge(y_done, h * NL)
                        sp.wait_ge(res_done, h)
                    load(h + 1, 1 - q)
                if has_prev:
                    sp.wait_ge(bk_read, 2 * h)
                    sp.dma_start(x2[h - 1], xres[:, 1 - q, :]).then_inc(x2_out[1 - q], 16)

            channel_loop(sp, nh, channel)
            sp.wait_ge(bk_read, 2 * nh)
            sp.dma_start(x2[nh - 1], xres[:, (nh - 1) % 2, :]).then_inc(x2_out[(nh - 1) % 2], 16)
            for i in range(2):
                sp.wait_ge(x2_out[i], 16 * (nh // 2))

        @block.gpsimd
        def _(pool):
            nc.gpsimd.memset(mhalf[:, :], -0.5).then_inc(ready, 1)
            pool.wait_ge(const_in, 32)
            nc.gpsimd.tensor_scalar(skp[:, :, :], skp[:, :, :], T_S, None, ALU.mult).then_inc(skp_done, 1)
            pool.wait_ge(ready, 1)
            pool.wait_ge(skp_done, 1)

            def skip_share(h, q):
                pool.wait_ge(tr_read, 4 * (h + 1))
                n = Count(h * 6)
                nc.gpsimd.tensor_tensor(st1[:, :, :], vT[:, :, :], gT[:, q, :, :], ALU.mult).then_inc(skip_step, 1)
                pool.wait_ge(skip_step, n.next() + 1)
                s = st1[:, :, :].rearrange("p c (b i) -> p (c b) i", i=HX)
                w = skp[:, h, :].unsqueeze(1).to_broadcast([P, P, HX])
                nc.gpsimd.tensor_tensor(s, s, w, ALU.mult).then_inc(skip_step, 1)
                for width in (4, 2, 1):
                    pool.wait_ge(skip_step, n.next() + 1)
                    nc.gpsimd.tensor_tensor(s[:, :, 0:width], s[:, :, 0:width], s[:, :, width:2 * width], ALU.add).then_inc(skip_step, 1)
                pool.wait_ge(skip_step, n.next() + 1)
                nc.gpsimd.tensor_tensor(sterm[:, q, :, :].rearrange("p c (b j) -> p (c b) j", j=HX),
                                        uT[:, q, :, :].rearrange("p c (b j) -> p (c b) j", j=HX),
                                        s[:, :, 0:1].to_broadcast([P, P, HX]), ALU.mult).then_inc(skip_step, 1)
                n.next()

            def norm_scale1(h):
                pool.wait_ge(veps_done, h + 1)
                nc.gpsimd.tensor_tensor(rstd[:, :], veps[:, 0:1], mhalf[:, :], ALU.pow).then_inc(rstd_done, 1)

            def norm_scale2(h):
                pool.wait_ge(veps2_done, h + 1)
                nc.gpsimd.tensor_tensor(mv2[:, 1:2], veps[:, 1:2], mhalf[:, :], ALU.pow).then_inc(rstd2_done, 1)

            def sum_block(h, q, a):
                n = Count(h * NL * 3 + a * 3)
                pool.wait_ge(z_done, h * NL + a + 1)
                wait(pool, o_done, h * NL + a - 1)
                zz, tr = z[:, a % 2, :], tree[:, a % 2, :]
                nc.gpsimd.tensor_tensor(tr[:, 0:512], zz[:, 0:512], zz[:, 512:1024], ALU.add).then_inc(tree_step, 1)
                pool.wait_ge(tree_step, n.next() + 1)
                nc.gpsimd.tensor_tensor(tr[:, 0:256], tr[:, 0:256], tr[:, 256:512], ALU.add).then_inc(tree_step, 1)
                pool.wait_ge(tree_step, n.next() + 1)
                nc.gpsimd.tensor_tensor(tr[:, 0:128], tr[:, 0:128], tr[:, 128:256], ALU.add).then_inc(tree_step, 1)
                pool.wait_ge(tree_step, n.next() + 1)
                nc.gpsimd.tensor_tensor(oT[:, q, a, :], tr[:, 0:128], sterm[:, q, a, :], ALU.add).then_inc(o_done, 1)

            norm_scale1(0)
            skip_share(0, 0)

            def channel(h, pair, q, has_prev, has_next):
                if has_next:
                    norm_scale1(h + 1)
                sum_block(h, q, 0)
                sum_block(h, q, 1)
                if has_prev:
                    norm_scale2(h - 1)
                for a in range(2, NL):
                    sum_block(h, q, a)
                    if a == 3 and has_next:
                        skip_share(h + 1, 1 - q)

            channel_loop(pool, nh, channel)
            norm_scale2(nh - 1)

        @block.tensor
        def _(pe):
            pe.wait_ge(const_in, 32)

            def forward(h, q):
                pe.wait_ge(vh_done, h + 1)
                for src in range(2):
                    if src:
                        pe.wait_ge(c_in[q], pair_count(h, q))
                    for c in range(2):
                        wait(pe, tr_read, 4 * h + 2 * src + c - 1)
                        for k in range(4):
                            cols = slice((4 * c + k) * P, (4 * c + k + 1) * P)
                            m = nc.tensor.transpose(bankT[c][:, k * P:(k + 1) * P], vh[:, cols] if src == 0 else ch[:, q, cols], ident[:, :])
                        m.then_inc(tr_filled, 1)

            def backward(h, q):
                for c in range(2):
                    pe.wait_ge(o_done, h * NL + 4 * c + 4)
                    wait(pe, bk_read, 2 * h + c - 1)
                    for k in range(4):
                        m = nc.tensor.transpose(bankT[2 + c][:, k * P:(k + 1) * P], oT[:, q, 4 * c + k, :], ident[:, :])
                    m.then_inc(bk_filled, 1)

            def conv(h, q, a):
                wait(pe, z_done, h * NL + a - 1)
                for c in range(a + 1):
                    wt_hi = toe[:, q, 0, (a - c) * P:(a - c + 1) * P]
                    wt_lo = toe[:, q, 1, (a - c) * P:(a - c + 1) * P]
                    if c == a:
                        pe.wait_ge(lo_done, h * NL + a + 1)
                    for wt, src, first, last in ((wt_hi, u_hi, True, False), (wt_hi, u_lo, False, False), (wt_lo, u_hi, False, True)):
                        for n in range(2):
                            m = nc.tensor.matmul(y[a % 2][:, n, :], wt, src[:, q, c, n * 512:(n + 1) * 512],
                                                 start=(first and c == 0), stop=(last and c == a))
                m.then_inc(y_done, 1)

            forward(0, 0)

            def channel(h, pair, q, has_prev, has_next):
                pe.wait_ge(t_in[q], pair_count(h, q))
                conv(h, q, 0)
                conv(h, q, 1)
                if has_next:
                    forward(h + 1, 1 - q)
                if has_prev:
                    backward(h - 1, 1 - q)
                for a in range(2, NL):
                    conv(h, q, a)

            channel_loop(pe, nh, channel)
            backward(nh - 1, (nh - 1) % 2)

        @block.scalar
        def _(act):
            def evacuate(h, q):
                for n in range(4):
                    src, c = n // 2, n % 2
                    act.wait_ge(tr_filled, 4 * h + n + 1)
                    bank, blocks = bankT[c][:, :].rearrange("p (k e) -> p k e", k=4), slice(4 * c, 4 * c + 4)
                    if src == 0:
                        if n == 0:
                            wait(act, u_done, NL * h)
                            wait(act, skip_step, 6 * h)
                        nc.scalar.activation(vT[:, blocks, :], bank, ACT.Copy).then_inc(tr_read, 1)
                    else:
                        if n == 2:
                            wait(act, z_done, NL * (h - 1))
                        nc.scalar.activation(uT[:, q, blocks, :], bank, ACT.Copy, scale=U_S)
                        nc.scalar.activation(gT[:, q, blocks, :], bank, ACT.Copy, scale=1.0 / (T_S * U_S)).then_inc(tr_read, 1)

            def residual(h, q):
                act.wait_ge(x_in[q], pair_count(h, q))
                wait(act, x2_out[q], pair_count(h, q) - 16)
                wait(act, zn_done, h - 1)
                nc.scalar.activation(xres[:, q, :], xh[:, q, :], ACT.Copy).then_inc(res_done, 1)

            def high(h, q, c):
                act.wait_ge(u_done, h * NL + c + 1)
                if c == 0:
                    wait(act, y_done, NL * (h - 1))
                nc.scalar.activation(u_hi[:, q, c, :], u[:, c % 3, :], ACT.Copy).then_inc(hi_done, 1)

            residual(0, 0)
            evacuate(0, 0)
            for c in range(NL):
                high(0, 0, c)

            def channel(h, pair, q, has_prev, has_next):
                if has_next:
                    evacuate(h + 1, 1 - q)
                    for c in range(NL):
                        high(h + 1, 1 - q, c)
                    residual(h + 1, 1 - q)

            channel_loop(act, nh, channel)

        @block.vector
        def _(dve):
            def normalise(h, q):
                dve.wait_ge(x_in[q], pair_count(h, q))
                for c in range(2):
                    nc.vector.bn_stats(out=stats[:, c, :], in_=xh[:, q, c * 512:(c + 1) * 512]).then_inc(bn_step, 1)
                wait_on_cell(nc, cell[:, :], dve, bn_step, 3 * h + 2)
                nc.vector.bn_aggr(out=mv[:, :], in_=stats[:, :, :]).then_inc(bn_step, 1)
                dve.wait_ge(bn_step, 3 * h + 3)
                nc.vector.tensor_scalar(veps[:, 0:1], mv[:, 1:2], LN_EPS, None, ALU.add).then_inc(veps_done, 1)

            def normalise_end(h, q):
                dve.wait_ge(rstd_done, h + 1)
                wait(dve, tr_filled, 4 * h - 2)
                nc.vector.tensor_scalar(vh[:, :], xh[:, q, :], mv[:, 0:1], rstd[:, :], ALU.subtract, ALU.mult).then_inc(vh_done, 1)

            def product(h, q, c):
                if c == 0:
                    dve.wait_ge(tr_read, 4 * (h + 1))
                wait(dve, lo_done, h * NL + c - 2)
                n = nc.vector.tensor_tensor(u[:, c % 3, :].rearrange("p (i b j) -> p i b j", i=HX, j=HX),
                                            vT[:, c, :].rearrange("p (b i) -> p i b", i=HX).unsqueeze(3).to_broadcast([P, HX, B, HX]),
                                            uT[:, q, c, :].rearrange("p (b j) -> p b j", j=HX).unsqueeze(1).to_broadcast([P, HX, B, HX]),
                                            ALU.mult)
                n.then_inc(u_done, 1)

            def low(h, q, c):
                dve.wait_ge(hi_done, h * NL + c + 1)
                nc.vector.tensor_tensor(u_lo[:, q, c, :], u[:, c % 3, :], u_hi[:, q, c, :], ALU.subtract).then_inc(lo_done, 1)

            def gate(h, q, a):
                dve.wait_ge(y_done, h * NL + a + 1)
                wait(dve, tree_step, 3 * (h * NL + a - 1) - 2)
                nc.vector.tensor_tensor(z[:, a % 2, :].rearrange("p (i b j) -> p i b j", i=HX, j=HX),
                                        y[a % 2][:, :, :].rearrange("p n (i b j) -> p (n i) b j", i=HX // 2, j=HX),
                                        gT[:, q, a, :].rearrange("p (b i) -> p i b", i=HX).unsqueeze(3).to_broadcast([P, HX, B, HX]),
                                        ALU.mult).then_inc(z_done, 1)

            def add_result(h, q):
                dve.wait_ge(res_done, h + 1)
                for c in range(2):
                    dve.wait_ge(bk_filled, 2 * h + c + 1)
                    part = xres[:, q, c * 512:(c + 1) * 512]
                    nc.vector.tensor_tensor(part, part, bankT[2 + c][:, :], ALU.add).then_inc(bk_read, 1)
                for c in range(2):
                    dve.wait_ge(bk_read, 2 * h + c + 1)
                    nc.vector.bn_stats(out=stats2[:, c, :], in_=xres[:, q, c * 512:(c + 1) * 512]).then_inc(bn2_step, 1)
                wait_on_cell(nc, cell[:, :], dve, bn2_step, 3 * h + 2)
                nc.vector.bn_aggr(out=mv2[:, 0:2], in_=stats2[:, :, :]).then_inc(bn2_step, 1)
                dve.wait_ge(bn2_step, 3 * h + 3)
                nc.vector.tensor_scalar(veps[:, 1:2], mv2[:, 1:2], LN_EPS, None, ALU.add).then_inc(veps2_done, 1)

            def largest(h, q):
                dve.wait_ge(rstd2_done, h + 1)
                nc.vector.tensor_scalar(zn[:, :], xres[:, q, :], mv2[:, 0:1], mv2[:, 1:2], ALU.subtract, ALU.mult).then_inc(zn_done, 1)
                nc.vector.tensor_copy(moments[:, h, :], mv2[:, 0:2])
                dve.wait_ge(zn_done, h + 1)
                nc.vector.tensor_reduce(absmax[:, bass.ds(h, 1)], zn[:, :], axis=AX_X, op=ALU.max, apply_absolute_value=True)

            normalise(0, 0)
            normalise_end(0, 0)
            product(0, 0, 0)
            for c in range(NL):
                if c + 1 < NL:
                    product(0, 0, c + 1)
                low(0, 0, c)

            def channel(h, pair, q, has_prev, has_next):
                if has_next:
                    normalise(h + 1, 1 - q)
                    normalise_end(h + 1, 1 - q)
                gate(h, q, 0)
                gate(h, q, 1)
                if has_prev:
                    add_result(h - 1, 1 - q)
                c = 0
                for a in range(2, NL):
                    if has_next and a >= 3:
                        for _ in range(2 if a in (5, 6, 7) else 1):
                            product(h + 1, 1 - q, c)
                            if c:
                                low(h + 1, 1 - q, c - 1)
                            c += 1
                    gate(h, q, a)
                    if a == 3 and has_prev:
                        largest(h - 1, 1 - q)
                if has_next:
                    low(h + 1, 1 - q, NL - 1)

            channel_loop(dve, nh, channel)
            add_result(nh - 1, (nh - 1) % 2)
            largest(nh - 1, (nh - 1) % 2)


def channel_loop(eng, n, body):
    for q in range(2):
        body(q, 0, q, q > 0, q + 1 < n)
    if n > 4:
        with eng.Fori(1, n // 2 - 1) as pair:
            for q in range(2):
                body(pair * 2 + q, pair, q, True, True)
    if n > 2:
        for q in range(2):
            body(n - 2 + q, n // 2 - 1, q, True, q == 0)


def pair_count(h, q):
    return (h - q) * 8 + 16


def ffn_phase(nc, x2, weight, weight_scale, bias, ident_in, absmax, moments, out, nt):
    NT3 = 3
    with ExitStack() as ctx:
        def sb(name, shape, dt=F32):
            return ctx.enter_context(nc.sbuf_tensor(name, shape, dt))

        def sem(name):
            return ctx.enter_context(nc.semaphore(name))

        ident = sb("g_ident", [P, P])
        ident16 = sb("g_ident16", [P, P], F16)
        ones = sb("g_ones", [1, P])
        wrow = sb("g_wrow", [P, 2, D])
        w_hi = sb("g_w_hi", [P, ND, D], F16)
        w_lo = sb("g_w_lo", [P, ND, D], F16)
        wscale = sb("g_wscale", [P, 2])
        bias_all = sb("g_bias", [P, D])
        top = sb("g_top", [P, 1])
        row = sb("g_row", [1, P + 4])
        inv = sb("g_inv", [P, 1])
        gain = sb("g_gain", [P, NHC])
        xt = sb("g_xt", [P, 4, D])
        xb = sb("g_xb", [P, 2, D])
        zt = sb("g_zt", [P, 2, D])
        power = sb("g_power", [P, 2, D])
        xq = sb("g_xq", [P, 2, D], F16)
        xqT = sb("g_xqT", [P, 2, ND, P], F16)
        res = sb("g_res", [P, 2, D])

        bank = [ctx.enter_context(nc.psum_tensor(f"g_b{i}", [P, 512], F32)) for i in range(2)]
        bankT = [ctx.enter_context(nc.psum_tensor(f"g_t{i}", [P, ND, P], F16)) for i in range(2)]
        acc = [ctx.enter_context(nc.psum_tensor(f"g_acc{i}", [P, 2, 512], F32)) for i in range(2)]

        const_in = sem("g_const_in")
        w_in = [sem(f"g_w_in{i}") for i in range(2)]
        w_filled = sem("g_w_filled")
        w_hi_done = sem("g_w_hi_done")
        w_done = sem("g_w_done")
        id16_done = sem("g_id16_done")
        ones_done = sem("g_ones_done")
        ws_done = sem("g_ws_done")
        top_step = sem("g_top_step")
        top_T = sem("g_top_T")
        top_B = sem("g_top_B")
        x_in = [sem(f"g_x_in{i}") for i in range(4)]
        xb_done = sem("g_xb_done")
        z_step = sem("g_z_step")
        sum_step = sem("g_sum_step")
        xq_done = sem("g_xq_done")
        tr_done = sem("g_tr_done")
        xqT_done = sem("g_xqT_done")
        mm_done = sem("g_mm_done")
        res_done = sem("g_res_done")
        stored = [sem(f"g_stored{i}") for i in range(2)]

        block = ctx.enter_context(nc.Block())
        rows_out = out.rearrange("b (h i) d -> h b i d", i=HX)

        @block.sync
        def _(sp):
            sp.dma_start(ident[:, :], ident_in).then_inc(const_in, 16)
            sp.dma_start(wscale[:, 0:1], weight_scale.to_broadcast([P, 1])).then_inc(const_in, 16)
            sp.dma_start(bias_all[:, :], bias.rearrange("(a n) -> a n", a=1).to_broadcast([P, D])).then_inc(const_in, 16)
            for n in range(ND):
                wait(sp, w_done, 2 * (n - 1))
                sp.dma_start(wrow[:, n % 2, :], weight[n * P:(n + 1) * P, :]).then_inc(w_in[n % 2], 16)
            for n in range(NT3):
                sp.dma_start(xt[:, n, :], x2[n]).then_inc(x_in[n], 16)

            def tile(n, quad, r):
                if n_static(n) is None or n + NT3 < nt:
                    wait(sp, xb_done, n)
                    wait(sp, xq_done, n)
                    sp.dma_start(xt[:, (r + NT3) % 4, :], x2[n + NT3]).then_inc(x_in[(r + NT3) % 4], 16)
                sp.wait_ge(res_done, n + 1)
                sp.dma_start(rows_out[n], res[:, r % 2, :]).then_inc(stored[r % 2], 16)

            quad_loop(sp, nt, tile)
            for i in range(2):
                sp.wait_ge(stored[i], 16 * (nt // 2))

        @block.gpsimd
        def _(pool):
            nc.gpsimd.memset(ones[:, :], 1.0).then_inc(ones_done, 1)
            pool.wait_ge(const_in, 48)

            def tile(n, quad, r):
                pool.wait_ge(x_in[r], 16 * (quad + 1))
                wait(pool, res_done, n - 1)
                nc.gpsimd.tensor_tensor(xb[:, r % 2, :], xt[:, r, :], bias_all[:, :], ALU.add).then_inc(xb_done, 1)

            quad_loop(pool, nt, tile)

        @block.tensor
        def _(pe):
            pe.wait_ge(const_in, 48)
            for n in range(ND):
                pe.wait_ge(w_in[n % 2], 16 * (n // 2 + 1))
                for c in range(2):
                    wait(pe, w_done, 2 * n + c - 1)
                    for k in range(4):
                        m = nc.tensor.transpose(bank[c][:, k * P:(k + 1) * P], wrow[:, n % 2, (4 * c + k) * P:(4 * c + k + 1) * P], ident[:, :])
                    m.then_inc(w_filled, 1)
            pe.wait_ge(w_done, 2 * ND)
            pe.wait_ge(top_step, 1)
            nc.tensor.matmul(bank[0][0:1, 0:P], top[:, :], ident[:, :], start=True, stop=True).then_inc(top_T, 1)
            pe.wait_ge(top_step, 4)
            pe.wait_ge(ones_done, 1)
            nc.tensor.matmul(bank[1][:, 0:1], ones[0:1, :], row[0:1, P + 2:P + 3], start=True, stop=True).then_inc(top_B, 1)
            pe.wait_ge(id16_done, 1)

            def transposes(n, r):
                pe.wait_ge(xq_done, n + 1)
                wait(pe, xqT_done, n - 1)
                for k in range(ND):
                    m = nc.tensor.transpose(bankT[r % 2][:, k, :], xq[:, r % 2, k * P:(k + 1) * P], ident16[:, :])
                m.then_inc(tr_done, 1)

            transposes(0, 0)

            def tile(n, quad, r):
                if n_static(n) is None or n + 1 < nt:
                    transposes(n + 1, r + 1)
                pe.wait_ge(xqT_done, n + 1)
                wait(pe, res_done, n - 1)
                for k in range(ND):
                    for w in (w_hi, w_lo):
                        for c in range(2):
                            m = nc.tensor.matmul(acc[r % 2][:, c, :], xqT[:, r % 2, k, :], w[:, k, c * 512:(c + 1) * 512],
                                                 start=(k == 0 and w is w_hi), stop=(k == ND - 1 and w is w_lo))
                m.then_inc(mm_done, 1)

            quad_loop(pe, nt, tile)

        @block.scalar
        def _(act):
            act.wait_ge(const_in, 48)
            nc.scalar.activation(wscale[:, 1:2], wscale[:, 0:1], ACT.Copy, scale=W_S).then_inc(ws_done, 1)
            nc.scalar.activation(ident16[:, :], ident[:, :], ACT.Copy).then_inc(id16_done, 1)
            act.wait_ge(ws_done, 1)
            for n in range(2 * ND):
                act.wait_ge(w_filled, n + 1)
                dst = w_hi[:, 4 * (n % 2):4 * (n % 2) + 4, (n // 2) * P:(n // 2 + 1) * P]
                nc.scalar.activation(dst, bank[n % 2][:, :].rearrange("p (k e) -> p k e", k=4), ACT.Copy, scale=wscale[:, 1:2]).then_inc(w_hi_done, 1)

            def tile(n, quad, r):
                act.wait_ge(tr_done, n + 1)
                wait(act, mm_done, n - 1)
                nc.scalar.activation(xqT[:, r % 2, :, :], bankT[r % 2][:, :, :], ACT.Copy).then_inc(xqT_done, 1)

            quad_loop(act, nt, tile)

        @block.vector
        def _(dve):
            for n in range(2 * ND):
                dve.wait_ge(w_hi_done, n + 1)
                part = (slice(None), slice(4 * (n % 2), 4 * (n % 2) + 4), slice((n // 2) * P, (n // 2 + 1) * P))
                nc.vector.scalar_tensor_tensor(out=w_lo[part], in0=bank[n % 2][:, :].rearrange("p (k e) -> p k e", k=4), scalar=wscale[:, 1:2],
                                               in1=w_hi[part], op0=ALU.mult, op1=ALU.subtract).then_inc(w_done, 1)
            nc.vector.reduce_max(top[:, :], absmax[:, 0:nt], AX_X).then_inc(top_step, 1)
            dve.wait_ge(top_T, 1)
            nc.vector.reduce_max(row[:, P:P + 1], bank[0][0:1, 0:P], AX_X).then_inc(top_step, 1)
            dve.wait_ge(top_step, 2)
            nc.vector.tensor_scalar(row[:, P + 1:P + 2], row[:, P:P + 1], 1.0 / 448.0, 1e-7, ALU.mult, ALU.max).then_inc(top_step, 1)
            dve.wait_ge(top_step, 3)
            nc.vector.reciprocal(row[:, P + 2:P + 3], row[:, P + 1:P + 2]).then_inc(top_step, 1)
            dve.wait_ge(top_B, 1)
            nc.vector.tensor_copy(inv[:, :], bank[1][:, 0:1]).then_inc(top_step, 1)
            dve.wait_ge(top_step, 5)
            nc.vector.tensor_scalar(gain[:, 0:nt], moments[:, 0:nt, 1], inv[:, :], None, ALU.mult).then_inc(top_step, 1)
            dve.wait_ge(top_step, 6)

            def quantise(n, quad, r):
                dve.wait_ge(x_in[r], 16 * (quad + 1))
                s = Count(n * 3)
                nc.vector.tensor_scalar(zt[:, r % 2, :], xt[:, r, :], moments[:, n, 0:1], gain[:, bass.ds(n, 1)], ALU.subtract, ALU.mult).then_inc(z_step, 1)
                dve.wait_ge(z_step, s.next() + 1)
                nc.vector.tensor_scalar(power[:, r % 2, :].bitcast(U32), zt[:, r % 2, :].bitcast(U32), 0x7F800000, None, ALU.bitwise_and).then_inc(z_step, 1)
                dve.wait_ge(z_step, s.next() + 1)
                nc.vector.tensor_scalar(power[:, r % 2, :], power[:, r % 2, :], 2.0 ** -6, 1.5 * 2.0 ** 20, ALU.max, ALU.mult).then_inc(z_step, 1)
                dve.wait_ge(z_step, s.next() + 1)
                nc.vector.tensor_tensor(zt[:, r % 2, :], zt[:, r % 2, :], power[:, r % 2, :], ALU.add).then_inc(sum_step, 1)
                dve.wait_ge(sum_step, n + 1)
                wait(dve, tr_done, n - 1)
                nc.vector.tensor_tensor(xq[:, r % 2, :], zt[:, r % 2, :], power[:, r % 2, :], ALU.subtract).then_inc(xq_done, 1)

            quantise(0, 0, 0)

            def tile(n, quad, r):
                if n_static(n) is None or n + 1 < nt:
                    quantise(n + 1, quad + (r + 1) // 4, (r + 1) % 4)
                dve.wait_ge(mm_done, n + 1)
                dve.wait_ge(xb_done, n + 1)
                wait(dve, stored[r % 2], 16 * (quad * 2 + r // 2))
                nc.vector.scalar_tensor_tensor(out=res[:, r % 2, :], in0=acc[r % 2][:, :, :].rearrange("p a n -> p (a n)"), scalar=1.0 / W_S,
                                               in1=xb[:, r % 2, :], op0=ALU.mult, op1=ALU.add).then_inc(res_done, 1)

            quad_loop(dve, nt, tile)


def n_static(n):
    return n if isinstance(n, int) else None


def quad_loop(eng, n, body):
    for r in range(4):
        body(r, 0, r)
    if n > 8:
        with eng.Fori(1, n // 4 - 1) as quad:
            for r in range(4):
                body(quad * 4 + r, quad, r)
    for r in range(4):
        body(n - 4 + r, n // 4 - 1, r)


def decoder_layer(nc, x, skip, context, Wq, Wk, Wv, memory, memory_norm, memory_weight, k, weight, weight_scale, bias, ident, out):
    x1 = nc.dram_tensor("x1_rows", [B, S, D], F32).ap()
    x2 = nc.dram_tensor("x2_rows", [NHC, P, D], F32).ap()
    toeplitz = nc.dram_tensor("toeplitz_halves", [NHC, P, 2, D], F16).ap()
    with (
        nc.sbuf_tensor("absmax", [P, NHC], F32) as absmax,
        nc.semaphore("toe_done") as toe_done,
        nc.sbuf_tensor("moments", [P, NHC, 2], F32) as moments,
    ):
        filter_phase(nc, k, toeplitz, toe_done)
        attention_phase(nc, x, Wq, Wk, Wv, memory, memory_norm, memory_weight, ident, x1, B)
        conv_phase(nc, x1, context, toeplitz, toe_done, skip, ident, x2, absmax, moments, NHC)
        ffn_phase(nc, x2, weight, weight_scale, bias, ident, absmax, moments, out, NHC)


_INS = ['x', 'fside_S2_0', 'ctx_2048', 'L0_attn_Wq', 'L0_attn_Wk', 'L0_attn_Wv', 'L0_attn_memory', 'L0_attn_memory_norm',
        'L0_attn_memory_weight', 'L0_xattn_k', 'L0_ffn_weight', 'L0_ffn_weight_scale', 'L0_ffn_bias']


def kernel(**inputs):
    import numpy as np
    import concourse.bacc as bacc
    from concourse.bass_utils import run_bass_kernel_spmd

    nc = bacc.Bacc("TRN2", target_bir_lowering=False, num_devices=1)
    arrays, args = {}, []
    for name in _INS:
        a = np.ascontiguousarray(inputs[name])
        if a.ndim == 0:
            a = a.reshape(1, 1)
        arrays[f"in_{name}"] = a
        args.append(nc.dram_tensor(f"in_{name}", a.shape, mybir.dt.from_np(a.dtype), kind="ExternalInput").ap())
    ident = np.eye(P, dtype=np.float32)
    arrays["in_ident"] = ident
    args.append(nc.dram_tensor("in_ident", ident.shape, F32, kind="ExternalInput").ap())
    args.append(nc.dram_tensor("out_0", (B, S, D), F32, kind="ExternalOutput").ap())
    decoder_layer(nc, *args)
    r = run_bass_kernel_spmd(nc, [arrays], core_ids=[0])
    return r.results[0]["out_0"]
```

```python
import concourse.bass as bass
from concourse import mybir
from contextlib import ExitStack

P = 128
F32 = mybir.dt.float32
F16 = mybir.dt.float16
U32 = mybir.dt.uint32
ALU = mybir.AluOpType
ACT = mybir.ActivationFunctionType
AX_X = mybir.AxisListType.X

B, S, D = 16, 512, 1024
NQ, NH, DH = 4, 8, 32
DKV = NH * DH
E_ALL = D + 2 * DKV
ND = D // P
NS = S // P
NG = NQ * NH // 4
HX = 8
NHC = S // HX
LN_EPS = 1e-5
TOE_PARTS = 2 * NG
TOE_DONE = 2 * 16 * TOE_PARTS

XN_S = 16.0
W_S = 256.0
QK_S = 16.0
T_S = 256.0
U_S = 16.0


def wait(eng, sem, value):
    if not (isinstance(value, int) and value <= 0):
        eng.wait_ge(sem, value)


def wait_on_cell(nc, cell, eng, sem, value):
    wait(eng, sem, value)
    nc.vector.memset(cell, 0.0)


def loop_first_last(eng, n, first, body):
    for i in range(first):
        body(i, i > 0, True)
    if n - 1 > first:
        with eng.Fori(first, n - 1) as i:
            body(i, True, True)
    body(n - 1, True, False)


class Count:

    def __init__(self, base=0):
        self.base, self.n = base, 0

    def next(self):
        v = self.base + self.n
        self.n += 1
        return v

    def now(self):
        return self.base + self.n


def s1_chunk(stage):
    order = ["q4", "q5", "am1", "q6", "q7", "am2", "v0", "v1"]
    return order.index(stage) if stage in order else None


PROJ = ["k0", "k1", "q0", "q1", "q2", "q3", "am0", "q4", "q5", "am1", "q6", "q7", "rows0", "am2", "v0", "v1"]
def fill_plan(has_next):
    n, at = 0, {}
    for stage in PROJ:
        n += 4 * (stage[:2] == "am") + 4 * (s1_chunk(stage) is not None) + (stage == "rows0")
        at[stage] = n
    at["rows", 0] = at["rows0"]
    for g in range(NG):
        for t in range(NS):
            if t == 1 and g + 1 < NG:
                n += 1
                at["rows", g + 1] = n
            n += 4 * (g + 2 < NG)
            n += g == NG - 1
            at["am3"] = n
            if has_next and (g, t) in XT_AT:
                n += 1
                at["xt"] = n
            n += 2 * (t == 2 and g > 0)
    at["all"] = n + 2
    return at


XT_AT = {(2, 1): 0, (3, 1): 1, (4, 1): 2, (5, 1): 3, (5, 3): 4, (6, 1): 5, (6, 3): 6, (7, 1): 7}


def attention_phase(nc, x, Wq, Wk, Wv, memory, memory_norm, memory_weight, ident_in, k_pad, toeplitz, toe_done, x1, nb):
    with ExitStack() as ctx:
        def sb(name, shape, dt=F32):
            return ctx.enter_context(nc.sbuf_tensor(name, shape, dt))

        def sem(name):
            return ctx.enter_context(nc.semaphore(name))

        ident = sb("a_ident", [P, P])
        w_hi = sb("a_w_hi", [P, ND, E_ALL], F16)
        w_lo = sb("a_w_lo", [P, ND, E_ALL], F16)
        xin = sb("a_xin", [P, NS, D])
        xres = sb("a_xres", [P, NS, D])
        xT_hi = sb("a_xT_hi", [P, ND, S], F16)
        xT_lo = sb("a_xT_lo", [P, ND, S], F16)
        qk_hi = sb("a_qk_hi", [P, 4, S], F16)
        qk_lo = sb("a_qk_lo", [P, 4, S], F16)
        qs = sb("a_qs", [P, NQ * NH, S], F16)
        ks = sb("a_ks", [P, NH, S], F16)
        v = sb("a_v", [P, NS, DKV])
        probs = sb("a_probs", [P, 2, 4, S])
        sumT = sb("a_sumT", [P, S])
        oT = sb("a_oT", [P, S])
        rsum = sb("a_rsum", [P, 2, 4 * NS])
        mixed = sb("a_mixed", [P, S])
        sq = sb("a_sq", [P, 4, S])
        eq = sb("a_eq", [P, 2, S])
        rq = sb("a_rq", [P, 2, S])
        mem = sb("a_mem", [P, 2, DKV + 1])
        ones = sb("a_ones", [P, DH])
        maxima = sb("a_max", [P, 2, 4, NS])
        mrow = sb("a_mrow", [16, 2, P], F16)
        stats = sb("a_stats", [P, NS, 2, 6])
        mv = sb("a_mv", [P, NS, 2])
        veps = sb("a_veps", [P, NS])
        rstd = sb("a_rstd", [P, NS])
        cell = sb("a_cell", [P, 1])
        mhalf = sb("a_mhalf", [P, NS])
        mixw = sb("a_mixw", [P, 8])
        den = sb("a_den", [P, 2, 2])

        psum = [ctx.enter_context(nc.psum_tensor(f"a_ps{i}", [P, 512], F32)) for i in range(4)]
        misc, ps_av, ps_sum = psum[0:2], psum[2], psum[3]
        score = [ctx.enter_context(nc.psum_tensor(f"a_score{i}", [P, 2, S], F32)) for i in range(2)]

        const_in = sem("a_const_in")
        w_in = [sem(f"a_w_in{i}") for i in range(4)]
        w_done = sem("a_w_done")
        xin_in = sem("a_xin_in")
        xres_in = sem("a_xres_in")
        x1_out = sem("a_x1_out")
        ready = sem("a_ready")
        filled = sem("a_filled")
        freed = sem("a_freed")
        pr_filled = sem("a_pr_filled")
        pr_freed = sem("a_pr_freed")
        hi_done = sem("a_hi_done")
        eq_done = sem("a_eq_done")
        sq_done = sem("a_sq_done")
        stacked = [sem(f"a_stacked{i}") for i in range(2)]
        ms_in = [sem(f"a_ms_in{i}") for i in range(2)]
        s2_filled = sem("a_s2_filled")
        exp_done = sem("a_exp_done")
        av_tick = sem("a_av_tick")
        av_done = sem("a_av_done")
        oT_done = sem("a_oT_done")
        mixed_done = sem("a_mixed_done")
        stats_done = sem("a_stats_done")
        rstd_done = sem("a_rstd_done")
        norm_done = sem("a_norm_done")
        dve_step = sem("a_dve_step")
        mix1 = sem("a_mix1")
        w_filled = sem("a_w_filled")
        w_hi_done = sem("a_w_hi_done")
        elu_step = sem("a_elu_step")
        bn_step = sem("a_bn_step")
        aggr_step = sem("a_aggr_step")
        mem_step = sem("a_mem_step")
        quot_step = sem("a_quot_step")

        AT = fill_plan(True)
        assert AT["all"] % 2 == 0 and ND % 2 == 0
        FILLS = AT["all"]
        HIS = 2 + 8 + 8
        N_W = E_ALL // P

        block = ctx.enter_context(nc.Block())

        def w_rows(n):
            if n < ND:
                return Wq[n * P:(n + 1) * P, :]
            if n < ND + 2:
                return Wk[(n - ND) * P:(n - ND + 1) * P, :]
            return Wv[(n - ND - 2) * P:(n - ND - 1) * P, :]

        def stack_count(b, n):
            return 16 * 12 * (b * [3, 2][n % 2] + n // 2 + 1)

        @block.sync
        def _(sp):
            sp.dma_start(ident[:, :], ident_in).then_inc(const_in, 16)
            sp.dma_start(mixw[:, 0:1], memory_weight.rearrange("(a n) -> a n", a=1).to_broadcast([P, 1])).then_inc(const_in, 16)
            for c in range(2):
                sp.dma_start(mem[:, c, 0:DKV], memory[c * P:(c + 1) * P, :]).then_inc(const_in, 16)
                sp.dma_start(mem[:, c, DKV:DKV + 1], memory_norm[c * P:(c + 1) * P, :]).then_inc(const_in, 16)
            sp.dma_start(xin[:, :, :], x[0].rearrange("(t p) d -> p t d", p=P)).then_inc(xin_in, 16)
            for n in range(N_W):
                wait(sp, w_done, 2 * (n - 3))
                sp.dma_start(xres[:, n % 4, :], w_rows(n)).then_inc(w_in[n % 4], 16)
            sp.wait_ge(w_done, 2 * N_W)

            def batch(b, has_prev, has_next):
                if has_next:
                    sp.wait_ge(filled, b * FILLS + ND - (FILLS - AT["xt"]) if has_prev else ND)
                    sp.dma_start(xin[:, :, :], x[b + 1].rearrange("(t p) d -> p t d", p=P)).then_inc(xin_in, 16)
                if has_prev:
                    store(b - 1, b * NG)
                for n in range(5):
                    sp.wait_ge(pr_freed, b * 12 + 2 * n + 2)
                    for j in range(4):
                        rows, slots = slice(DH * j, DH * j + DH), slice(2 * (n % 2), 2 * (n % 2) + 2)
                        hi, lo = qk_hi[rows, slots, :], qk_lo[rows, slots, :]
                        if n == 0:
                            dst, mid, last = ks[:, j:j + 5:4, :], hi, lo
                        else:
                            dst, mid, last = qs[:, 8 * (n - 1) + j:8 * (n - 1) + j + 5:4, :], lo, hi
                        for at, half in ((0, hi), (DH, mid), (2 * DH, last)):
                            sp.dma_start(dst[at:at + DH], half).then_inc(stacked[n % 2], 16)
                    if n == 1:
                        if has_prev:
                            sp.wait_ge(x1_out, 16 * b)
                        sp.dma_start(xres[:, :, :], x[b].rearrange("(t p) d -> p t d", p=P)).then_inc(xres_in, 16)
                for g in range(NG):
                    sp.wait_ge(freed, b * FILLS + ND + fill_plan(has_next)["rows", g])
                    sp.dma_start(qs[3 * DH:3 * DH + 1, 4 * g:4 * g + 4, :], mrow[:, g % 2, :]).then_inc(ms_in[g % 2], 16)
                    if not (has_prev and has_next):
                        copy_toeplitz(sp, k_pad, toeplitz, toe_done, g + (NG if has_prev else 0))

            def store(b, mixes):
                sp.wait_ge(mixed_done, mixes)
                sp.dma_start(x1[b].rearrange("(t p) d -> p t d", p=P), xres[:, :, :]).then_inc(x1_out, 16)

            loop_first_last(sp, nb, 1, batch)
            store(nb - 1, nb * NG)
            sp.wait_ge(x1_out, 16 * nb)


        @block.gpsimd
        def _(pool):
            nc.gpsimd.memset(ones[:, :], 1.0).then_inc(ready, 1)
            nc.gpsimd.memset(mhalf[:, :], -0.5).then_inc(ready, 1)
            pool.wait_ge(ready, 2)
            nc.gpsimd.memset(ks[3 * DH:3 * DH + 1, :, :], QK_S * QK_S).then_inc(ready, 1)
            pool.wait_ge(ready, 3)

            def norm_scale(n):
                pool.wait_ge(stats_done, n + 1)
                nc.gpsimd.tensor_tensor(rstd[:, :], veps[:, :], mhalf[:, :], ALU.pow).then_inc(rstd_done, 1)

            norm_scale(0)

            def batch(b, has_prev, has_next):
                for t in range(8):
                    n = b * 8 + t
                    pool.wait_ge(elu_step, n + 1)
                    if t >= 4:
                        pool.wait_ge(filled, b * FILLS + ND + AT[f"am{t // 2 - 2}"])
                    elif has_prev:
                        pool.wait_ge(filled, b * FILLS + ND - (FILLS - AT[f"am{t // 2 + 2}"]))
                    nc.gpsimd.tensor_tensor(sq[:, t % 4, :], eq[:, t % 2, :], rq[:, t % 2, :], ALU.add).then_inc(sq_done, 1)
                if has_next:
                    norm_scale(b + 1)

            loop_first_last(pool, nb, 1, batch)

        @block.tensor
        def _(pe):
            pe.wait_ge(const_in, 16 * 6)
            pe.wait_ge(ready, 3)
            for n in range(N_W):
                pe.wait_ge(w_in[n % 4], 16 * (n // 4 + 1))
                for c in range(2):
                    wait(pe, w_done, 2 * n + c - 1)
                    for k in range(4):
                        m = nc.tensor.transpose(misc[c][:, k * P:(k + 1) * P], xres[:, n % 4, (4 * c + k) * P:(4 * c + k + 1) * P], ident[:, :])
                    m.then_inc(w_filled, 1)
            pe.wait_ge(w_done, 2 * N_W)

            def fill(f):
                n = f.next()
                wait(pe, freed, n - 1)
                return misc[(f.n - 1) % 2]

            def xn_transposes(f, kk):
                bank = fill(f)
                for st in range(NS):
                    m = nc.tensor.transpose(bank[:, st * P:(st + 1) * P], xin[:, st, kk * P:(kk + 1) * P], ident[:, :])
                m.then_inc(filled, 1)

            def three(out, lhs_hi, lhs_lo, rhs_hi, rhs_lo, first, last):
                nc.tensor.matmul(out, lhs_hi, rhs_hi, start=first, stop=False)
                nc.tensor.matmul(out, lhs_hi, rhs_lo, start=False, stop=False)
                return nc.tensor.matmul(out, lhs_lo, rhs_hi, start=False, stop=last)

            f0 = Count()
            pe.wait_ge(norm_done, NS)
            for kk in range(ND):
                xn_transposes(f0, kk)

            def batch(b, has_prev, has_next):
                f = Count(b * FILLS + ND)
                scored = {}
                pe.wait_ge(hi_done, (b + 1) * 8 + b * 10)
                pe.wait_ge(freed, b * FILLS + ND - 2 if has_prev else ND)

                def score_max(g, chunk, c):
                    if chunk == 0 and c == 0:
                        if g == 0:
                            pe.wait_ge(stacked[0], stack_count(b, 0))
                        n = g // 2 + 1
                        pe.wait_ge(stacked[n % 2], stack_count(b, n))
                    bank = fill(f)
                    nc.tensor.matmul(bank[:, :], qs[0:3 * DH, 4 * g + chunk, c * P:(c + 1) * P], ks[0:3 * DH, (g % 2) * 4 + chunk, :],
                                     start=True, stop=True).then_inc(filled, 1)
                    scored[g] = f.n

                def mem_products(qq, st):
                    if st == 0:
                        pe.wait_ge(sq_done, b * 8 + 2 * qq + 2)
                    bank = fill(f)
                    for c in range(2):
                        m = nc.tensor.matmul(bank[:, 0:DKV + 1], sq[:, (2 * qq + c) % 4, st * P:(st + 1) * P], mem[:, c, :],
                                             start=(c == 0), stop=(c == 1))
                    m.then_inc(filled, 1)

                def max_rows(g):
                    pe.wait_ge(freed, f.base + scored[g])
                    bank = fill(f)
                    nc.tensor.matmul(bank[0:16, 0:P], maxima[:, g % 2, :, :].rearrange("p j s -> p (j s)"), ident[:, :],
                                     start=True, stop=True).then_inc(filled, 1)

                def out_transposes(g, f, copies):
                    pe.wait_ge(oT_done, copies)
                    bank = fill(f)
                    for st in range(NS):
                        m = nc.tensor.matmul(bank[:, 4 * st:4 * st + 4], sumT[:, st * P:(st + 1) * P], ident[:, 0:P:DH], start=True, stop=True)
                    m.then_inc(filled, 1)
                    bank = fill(f)
                    for st in range(NS):
                        m = nc.tensor.transpose(bank[:, st * P:(st + 1) * P], oT[:, st * P:(st + 1) * P], ident[:, :])
                    m.then_inc(filled, 1)

                tile = Count(b * 12)

                def proj_bank():
                    wait(pe, pr_freed, tile.next() - 1)
                    return score[(tile.n - 1) % 2][:, 0, :]

                for stage in PROJ:
                    chunk = s1_chunk(stage)
                    if stage[:2] == "am":
                        for st in range(NS):
                            if chunk is not None:
                                score_max(chunk // 4, chunk % 4, st)
                            mem_products(int(stage[2]), st)
                    elif stage == "rows0":
                        max_rows(0)
                    elif stage[0] == "v":
                        bank = proj_bank()
                        for s in range(2):
                            st = 2 * int(stage[1]) + s
                            for kk in range(ND):
                                if kk % 4 == 0:
                                    score_max(chunk // 4, chunk % 4, 2 * s + kk // 4)
                                m = three(bank[:, s * DKV:(s + 1) * DKV], xT_hi[:, kk, st * P:(st + 1) * P], xT_lo[:, kk, st * P:(st + 1) * P],
                                          w_hi[:, kk, D + DKV:E_ALL], w_lo[:, kk, D + DKV:E_ALL], kk == 0, kk == ND - 1)
                        m.then_inc(pr_filled, 1)
                    else:
                        e0 = (D if stage[0] == "k" else 0) + int(stage[1]) * P
                        bank = proj_bank()
                        for kk in range(ND):
                            if chunk is not None and kk % 2 == 0:
                                score_max(chunk // 4, chunk % 4, kk // 2)
                            m = three(bank, w_hi[:, kk, e0:e0 + P], w_lo[:, kk, e0:e0 + P], xT_hi[:, kk, :], xT_lo[:, kk, :],
                                      kk == 0, kk == ND - 1)
                        m.then_inc(pr_filled, 1)
                    if stage == "k0" and has_prev:
                        out_transposes(NG - 1, Count(b * FILLS + ND - 2), 2 * b * NG)

                def scores(g, t, pair):
                    n = b * 64 + (g * 4 + t) * 2 + pair
                    wait(pe, exp_done, n - 1)
                    if (g, t, pair) == (0, 0, 0):
                        pe.wait_ge(pr_freed, (b + 1) * 12)
                    if t == 0 and pair == 0:
                        pe.wait_ge(ms_in[g % 2], 16 * (b * 4 + g // 2 + 1))
                    for i in range(2):
                        j = 2 * pair + i
                        m = nc.tensor.matmul(score[pair][:, i, :], ks[0:3 * DH + 1, (g % 2) * 4 + j, t * P:(t + 1) * P],
                                             qs[0:3 * DH + 1, 4 * g + j, :], start=True, stop=True)
                    m.then_inc(s2_filled, 1)

                def weighted(g, t):
                    tick = g * 4 + t
                    pe.wait_ge(exp_done, b * 64 + 2 * tick + 2)
                    if t == 0:
                        wait(pe, oT_done, 2 * (b * NG + g))
                    for j in range(4):
                        rows = slice(DH * j, DH * j + DH)
                        head = (g % 2) * 4 + j
                        nc.tensor.matmul(ps_av[rows, :], v[:, t, head * DH:(head + 1) * DH], probs[:, tick % 2, j, :], start=(t == 0), stop=(t == 3))

                def summed(g, t):
                    tick = g * 4 + t
                    for j in range(4):
                        rows = slice(DH * j, DH * j + DH)
                        m = nc.tensor.matmul(ps_sum[rows, :], ones[:, :], probs[:, tick % 2, j, :], start=(t == 0), stop=(t == 3))
                    m.then_inc(av_done if t == 3 else av_tick, 1)

                for g in range(NG):
                    for t in range(NS):
                        more = g + 2 < NG
                        last = (g, t - 1) if t else (g - 1, 3)
                        if t == 1 and g + 1 < NG:
                            max_rows(g + 1)
                        scores(g, t, 0)
                        if more:
                            score_max(g + 2, t, 0)
                        if last[0] >= 0:
                            weighted(*last)
                        if g == NG - 1:
                            mem_products(3, t)
                        if more:
                            score_max(g + 2, t, 1)
                        scores(g, t, 1)
                        if more:
                            score_max(g + 2, t, 2)
                        if last[0] >= 0:
                            summed(*last)
                        if more:
                            score_max(g + 2, t, 3)
                        if has_next and (g, t) in XT_AT:
                            kk = XT_AT[g, t]
                            if kk == 0:
                                pe.wait_ge(norm_done, (b + 2) * NS)
                            xn_transposes(f, kk)
                        if t == 2 and g > 0:
                            out_transposes(g - 1, f, 2 * (b * NG + g))
                weighted(NG - 1, 3)
                summed(NG - 1, 3)
                if not has_next:
                    out_transposes(NG - 1, f, 2 * (b + 1) * NG)

            loop_first_last(pe, nb, 1, batch)

        @block.scalar
        def _(act):
            act.wait_ge(const_in, 16 * 6)
            nc.scalar.activation(mixw[:, 1:2], mixw[:, 0:1], ACT.Exp, scale=-1.0).then_inc(mix1, 1)
            for n in range(2 * N_W):
                act.wait_ge(w_filled, n + 1)
                dst = w_hi[:, 4 * (n % 2):4 * (n % 2) + 4, (n // 2) * P:(n // 2 + 1) * P]
                nc.scalar.activation(dst, misc[n % 2][:, :].rearrange("p (k e) -> p k e", k=4), ACT.Copy, scale=W_S).then_inc(w_hi_done, 1)

            def xn_hi(n_fill, slot, kk):
                act.wait_ge(filled, n_fill + 1)
                nc.scalar.activation(xT_hi[:, kk, :], misc[slot][:, :], ACT.Copy, scale=XN_S).then_inc(hi_done, 1)

            for kk in range(ND):
                xn_hi(kk, kk % 2, kk)

            def batch(b, has_prev, has_next):
                f = Count(b * FILLS + ND)
                for stage in PROJ:
                    f.n += 4 * (s1_chunk(stage) is not None)
                    if stage[0] in "kq":
                        tile = int(stage[1]) + (2 if stage[0] == "q" else 0)
                        bank = score[tile % 2][:, 0, :]
                        act.wait_ge(pr_filled, b * 12 + tile + 1)
                        if tile >= 4:
                            act.wait_ge(stacked[tile // 2 % 2], stack_count(b, tile // 2 - 2))
                        elif has_prev:
                            act.wait_ge(stacked[tile // 2], 16 * 12 * b * [3, 2][tile // 2])
                        nc.scalar.activation(qk_hi[:, tile % 4, :], bank, ACT.Copy, scale=QK_S / (XN_S * W_S)).then_inc(hi_done, 1)
                        if stage[0] == "q":
                            t = tile - 2
                            wait(act, sq_done, b * 8 + t - 1)
                            nc.scalar.activation(eq[:, t % 2, :], bank, ACT.Exp, scale=1.0 / (XN_S * W_S))
                            nc.scalar.activation(rq[:, t % 2, :], bank, ACT.Relu, scale=1.0 / (XN_S * W_S)).then_inc(eq_done, 1)
                    elif stage[0] == "a":
                        f.n += 4
                    elif stage == "rows0":
                        f.n += 1

                def copy_sums(g):
                    act.wait_ge(av_done, b * NG + g + 1)
                    if g > 0:
                        act.wait_ge(filled, out_end)
                    elif has_prev:
                        act.wait_ge(filled, b * FILLS + ND)
                    nc.scalar.activation(oT[:, :], ps_av[:, :], ACT.Copy).then_inc(oT_done, 1)
                    nc.scalar.activation(sumT[:, :], ps_sum[:, :], ACT.Copy).then_inc(oT_done, 1)
                for g in range(NG):
                    for t in range(NS):
                        tick = g * 4 + t
                        for pair in range(2):
                            n = b * 64 + 2 * tick + pair
                            act.wait_ge(s2_filled, n + 1)
                            if pair == 0:
                                if tick >= 2:
                                    back = tick - 2
                                    if back % 4 == 3:
                                        act.wait_ge(av_done, b * NG + back // 4 + 1)
                                    else:
                                        act.wait_ge(av_tick, b * NG * 3 + (back // 4) * 3 + back % 4 + 1)
                                elif has_prev:
                                    act.wait_ge(av_done, b * NG)
                            nc.scalar.activation(probs[:, tick % 2, 2 * pair:2 * pair + 2, :], score[pair][:, :, :], ACT.Exp,
                                                 scale=DH ** -0.5 / (QK_S * QK_S)).then_inc(exp_done, 1)
                        if t == 1 and g + 1 < NG:
                            f.n += 1
                        if g + 2 < NG:
                            f.n += 4
                        if g == NG - 1:
                            f.n += 1
                        if t == 0 and g > 0:
                            copy_sums(g - 1)
                        if has_next and (g, t) in XT_AT:
                            n = f.next()
                            xn_hi(n, (f.n - 1) % 2, XT_AT[g, t])
                        if t == 2 and g > 0:
                            f.n += 2
                            out_end = f.now()
                copy_sums(NG - 1)

            loop_first_last(act, nb, 1, batch)

        @block.vector
        def _(dve):
            dve.wait_ge(mix1, 1)
            nc.vector.tensor_scalar(mixw[:, 2:3], mixw[:, 1:2], 1.0, None, ALU.add).then_inc(dve_step, 1)
            dve.wait_ge(dve_step, 1)
            nc.vector.reciprocal(mixw[:, 3:4], mixw[:, 2:3]).then_inc(dve_step, 1)
            dve.wait_ge(dve_step, 2)
            nc.vector.tensor_scalar(mixw[:, 4:5], mixw[:, 3:4], -1.0, 1.0, ALU.mult, ALU.add).then_inc(dve_step, 1)
            dve.wait_ge(dve_step, 3)
            for n in range(2 * N_W):
                dve.wait_ge(w_hi_done, n + 1)
                rows = (slice(None), slice(4 * (n % 2), 4 * (n % 2) + 4), slice((n // 2) * P, (n // 2 + 1) * P))
                nc.vector.scalar_tensor_tensor(out=w_lo[rows], in0=misc[n % 2][:, :].rearrange("p (k e) -> p k e", k=4), scalar=W_S,
                                               in1=w_hi[rows], op0=ALU.mult, op1=ALU.subtract).then_inc(w_done, 1)

            def bn(n, st):
                if st == 0:
                    dve.wait_ge(xin_in, 16 * (n + 1))
                for h in range(2):
                    nc.vector.bn_stats(out=stats[:, st, h, :], in_=xin[:, st, h * 512:(h + 1) * 512]).then_inc(bn_step, 1)
                wait_on_cell(nc, cell[:, :], dve, bn_step, n * 2 * NS + 2 * st + 2)
                nc.vector.bn_aggr(out=mv[:, st, :], in_=stats[:, st, :, :]).then_inc(aggr_step, 1)
                if st == NS - 1:
                    dve.wait_ge(aggr_step, n * NS + NS)
                    nc.vector.tensor_scalar(veps[:, :], mv[:, :, 1], LN_EPS, None, ALU.add).then_inc(stats_done, 1)

            def normalise(n, st):
                dve.wait_ge(rstd_done, n + 1)
                nc.vector.tensor_scalar(xin[:, st, :], xin[:, st, :], mv[:, st, 0:1], rstd[:, st:st + 1], ALU.subtract, ALU.mult).then_inc(norm_done, 1)

            def xn_lo(n_fill, n_hi, slot, kk):
                dve.wait_ge(hi_done, n_hi + 1)
                nc.vector.scalar_tensor_tensor(out=xT_lo[:, kk, :], in0=misc[slot][:, :], scalar=XN_S, in1=xT_hi[:, kk, :],
                                               op0=ALU.mult, op1=ALU.subtract).then_inc(freed, 1)

            for st in range(NS):
                bn(0, st)
            for st in range(NS):
                normalise(0, st)
            for kk in range(ND):
                xn_lo(kk, kk, kk % 2, kk)

            def batch(b, has_prev, has_next):
                f = Count(b * FILLS + ND)
                his = Count(b * HIS + ND)

                def bank_ready(f=f):
                    n = f.next()
                    dve.wait_ge(filled, n + 1)
                    return misc[(f.n - 1) % 2]

                def maximum_of(g, chunk, c):
                    bank = bank_ready()
                    nc.vector.reduce_max(maxima[:, g % 2, chunk, c:c + 1], bank[:, :], AX_X).then_inc(freed, 1)

                def mem_mix(qq, st):
                    bank = bank_ready()
                    k = Count(b * 32 + (qq * 4 + st) * 2)
                    nc.vector.reciprocal(den[:, st % 2, 0:1], bank[:, DKV:DKV + 1]).then_inc(mem_step, 1)
                    dve.wait_ge(mem_step, k.next() + 1)
                    nc.vector.tensor_scalar(den[:, st % 2, 1:2], den[:, st % 2, 0:1], mixw[:, 3:4], None, ALU.mult).then_inc(mem_step, 1)
                    dve.wait_ge(mem_step, k.next() + 1)
                    part = xres[:, st, qq * DKV:(qq + 1) * DKV]
                    nc.vector.scalar_tensor_tensor(out=part, in0=bank[:, 0:DKV], scalar=den[:, st % 2, 1:2], in1=part,
                                                   op0=ALU.mult, op1=ALU.add).then_inc(freed, 1)

                def rows_out(g):
                    bank = bank_ready()
                    if g >= 2:
                        dve.wait_ge(ms_in[g % 2], 16 * (b * 4 + g // 2))
                    elif has_prev:
                        dve.wait_ge(ms_in[g % 2], 16 * (b * 4))
                    nc.vector.tensor_scalar(mrow[:, g % 2, :], bank[0:16, 0:P], -1.0 / (QK_S * QK_S), None, ALU.mult).then_inc(freed, 1)

                def attn_mix(g, n, f):
                    bank = bank_ready(f)
                    nc.vector.reciprocal(rsum[:, 0, :], bank[:, 0:4 * NS]).then_inc(freed, 1)
                    dve.wait_ge(freed, f.now())
                    nc.vector.tensor_scalar(rsum[:, 1, :], rsum[:, 0, :], mixw[:, 4:5], None, ALU.mult).then_inc(quot_step, 1)
                    dve.wait_ge(quot_step, n + 1)
                    bank = bank_ready(f)
                    nc.vector.tensor_tensor(mixed[:, :].rearrange("p (h d) -> p h d", d=DH), bank[:, :].rearrange("p (h d) -> p h d", d=DH),
                                            rsum[:, 1, :].unsqueeze(2).to_broadcast([P, 4 * NS, DH]), ALU.mult).then_inc(freed, 1)
                    part = xres[:, :, g * P:(g + 1) * P]
                    dve.wait_ge(freed, f.now())
                    nc.vector.tensor_tensor(part, part, mixed[:, :].rearrange("p (s e) -> p s e", s=NS), ALU.add).then_inc(mixed_done, 1)

                for stage in PROJ:
                    chunk = s1_chunk(stage)
                    if chunk is not None and stage[0] != "a":
                        for c in range(4):
                            maximum_of(chunk // 4, chunk % 4, c)
                    if stage[0] in "kq":
                        tile = int(stage[1]) + (2 if stage[0] == "q" else 0)
                        bank = score[tile % 2][:, 0, :]
                        dve.wait_ge(hi_done, his.next() + 1)
                        if stage[0] == "q":
                            dve.wait_ge(eq_done, b * 8 + tile - 1)
                        nc.vector.scalar_tensor_tensor(out=qk_lo[:, tile % 4, :], in0=bank, scalar=QK_S / (XN_S * W_S),
                                                       in1=qk_hi[:, tile % 4, :], op0=ALU.mult, op1=ALU.subtract).then_inc(pr_freed, 1)
                        if stage[0] == "q":
                            e = eq[:, tile % 2, :]
                            nc.vector.tensor_scalar(e, e, 1.0, 0.0, ALU.subtract, ALU.min).then_inc(elu_step, 1)
                    elif stage[0] == "v":
                        i = int(stage[1])
                        dve.wait_ge(pr_filled, b * 12 + 10 + i + 1)
                        nc.vector.tensor_scalar(v[:, 2 * i:2 * i + 2, :], score[i][:, 0, :].rearrange("p (s e) -> p s e", s=2),
                                                1.0 / (XN_S * W_S), None, ALU.mult).then_inc(pr_freed, 1)
                    elif stage == "rows0":
                        rows_out(0)
                    else:
                        if stage == "am0":
                            dve.wait_ge(xres_in, 16 * (b + 1))
                        for st in range(NS):
                            if chunk is not None:
                                maximum_of(chunk // 4, chunk % 4, st)
                            mem_mix(int(stage[2]), st)
                    if stage == "k0" and has_prev:
                        attn_mix(NG - 1, b * NG - 1, Count(b * FILLS + ND - 2))

                for g in range(NG):
                    for t in range(NS):
                        if t == 1 and g + 1 < NG:
                            rows_out(g + 1)
                        if g + 2 < NG:
                            for c in range(4):
                                maximum_of(g + 2, t, c)
                        if g == NG - 1:
                            mem_mix(3, t)
                        if has_next and g == 0:
                            bn(b + 1, t)
                        if has_next and g == 1:
                            normalise(b + 1, t)
                        if has_next and (g, t) in XT_AT:
                            n = f.next()
                            xn_lo(n, his.next(), (f.n - 1) % 2, XT_AT[g, t])
                        if t == 2 and g > 0:
                            attn_mix(g - 1, b * NG + g - 1, f)
                if not has_next:
                    attn_mix(NG - 1, (b + 1) * NG - 1, f)
                assert f.n == fill_plan(has_next)["all"] - 2 * has_next, f.n

            loop_first_last(dve, nb, 1, batch)


def filter_phase(nc, k, k_pad):
    with (
        nc.sbuf_tensor("f_k", [NHC, P + D], F32) as kf,
        nc.sbuf_tensor("f_hi", [NHC, P + D], F16) as k_hi,
        nc.sbuf_tensor("f_lo", [NHC, P + D], F16) as k_lo,
        nc.semaphore("f_zero") as zeroed,
        nc.semaphore("f_in") as k_in,
        nc.semaphore("f_split") as split,
        nc.semaphore("f_out") as k_out,
        nc.Block() as block,
    ):
        @block.vector
        def _(dve):
            nc.vector.memset(kf[:, 0:P], 0.0).then_inc(zeroed, 1)
            dve.wait_ge(zeroed, 1)
            dve.wait_ge(k_in, 16)
            nc.vector.tensor_scalar(k_hi[:, :], kf[:, :], T_S, None, ALU.mult).then_inc(split, 1)
            dve.wait_ge(split, 1)
            nc.vector.scalar_tensor_tensor(out=k_lo[:, :], in0=kf[:, :], scalar=T_S, in1=k_hi[:, :],
                                           op0=ALU.mult, op1=ALU.subtract).then_inc(split, 1)

        @block.sync
        def _(sp):
            sp.dma_start(kf[:, P:P + D], k).then_inc(k_in, 16)
            sp.wait_ge(split, 2)
            sp.dma_start(k_pad[0], k_hi[:, :]).then_inc(k_out, 16)
            sp.dma_start(k_pad[1], k_lo[:, :]).then_inc(k_out, 16)
            sp.wait_ge(k_out, 32)


def copy_toeplitz(sp, k_pad, toeplitz, toe_done, part):
    h0 = part * NHC // TOE_PARTS
    for half in range(2):
        rows = k_pad[half, h0, P:]
        shifted = bass.AP(rows.tensor, rows.offset, [[P + D, NHC // TOE_PARTS], [-1, P], [1, D]])
        sp.dma_start(toeplitz[h0:h0 + NHC // TOE_PARTS, :, half, :], shifted).then_inc(toe_done, 16)


def conv_phase(nc, x1, ctx_in, toeplitz, toe_done, skip, ident_in, x2, absmax, moments, nh):
    NL = D // P
    NP = HX * P
    with ExitStack() as ctx:
        def sb(name, shape, dt=F32):
            return ctx.enter_context(nc.sbuf_tensor(name, shape, dt))

        def sem(name):
            return ctx.enter_context(nc.semaphore(name))

        ident = sb("c_ident", [P, P])
        xh = sb("c_xh", [P, 2, D])
        ch = sb("c_ch", [P, 2, D])
        xres = sb("c_xres", [P, 2, D])
        vh = sb("c_vh", [P, D])
        vT = sb("c_vT", [P, NL, P])
        uT = sb("c_uT", [P, 2, NL, P])
        gT = sb("c_gT", [P, 2, NL, P])
        toe = sb("c_toe", [P, 2, 2, D], F16)
        u = sb("c_u", [P, 3, NP])
        u_hi = sb("c_u_hi", [P, 2, NL, NP], F16)
        u_lo = sb("c_u_lo", [P, 2, NL, NP], F16)
        z = sb("c_z", [P, 2, NP])
        tree = sb("c_tree", [P, 2, NP // 2])
        skp = sb("c_skp", [P, NHC, HX])
        sterm = sb("c_sterm", [P, 2, NL, P])
        st1 = sb("c_st1", [P, NL, P])
        oT = sb("c_oT", [P, 2, NL, P])
        zn = sb("c_zn", [P, D])
        stats = sb("c_stats", [P, 2, 6])
        mv = sb("c_mv", [P, 2])
        rstd = sb("c_rstd", [P, 1])
        stats2 = sb("c_stats2", [P, 2, 6])
        veps = sb("c_veps", [P, 2])
        cell = sb("c_cell", [P, 1])
        mv2 = sb("c_mv2", [P, 2])
        mhalf = sb("c_mhalf", [P, 1])

        bankT = [ctx.enter_context(nc.psum_tensor(f"c_bt{i}", [P, 512], F32)) for i in range(4)]
        y = [ctx.enter_context(nc.psum_tensor(f"c_y{i}", [P, 2, 512], F32)) for i in range(2)]

        const_in = sem("c_const_in")
        ready = sem("c_ready")
        skp_done = sem("c_skp_done")
        x_in = [sem(f"c_x_in{i}") for i in range(2)]
        c_in = [sem(f"c_c_in{i}") for i in range(2)]
        t_in = [sem(f"c_t_in{i}") for i in range(2)]
        x2_out = [sem(f"c_x2_out{i}") for i in range(2)]
        bn_step = sem("c_bn_step")
        veps_done = sem("c_veps_done")
        rstd_done = sem("c_rstd_done")
        rstd2_done = sem("c_rstd2_done")
        vh_done = sem("c_vh_done")
        res_done = sem("c_res_done")
        tr_filled = sem("c_tr_filled")
        tr_read = sem("c_tr_read")
        bk_filled = sem("c_bk_filled")
        bk_read = sem("c_bk_read")
        u_done = sem("c_u_done")
        hi_done = sem("c_hi_done")
        lo_done = sem("c_lo_done")
        y_done = sem("c_y_done")
        z_done = sem("c_z_done")
        tree_step = sem("c_tree_step")
        o_done = sem("c_o_done")
        skip_step = sem("c_skip_step")
        bn2_step = sem("c_bn2_step")
        zn_done = sem("c_zn_done")
        veps2_done = sem("c_veps2_done")

        block = ctx.enter_context(nc.Block())

        rows_x1 = x1.rearrange("b (h i) d -> h b i d", i=HX)
        rows_c = ctx_in.rearrange("b (h i) d -> h b i d", i=HX)

        @block.sync
        def _(sp):
            sp.dma_start(ident[:, :], ident_in).then_inc(const_in, 16)
            sp.dma_start(skp[:, :, :], skip.rearrange("(a h i) -> a h i", a=1, i=HX).to_broadcast([P, NHC, HX])).then_inc(const_in, 16)

            def load_filter(h, q):
                sp.dma_start(toe[:, q, :, :], toeplitz[h]).then_inc(t_in[q], 16)

            def load_rows(h, q):
                sp.dma_start(xh[:, q, :], rows_x1[h]).then_inc(x_in[q], 16)
                sp.dma_start(ch[:, q, :], rows_c[h]).then_inc(c_in[q], 16)

            load_rows(0, 0)
            load_rows(1, 1)
            sp.wait_ge(toe_done, TOE_DONE)
            load_filter(0, 0)

            def channel(h, pair, q, has_prev, has_next, ahead):
                if has_next:
                    if has_prev:
                        sp.wait_ge(y_done, h * NL)
                    load_filter(h + 1, 1 - q)
                if ahead:
                    sp.wait_ge(res_done, h + 1)
                    if not has_prev:
                        sp.wait_ge(tr_filled, 4)
                    load_rows(h + 2, q)
                if has_prev:
                    sp.wait_ge(bk_read, 2 * h)
                    sp.dma_start(x2[h - 1], xres[:, 1 - q, :]).then_inc(x2_out[1 - q], 16)

            channel_loop(sp, nh, channel)
            sp.wait_ge(bk_read, 2 * nh)
            sp.dma_start(x2[nh - 1], xres[:, (nh - 1) % 2, :]).then_inc(x2_out[(nh - 1) % 2], 16)
            for i in range(2):
                sp.wait_ge(x2_out[i], 16 * (nh // 2))

        @block.gpsimd
        def _(pool):
            nc.gpsimd.memset(mhalf[:, :], -0.5).then_inc(ready, 1)
            pool.wait_ge(const_in, 32)
            nc.gpsimd.tensor_scalar(skp[:, :, :], skp[:, :, :], T_S, None, ALU.mult).then_inc(skp_done, 1)
            pool.wait_ge(ready, 1)
            pool.wait_ge(skp_done, 1)

            def skip_share(h, q):
                pool.wait_ge(tr_read, 4 * (h + 1))
                n = Count(h * 6)
                nc.gpsimd.tensor_tensor(st1[:, :, :], vT[:, :, :], gT[:, q, :, :], ALU.mult).then_inc(skip_step, 1)
                pool.wait_ge(skip_step, n.next() + 1)
                s = st1[:, :, :].rearrange("p c (b i) -> p (c b) i", i=HX)
                w = skp[:, h, :].unsqueeze(1).to_broadcast([P, P, HX])
                nc.gpsimd.tensor_tensor(s, s, w, ALU.mult).then_inc(skip_step, 1)
                for width in (4, 2, 1):
                    pool.wait_ge(skip_step, n.next() + 1)
                    nc.gpsimd.tensor_tensor(s[:, :, 0:width], s[:, :, 0:width], s[:, :, width:2 * width], ALU.add).then_inc(skip_step, 1)
                pool.wait_ge(skip_step, n.next() + 1)
                nc.gpsimd.tensor_tensor(sterm[:, q, :, :].rearrange("p c (b j) -> p (c b) j", j=HX),
                                        uT[:, q, :, :].rearrange("p c (b j) -> p (c b) j", j=HX),
                                        s[:, :, 0:1].to_broadcast([P, P, HX]), ALU.mult).then_inc(skip_step, 1)
                n.next()

            def norm_scale1(h):
                pool.wait_ge(veps_done, h + 1)
                nc.gpsimd.tensor_tensor(rstd[:, :], veps[:, 0:1], mhalf[:, :], ALU.pow).then_inc(rstd_done, 1)

            def norm_scale2(h):
                pool.wait_ge(veps2_done, h + 1)
                nc.gpsimd.tensor_tensor(mv2[:, 1:2], veps[:, 1:2], mhalf[:, :], ALU.pow).then_inc(rstd2_done, 1)

            def sum_block(h, q, a):
                n = Count(h * NL * 3 + a * 3)
                pool.wait_ge(z_done, h * NL + a + 1)
                wait(pool, o_done, h * NL + a - 1)
                zz, tr = z[:, a % 2, :], tree[:, a % 2, :]
                nc.gpsimd.tensor_tensor(tr[:, 0:512], zz[:, 0:512], zz[:, 512:1024], ALU.add).then_inc(tree_step, 1)
                pool.wait_ge(tree_step, n.next() + 1)
                nc.gpsimd.tensor_tensor(tr[:, 0:256], tr[:, 0:256], tr[:, 256:512], ALU.add).then_inc(tree_step, 1)
                pool.wait_ge(tree_step, n.next() + 1)
                nc.gpsimd.tensor_tensor(tr[:, 0:128], tr[:, 0:128], tr[:, 128:256], ALU.add).then_inc(tree_step, 1)
                pool.wait_ge(tree_step, n.next() + 1)
                nc.gpsimd.tensor_tensor(oT[:, q, a, :], tr[:, 0:128], sterm[:, q, a, :], ALU.add).then_inc(o_done, 1)

            norm_scale1(0)
            skip_share(0, 0)

            norm_scale1(1)

            def channel(h, pair, q, has_prev, has_next, ahead):
                for a in range(NL):
                    if a == 2 and has_next:
                        skip_share(h + 1, 1 - q)
                    if a == 3 and has_prev:
                        norm_scale2(h - 1)
                    if a == 4 and ahead:
                        norm_scale1(h + 2)
                    sum_block(h, q, a)

            channel_loop(pool, nh, channel)
            norm_scale2(nh - 1)

        @block.tensor
        def _(pe):
            pe.wait_ge(const_in, 32)

            def forward(h, q):
                pe.wait_ge(vh_done, h + 1)
                for src in range(2):
                    if src:
                        pe.wait_ge(c_in[q], pair_count(h, q))
                    for c in range(2):
                        wait(pe, tr_read, 4 * h + 2 * src + c - 1)
                        for k in range(4):
                            cols = slice((4 * c + k) * P, (4 * c + k + 1) * P)
                            m = nc.tensor.transpose(bankT[c][:, k * P:(k + 1) * P], vh[:, cols] if src == 0 else ch[:, q, cols], ident[:, :])
                        m.then_inc(tr_filled, 1)

            def backward(h, q):
                for c in range(2):
                    pe.wait_ge(o_done, h * NL + 4 * c + 4)
                    wait(pe, bk_read, 2 * h + c - 1)
                    for k in range(4):
                        m = nc.tensor.transpose(bankT[2 + c][:, k * P:(k + 1) * P], oT[:, q, 4 * c + k, :], ident[:, :])
                    m.then_inc(bk_filled, 1)

            def conv(h, q, a):
                wait(pe, z_done, h * NL + a - 1)
                for c in range(a + 1):
                    wt_hi = toe[:, q, 0, (a - c) * P:(a - c + 1) * P]
                    wt_lo = toe[:, q, 1, (a - c) * P:(a - c + 1) * P]
                    if c == a:
                        pe.wait_ge(lo_done, h * NL + a + 1)
                    for wt, src, first, last in ((wt_hi, u_hi, True, False), (wt_hi, u_lo, False, False), (wt_lo, u_hi, False, True)):
                        for n in range(2):
                            m = nc.tensor.matmul(y[a % 2][:, n, :], wt, src[:, q, c, n * 512:(n + 1) * 512],
                                                 start=(first and c == 0), stop=(last and c == a))
                m.then_inc(y_done, 1)

            forward(0, 0)

            def channel(h, pair, q, has_prev, has_next, ahead):
                if has_next:
                    forward(h + 1, 1 - q)
                pe.wait_ge(t_in[q], pair_count(h, q))
                for a in range(NL):
                    if a == 3 and has_prev:
                        backward(h - 1, 1 - q)
                    conv(h, q, a)

            channel_loop(pe, nh, channel)
            backward(nh - 1, (nh - 1) % 2)

        @block.scalar
        def _(act):
            def evacuate(h, q):
                for n in range(4):
                    src, c = n // 2, n % 2
                    act.wait_ge(tr_filled, 4 * h + n + 1)
                    bank, blocks = bankT[c][:, :].rearrange("p (k e) -> p k e", k=4), slice(4 * c, 4 * c + 4)
                    if src == 0:
                        if n == 0:
                            wait(act, u_done, NL * h)
                            wait(act, skip_step, 6 * h)
                        nc.scalar.activation(vT[:, blocks, :], bank, ACT.Copy).then_inc(tr_read, 1)
                    else:
                        if n == 2:
                            wait(act, z_done, NL * (h - 1))
                        nc.scalar.activation(uT[:, q, blocks, :], bank, ACT.Copy, scale=U_S)
                        nc.scalar.activation(gT[:, q, blocks, :], bank, ACT.Copy, scale=1.0 / (T_S * U_S)).then_inc(tr_read, 1)

            def residual(h, q):
                act.wait_ge(x_in[q], pair_count(h, q))
                wait(act, x2_out[q], pair_count(h, q) - 16)
                wait(act, zn_done, h - 1)
                nc.scalar.activation(xres[:, q, :], xh[:, q, :], ACT.Copy).then_inc(res_done, 1)

            def high(h, q, c):
                act.wait_ge(u_done, h * NL + c + 1)
                if c == 0:
                    wait(act, y_done, NL * (h - 1))
                nc.scalar.activation(u_hi[:, q, c, :], u[:, c % 3, :], ACT.Copy).then_inc(hi_done, 1)

            residual(0, 0)
            evacuate(0, 0)
            for c in range(NL):
                high(0, 0, c)

            def channel(h, pair, q, has_prev, has_next, ahead):
                if has_next:
                    evacuate(h + 1, 1 - q)
                    for c in range(NL):
                        high(h + 1, 1 - q, c)
                    residual(h + 1, 1 - q)

            channel_loop(act, nh, channel)

        @block.vector
        def _(dve):
            def normalise(h, q):
                dve.wait_ge(x_in[q], pair_count(h, q))
                for c in range(2):
                    nc.vector.bn_stats(out=stats[:, c, :], in_=xh[:, q, c * 512:(c + 1) * 512]).then_inc(bn_step, 1)
                wait_on_cell(nc, cell[:, :], dve, bn_step, 3 * h + 2)
                nc.vector.bn_aggr(out=mv[:, :], in_=stats[:, :, :]).then_inc(bn_step, 1)
                dve.wait_ge(bn_step, 3 * h + 3)
                nc.vector.tensor_scalar(veps[:, 0:1], mv[:, 1:2], LN_EPS, None, ALU.add).then_inc(veps_done, 1)

            def normalise_end(h, q):
                dve.wait_ge(rstd_done, h + 1)
                wait(dve, tr_filled, 4 * h - 2)
                nc.vector.tensor_scalar(vh[:, :], xh[:, q, :], mv[:, 0:1], rstd[:, :], ALU.subtract, ALU.mult).then_inc(vh_done, 1)

            def product(h, q, c):
                if c == 0:
                    dve.wait_ge(tr_read, 4 * (h + 1))
                wait(dve, lo_done, h * NL + c - 2)
                n = nc.vector.tensor_tensor(u[:, c % 3, :].rearrange("p (i b j) -> p i b j", i=HX, j=HX),
                                            vT[:, c, :].rearrange("p (b i) -> p i b", i=HX).unsqueeze(3).to_broadcast([P, HX, B, HX]),
                                            uT[:, q, c, :].rearrange("p (b j) -> p b j", j=HX).unsqueeze(1).to_broadcast([P, HX, B, HX]),
                                            ALU.mult)
                n.then_inc(u_done, 1)

            def low(h, q, c):
                dve.wait_ge(hi_done, h * NL + c + 1)
                nc.vector.tensor_tensor(u_lo[:, q, c, :], u[:, c % 3, :], u_hi[:, q, c, :], ALU.subtract).then_inc(lo_done, 1)

            def gate(h, q, a):
                dve.wait_ge(y_done, h * NL + a + 1)
                wait(dve, tree_step, 3 * (h * NL + a - 1) - 2)
                nc.vector.tensor_tensor(z[:, a % 2, :].rearrange("p (i b j) -> p i b j", i=HX, j=HX),
                                        y[a % 2][:, :, :].rearrange("p n (i b j) -> p (n i) b j", i=HX // 2, j=HX),
                                        gT[:, q, a, :].rearrange("p (b i) -> p i b", i=HX).unsqueeze(3).to_broadcast([P, HX, B, HX]),
                                        ALU.mult).then_inc(z_done, 1)

            def add_result(h, q):
                dve.wait_ge(res_done, h + 1)
                for c in range(2):
                    dve.wait_ge(bk_filled, 2 * h + c + 1)
                    part = xres[:, q, c * 512:(c + 1) * 512]
                    nc.vector.tensor_tensor(part, part, bankT[2 + c][:, :], ALU.add).then_inc(bk_read, 1)
                for c in range(2):
                    dve.wait_ge(bk_read, 2 * h + c + 1)
                    nc.vector.bn_stats(out=stats2[:, c, :], in_=xres[:, q, c * 512:(c + 1) * 512]).then_inc(bn2_step, 1)
                wait_on_cell(nc, cell[:, :], dve, bn2_step, 3 * h + 2)
                nc.vector.bn_aggr(out=mv2[:, 0:2], in_=stats2[:, :, :]).then_inc(bn2_step, 1)
                dve.wait_ge(bn2_step, 3 * h + 3)
                nc.vector.tensor_scalar(veps[:, 1:2], mv2[:, 1:2], LN_EPS, None, ALU.add).then_inc(veps2_done, 1)

            def largest(h, q):
                dve.wait_ge(rstd2_done, h + 1)
                nc.vector.tensor_scalar(zn[:, :], xres[:, q, :], mv2[:, 0:1], mv2[:, 1:2], ALU.subtract, ALU.mult).then_inc(zn_done, 1)
                nc.vector.tensor_copy(moments[:, h, :], mv2[:, 0:2])
                dve.wait_ge(zn_done, h + 1)
                nc.vector.tensor_reduce(absmax[:, bass.ds(h, 1)], zn[:, :], axis=AX_X, op=ALU.max, apply_absolute_value=True)

            normalise(0, 0)
            normalise_end(0, 0)
            product(0, 0, 0)
            for c in range(NL):
                if c + 1 < NL:
                    product(0, 0, c + 1)
                low(0, 0, c)

            normalise(1, 1)
            normalise_end(1, 1)

            def channel(h, pair, q, has_prev, has_next, ahead):
                c = 0
                for a in range(NL):
                    if has_next and a >= 2:
                        for _ in range(2 if a in (4, 5) else 1):
                            product(h + 1, 1 - q, c)
                            if c:
                                low(h + 1, 1 - q, c - 1)
                            c += 1
                        if a == NL - 1:
                            low(h + 1, 1 - q, NL - 1)
                    if a == 3 and has_prev:
                        add_result(h - 1, 1 - q)
                    if a == 4 and ahead:
                        normalise(h + 2, q)
                    if a == 5 and has_prev:
                        largest(h - 1, 1 - q)
                    if a == 6 and ahead:
                        normalise_end(h + 2, q)
                    gate(h, q, a)

            channel_loop(dve, nh, channel)
            add_result(nh - 1, (nh - 1) % 2)
            largest(nh - 1, (nh - 1) % 2)


def channel_loop(eng, n, body):
    for q in range(2):
        body(q, 0, q, q > 0, True, True)
    if n > 4:
        with eng.Fori(1, n // 2 - 1) as pair:
            for q in range(2):
                body(pair * 2 + q, pair, q, True, True, True)
    for q in range(2):
        body(n - 2 + q, n // 2 - 1, q, True, q == 0, False)


def pair_count(h, q):
    return (h - q) * 8 + 16


def ffn_phase(nc, x2, weight, weight_scale, bias, ident_in, absmax, moments, out, nt):
    NT3 = 3
    with ExitStack() as ctx:
        def sb(name, shape, dt=F32):
            return ctx.enter_context(nc.sbuf_tensor(name, shape, dt))

        def sem(name):
            return ctx.enter_context(nc.semaphore(name))

        ident = sb("g_ident", [P, P])
        ident16 = sb("g_ident16", [P, P], F16)
        ones = sb("g_ones", [1, P])
        wrow = sb("g_wrow", [P, 4, D])
        w_hi = sb("g_w_hi", [P, ND, D], F16)
        w_lo = sb("g_w_lo", [P, ND, D], F16)
        wscale = sb("g_wscale", [P, 2])
        bias_all = sb("g_bias", [P, D])
        top = sb("g_top", [P, 1])
        row = sb("g_row", [1, P + 4])
        inv = sb("g_inv", [P, 1])
        gain = sb("g_gain", [P, NHC])
        xt = sb("g_xt", [P, 4, D])
        xb = sb("g_xb", [P, 2, D])
        zt = sb("g_zt", [P, 2, D])
        power = sb("g_power", [P, 2, D])
        xq = sb("g_xq", [P, 2, D], F16)
        xqT = sb("g_xqT", [P, 2, ND, P], F16)
        res = sb("g_res", [P, 2, D])

        bank = [ctx.enter_context(nc.psum_tensor(f"g_b{i}", [P, 512], F32)) for i in range(2)]
        bankT = [ctx.enter_context(nc.psum_tensor(f"g_t{i}", [P, ND, P], F16)) for i in range(2)]
        acc = [ctx.enter_context(nc.psum_tensor(f"g_acc{i}", [P, 2, 512], F32)) for i in range(2)]

        const_in = sem("g_const_in")
        w_in = [sem(f"g_w_in{i}") for i in range(4)]
        w_filled = sem("g_w_filled")
        w_hi_done = sem("g_w_hi_done")
        w_done = sem("g_w_done")
        id16_done = sem("g_id16_done")
        ones_done = sem("g_ones_done")
        ws_done = sem("g_ws_done")
        top_step = sem("g_top_step")
        top_T = sem("g_top_T")
        top_B = sem("g_top_B")
        x_in = [sem(f"g_x_in{i}") for i in range(4)]
        xb_done = sem("g_xb_done")
        z_step = sem("g_z_step")
        sum_step = sem("g_sum_step")
        xq_done = sem("g_xq_done")
        tr_done = sem("g_tr_done")
        xqT_done = sem("g_xqT_done")
        mm_done = sem("g_mm_done")
        res_done = sem("g_res_done")
        stored = [sem(f"g_stored{i}") for i in range(2)]

        block = ctx.enter_context(nc.Block())
        rows_out = out.rearrange("b (h i) d -> h b i d", i=HX)

        @block.sync
        def _(sp):
            sp.dma_start(ident[:, :], ident_in).then_inc(const_in, 16)
            sp.dma_start(wscale[:, 0:1], weight_scale.to_broadcast([P, 1])).then_inc(const_in, 16)
            sp.dma_start(bias_all[:, :], bias.rearrange("(a n) -> a n", a=1).to_broadcast([P, D])).then_inc(const_in, 16)
            for n in range(ND):
                wait(sp, w_done, 2 * (n - 3))
                sp.dma_start(wrow[:, n % 4, :], weight[n * P:(n + 1) * P, :]).then_inc(w_in[n % 4], 16)
            for n in range(NT3):
                sp.dma_start(xt[:, n, :], x2[n]).then_inc(x_in[n], 16)

            def tile(n, quad, r):
                if n_static(n) is None or n + NT3 < nt:
                    wait(sp, xb_done, n)
                    wait(sp, xq_done, n)
                    sp.dma_start(xt[:, (r + NT3) % 4, :], x2[n + NT3]).then_inc(x_in[(r + NT3) % 4], 16)
                sp.wait_ge(res_done, n + 1)
                sp.dma_start(rows_out[n], res[:, r % 2, :]).then_inc(stored[r % 2], 16)

            quad_loop(sp, nt, tile)
            for i in range(2):
                sp.wait_ge(stored[i], 16 * (nt // 2))

        @block.gpsimd
        def _(pool):
            nc.gpsimd.memset(ones[:, :], 1.0).then_inc(ones_done, 1)
            pool.wait_ge(const_in, 48)

            def tile(n, quad, r):
                pool.wait_ge(x_in[r], 16 * (quad + 1))
                wait(pool, res_done, n - 1)
                nc.gpsimd.tensor_tensor(xb[:, r % 2, :], xt[:, r, :], bias_all[:, :], ALU.add).then_inc(xb_done, 1)

            quad_loop(pool, nt, tile)

        @block.tensor
        def _(pe):
            pe.wait_ge(const_in, 48)
            for n in range(ND):
                pe.wait_ge(w_in[n % 4], 16 * (n // 4 + 1))
                for c in range(2):
                    wait(pe, w_done, 2 * n + c - 1)
                    for k in range(4):
                        m = nc.tensor.transpose(bank[c][:, k * P:(k + 1) * P], wrow[:, n % 4, (4 * c + k) * P:(4 * c + k + 1) * P], ident[:, :])
                    m.then_inc(w_filled, 1)
            pe.wait_ge(w_done, 2 * ND)
            pe.wait_ge(top_step, 1)
            nc.tensor.matmul(bank[0][0:1, 0:P], top[:, :], ident[:, :], start=True, stop=True).then_inc(top_T, 1)
            pe.wait_ge(top_step, 4)
            pe.wait_ge(ones_done, 1)
            nc.tensor.matmul(bank[1][:, 0:1], ones[0:1, :], row[0:1, P + 2:P + 3], start=True, stop=True).then_inc(top_B, 1)
            pe.wait_ge(id16_done, 1)

            def transposes(n, r):
                pe.wait_ge(xq_done, n + 1)
                wait(pe, xqT_done, n - 1)
                for k in range(ND):
                    m = nc.tensor.transpose(bankT[r % 2][:, k, :], xq[:, r % 2, k * P:(k + 1) * P], ident16[:, :])
                m.then_inc(tr_done, 1)

            transposes(0, 0)

            def tile(n, quad, r):
                if n_static(n) is None or n + 1 < nt:
                    transposes(n + 1, r + 1)
                pe.wait_ge(xqT_done, n + 1)
                wait(pe, res_done, n - 1)
                for k in range(ND):
                    for w in (w_hi, w_lo):
                        for c in range(2):
                            m = nc.tensor.matmul(acc[r % 2][:, c, :], xqT[:, r % 2, k, :], w[:, k, c * 512:(c + 1) * 512],
                                                 start=(k == 0 and w is w_hi), stop=(k == ND - 1 and w is w_lo))
                m.then_inc(mm_done, 1)

            quad_loop(pe, nt, tile)

        @block.scalar
        def _(act):
            act.wait_ge(const_in, 48)
            nc.scalar.activation(wscale[:, 1:2], wscale[:, 0:1], ACT.Copy, scale=W_S).then_inc(ws_done, 1)
            nc.scalar.activation(ident16[:, :], ident[:, :], ACT.Copy).then_inc(id16_done, 1)
            act.wait_ge(ws_done, 1)
            for n in range(2 * ND):
                act.wait_ge(w_filled, n + 1)
                dst = w_hi[:, 4 * (n % 2):4 * (n % 2) + 4, (n // 2) * P:(n // 2 + 1) * P]
                nc.scalar.activation(dst, bank[n % 2][:, :].rearrange("p (k e) -> p k e", k=4), ACT.Copy, scale=wscale[:, 1:2]).then_inc(w_hi_done, 1)

            def tile(n, quad, r):
                act.wait_ge(tr_done, n + 1)
                wait(act, mm_done, n - 1)
                nc.scalar.activation(xqT[:, r % 2, :, :], bankT[r % 2][:, :, :], ACT.Copy).then_inc(xqT_done, 1)

            quad_loop(act, nt, tile)

        @block.vector
        def _(dve):
            for n in range(2 * ND):
                dve.wait_ge(w_hi_done, n + 1)
                part = (slice(None), slice(4 * (n % 2), 4 * (n % 2) + 4), slice((n // 2) * P, (n // 2 + 1) * P))
                nc.vector.scalar_tensor_tensor(out=w_lo[part], in0=bank[n % 2][:, :].rearrange("p (k e) -> p k e", k=4), scalar=wscale[:, 1:2],
                                               in1=w_hi[part], op0=ALU.mult, op1=ALU.subtract).then_inc(w_done, 1)
            nc.vector.reduce_max(top[:, :], absmax[:, 0:nt], AX_X).then_inc(top_step, 1)
            dve.wait_ge(top_T, 1)
            nc.vector.reduce_max(row[:, P:P + 1], bank[0][0:1, 0:P], AX_X).then_inc(top_step, 1)
            dve.wait_ge(top_step, 2)
            nc.vector.tensor_scalar(row[:, P + 1:P + 2], row[:, P:P + 1], 1.0 / 448.0, 1e-7, ALU.mult, ALU.max).then_inc(top_step, 1)
            dve.wait_ge(top_step, 3)
            nc.vector.reciprocal(row[:, P + 2:P + 3], row[:, P + 1:P + 2]).then_inc(top_step, 1)
            dve.wait_ge(top_B, 1)
            nc.vector.tensor_copy(inv[:, :], bank[1][:, 0:1]).then_inc(top_step, 1)
            dve.wait_ge(top_step, 5)
            nc.vector.tensor_scalar(gain[:, 0:nt], moments[:, 0:nt, 1], inv[:, :], None, ALU.mult).then_inc(top_step, 1)
            dve.wait_ge(top_step, 6)

            def quantise(n, quad, r):
                dve.wait_ge(x_in[r], 16 * (quad + 1))
                s = Count(n * 3)
                nc.vector.tensor_scalar(zt[:, r % 2, :], xt[:, r, :], moments[:, n, 0:1], gain[:, bass.ds(n, 1)], ALU.subtract, ALU.mult).then_inc(z_step, 1)
                dve.wait_ge(z_step, s.next() + 1)
                nc.vector.tensor_scalar(power[:, r % 2, :].bitcast(U32), zt[:, r % 2, :].bitcast(U32), 0x7F800000, None, ALU.bitwise_and).then_inc(z_step, 1)
                dve.wait_ge(z_step, s.next() + 1)
                nc.vector.tensor_scalar(power[:, r % 2, :], power[:, r % 2, :], 2.0 ** -6, 1.5 * 2.0 ** 20, ALU.max, ALU.mult).then_inc(z_step, 1)
                dve.wait_ge(z_step, s.next() + 1)
                nc.vector.tensor_tensor(zt[:, r % 2, :], zt[:, r % 2, :], power[:, r % 2, :], ALU.add).then_inc(sum_step, 1)
                dve.wait_ge(sum_step, n + 1)
                wait(dve, tr_done, n - 1)
                nc.vector.tensor_tensor(xq[:, r % 2, :], zt[:, r % 2, :], power[:, r % 2, :], ALU.subtract).then_inc(xq_done, 1)

            quantise(0, 0, 0)
            quantise(1, 0, 1)

            def tile(n, quad, r):
                if n_static(n) is None or n + 2 < nt:
                    quantise(n + 2, quad + (r + 2) // 4, (r + 2) % 4)
                dve.wait_ge(mm_done, n + 1)
                dve.wait_ge(xb_done, n + 1)
                wait(dve, stored[r % 2], 16 * (quad * 2 + r // 2))
                nc.vector.scalar_tensor_tensor(out=res[:, r % 2, :], in0=acc[r % 2][:, :, :].rearrange("p a n -> p (a n)"), scalar=1.0 / W_S,
                                               in1=xb[:, r % 2, :], op0=ALU.mult, op1=ALU.add).then_inc(res_done, 1)

            quad_loop(dve, nt, tile)


def n_static(n):
    return n if isinstance(n, int) else None


def quad_loop(eng, n, body):
    for r in range(4):
        body(r, 0, r)
    if n > 8:
        with eng.Fori(1, n // 4 - 1) as quad:
            for r in range(4):
                body(quad * 4 + r, quad, r)
    for r in range(4):
        body(n - 4 + r, n // 4 - 1, r)


def decoder_layer(nc, x, skip, context, Wq, Wk, Wv, memory, memory_norm, memory_weight, k, weight, weight_scale, bias, ident, out):
    x1 = nc.dram_tensor("x1_rows", [B, S, D], F32).ap()
    x2 = nc.dram_tensor("x2_rows", [NHC, P, D], F32).ap()
    k_pad = nc.dram_tensor("filter_halves", [2, NHC, P + D], F16).ap()
    toeplitz = nc.dram_tensor("toeplitz_halves", [NHC, P, 2, D], F16).ap()
    with (
        nc.sbuf_tensor("absmax", [P, NHC], F32) as absmax,
        nc.semaphore("toe_done") as toe_done,
        nc.sbuf_tensor("moments", [P, NHC, 2], F32) as moments,
    ):
        filter_phase(nc, k, k_pad)
        attention_phase(nc, x, Wq, Wk, Wv, memory, memory_norm, memory_weight, ident, k_pad, toeplitz, toe_done, x1, B)
        conv_phase(nc, x1, context, toeplitz, toe_done, skip, ident, x2, absmax, moments, NHC)
        ffn_phase(nc, x2, weight, weight_scale, bias, ident, absmax, moments, out, NHC)


_INS = ['x', 'fside_S2_0', 'ctx_2048', 'L0_attn_Wq', 'L0_attn_Wk', 'L0_attn_Wv', 'L0_attn_memory', 'L0_attn_memory_norm',
        'L0_attn_memory_weight', 'L0_xattn_k', 'L0_ffn_weight', 'L0_ffn_weight_scale', 'L0_ffn_bias']


def kernel(**inputs):
    import numpy as np
    import concourse.bacc as bacc
    from concourse.bass_utils import run_bass_kernel_spmd

    nc = bacc.Bacc("TRN2", target_bir_lowering=False, num_devices=1)
    arrays, args = {}, []
    for name in _INS:
        a = np.ascontiguousarray(inputs[name])
        if a.ndim == 0:
            a = a.reshape(1, 1)
        arrays[f"in_{name}"] = a
        args.append(nc.dram_tensor(f"in_{name}", a.shape, mybir.dt.from_np(a.dtype), kind="ExternalInput").ap())
    ident = np.eye(P, dtype=np.float32)
    arrays["in_ident"] = ident
    args.append(nc.dram_tensor("in_ident", ident.shape, F32, kind="ExternalInput").ap())
    args.append(nc.dram_tensor("out_0", (B, S, D), F32, kind="ExternalOutput").ap())
    decoder_layer(nc, *args)
    r = run_bass_kernel_spmd(nc, [arrays], core_ids=[0])
    return r.results[0]["out_0"]
```

```python
import concourse.bass as bass
from concourse import mybir
from contextlib import ExitStack

P = 128
F32 = mybir.dt.float32
F16 = mybir.dt.float16
U32 = mybir.dt.uint32
ALU = mybir.AluOpType
ACT = mybir.ActivationFunctionType
AX_X = mybir.AxisListType.X

B, S, D = 16, 512, 1024
NQ, NH, DH = 4, 8, 32
DKV = NH * DH
E_ALL = D + 2 * DKV
ND = D // P
NS = S // P
NG = NQ * NH // 4
HX = 8
NHC = S // HX
LN_EPS = 1e-5
TOE_PARTS = 2 * NG
TOE_DONE = 2 * 16 * TOE_PARTS

XN_S = 16.0
W_S = 256.0
QK_S = 16.0
T_S = 256.0
U_S = 16.0


def wait(eng, sem, value):
    if not (isinstance(value, int) and value <= 0):
        eng.wait_ge(sem, value)


def wait_on_cell(nc, cell, eng, sem, value):
    wait(eng, sem, value)
    nc.vector.memset(cell, 0.0)


def loop_first_last(eng, n, first, body):
    for i in range(first):
        body(i, i > 0, True)
    if n - 1 > first:
        with eng.Fori(first, n - 1) as i:
            body(i, True, True)
    body(n - 1, True, False)


class Count:

    def __init__(self, base=0, start=0):
        self.base, self.start, self.n = base, start, 0

    def next(self):
        v = self.base + self.n
        self.n += 1
        return v

    def now(self):
        return self.base + self.n


PROJ = ["k0", "k1", "q0", "q1", "q2", "q3", "q4", "q5", "q6", "q7", "v0", "v1"]


def side_jobs(stage):
    max_jobs = [("max", n // 4, n % 4) for n in range(8 * NS)]
    mem_jobs = {qq: [("mem", qq, st) for st in range(NS)] for qq in range(3)}
    mixed = lambda a, b: [job for pair in zip(a, b) for job in pair]
    return {"q4": mixed(mem_jobs[0], max_jobs[0:4]), "q5": mixed(mem_jobs[1], max_jobs[4:8]), "q6": max_jobs[8:16],
            "q7": mixed(mem_jobs[2], max_jobs[16:20]), "v0": max_jobs[20:22] + [("rows", 0)] + max_jobs[22:27],
            "v1": max_jobs[27:32]}.get(stage, [])


def fill_plan(has_next):
    n, at = 0, {}
    for stage in PROJ:
        for job in side_jobs(stage):
            n += 1
            if job[0] == "mem":
                at[f"am{job[1]}"] = n
            elif job[0] == "rows":
                at["rows", 0] = n
    for g in range(NG):
        for t in range(NS):
            if t == 1 and g + 1 < NG:
                n += 1
                at["rows", g + 1] = n
            n += 4 * (g + 2 < NG)
            n += g == NG - 1
            at["am3"] = n
            if has_next and (g, t) in XT_AT:
                n += 1
                at["xt"] = n
            n += (t == 0 and g > 0) + 2 * (t == 3 and g > 0)
            at["out", g - 1] = n
    at["all"] = at["out", NG - 1] = n + 3
    return at


XT_AT = {(5, 3): 0, (6, 0): 1, (6, 1): 2, (6, 2): 3, (6, 3): 4, (7, 0): 5, (7, 1): 6, (7, 2): 7}


def attention_phase(nc, x, Wq, Wk, Wv, memory, memory_norm, memory_weight, ident_in, k_pad, toeplitz, toe_done, x1, nb):
    with ExitStack() as ctx:
        def sb(name, shape, dt=F32):
            return ctx.enter_context(nc.sbuf_tensor(name, shape, dt))

        def sem(name):
            return ctx.enter_context(nc.semaphore(name))

        ident = sb("a_ident", [P, P])
        w_hi = sb("a_w_hi", [P, ND, E_ALL], F16)
        w_lo = sb("a_w_lo", [P, ND, E_ALL], F16)
        xin = sb("a_xin", [P, NS, D])
        xres = sb("a_xres", [P, NS, D])
        xT_hi = sb("a_xT_hi", [P, ND, S], F16)
        xT_lo = sb("a_xT_lo", [P, ND, S], F16)
        qk_hi = sb("a_qk_hi", [P, 4, S], F16)
        qk_lo = sb("a_qk_lo", [P, 4, S], F16)
        qs = sb("a_qs", [P, NQ * NH, S], F16)
        ks = sb("a_ks", [P, NH, S], F16)
        v = sb("a_v", [P, NS, DKV])
        probs = sb("a_probs", [P, 2, 4, S])
        base = sb("a_base", [P, 2, 4, S])
        sumT = sb("a_sumT", [P, S])
        oT = sb("a_oT", [P, S])
        rsum = sb("a_rsum", [P, 2, 4 * NS])
        mixed = sb("a_mixed", [P, S])
        sq = sb("a_sq", [P, 4, S])
        eq = sb("a_eq", [P, 2, S])
        rq = sb("a_rq", [P, 2, S])
        mem = sb("a_mem", [P, 2, DKV + 1])
        ones = sb("a_ones", [P, DH])
        maxima = sb("a_max", [P, 2, 4, NS])
        mrow = sb("a_mrow", [16, 2, P], F16)
        stats = sb("a_stats", [P, NS, 2, 6])
        mv = sb("a_mv", [P, NS, 2])
        veps = sb("a_veps", [P, NS])
        rstd = sb("a_rstd", [P, NS])
        cell = sb("a_cell", [P, 1])
        mhalf = sb("a_mhalf", [P, NS])
        mixw = sb("a_mixw", [P, 8])
        den = sb("a_den", [P, 2, 2])

        psum = [ctx.enter_context(nc.psum_tensor(f"a_ps{i}", [P, 512], F32)) for i in range(4)]
        misc, ps_av = psum[0:3], psum[3]
        score = [ctx.enter_context(nc.psum_tensor(f"a_score{i}", [P, 2, S], F32)) for i in range(2)]

        const_in = sem("a_const_in")
        w_in = [sem(f"a_w_in{i}") for i in range(4)]
        w_done = sem("a_w_done")
        xin_in = sem("a_xin_in")
        xres_in = sem("a_xres_in")
        x1_out = sem("a_x1_out")
        ready = sem("a_ready")
        filled = sem("a_filled")
        freed = sem("a_freed")
        pr_filled = sem("a_pr_filled")
        pr_freed = sem("a_pr_freed")
        hi_done = sem("a_hi_done")
        eq_done = sem("a_eq_done")
        sq_done = sem("a_sq_done")
        stacked = [sem(f"a_stacked{i}") for i in range(2)]
        ms_in = [sem(f"a_ms_in{i}") for i in range(2)]
        s2_filled = sem("a_s2_filled")
        exp_done = sem("a_exp_done")
        av_tick = sem("a_av_tick")
        added = sem("a_added")
        oT_done = sem("a_oT_done")
        x1_done = sem("a_x1_done")
        stats_done = sem("a_stats_done")
        rstd_done = sem("a_rstd_done")
        norm_done = sem("a_norm_done")
        mix_step = sem("a_mix_step")
        mix_exp = sem("a_mix_exp")
        w_filled = sem("a_w_filled")
        w_hi_done = sem("a_w_hi_done")
        elu_step = sem("a_elu_step")
        bn_step = sem("a_bn_step")
        aggr_step = sem("a_aggr_step")
        mem_step = sem("a_mem_step")
        quot_step = sem("a_quot_step")

        AT = fill_plan(True)
        FILLS = -(-AT["all"] // 3) * 3
        SKIP = FILLS - AT["all"]
        TAIL = 2 + SKIP
        HIS = 2 + 8 + 8
        N_W = E_ALL // P

        block = ctx.enter_context(nc.Block())

        def block_of(g, t):
            return base[:, g % 2, :, :] if t == 0 else probs[:, (3 * g + t - 1) % 2, :, :]

        def w_rows(n):
            if n < ND:
                return Wq[n * P:(n + 1) * P, :]
            if n < ND + 2:
                return Wk[(n - ND) * P:(n - ND + 1) * P, :]
            return Wv[(n - ND - 2) * P:(n - ND - 1) * P, :]

        def stack_count(b, n):
            return 16 * 12 * (b * [3, 2][n % 2] + n // 2 + 1)

        @block.sync
        def _(sp):
            sp.dma_start(ident[:, :], ident_in).then_inc(const_in, 16)
            sp.dma_start(mixw[:, 0:1], memory_weight.rearrange("(a n) -> a n", a=1).to_broadcast([P, 1])).then_inc(const_in, 16)
            for c in range(2):
                sp.dma_start(mem[:, c, 0:DKV], memory[c * P:(c + 1) * P, :]).then_inc(const_in, 16)
                sp.dma_start(mem[:, c, DKV:DKV + 1], memory_norm[c * P:(c + 1) * P, :]).then_inc(const_in, 16)
            sp.dma_start(xin[:, :, :], x[0].rearrange("(t p) d -> p t d", p=P)).then_inc(xin_in, 16)
            for n in range(N_W):
                wait(sp, w_done, 2 * (n - 3))
                sp.dma_start(xres[:, n % 4, :], w_rows(n)).then_inc(w_in[n % 4], 16)
            sp.wait_ge(w_done, 2 * N_W)

            def batch(b, has_prev, has_next):
                if has_next:
                    sp.wait_ge(filled, b * FILLS + ND - (FILLS - AT["xt"]) if has_prev else ND)
                    sp.dma_start(xin[:, :, :], x[b + 1].rearrange("(t p) d -> p t d", p=P)).then_inc(xin_in, 16)
                if has_prev:
                    store(b - 1, b * NG)
                for n in range(5):
                    if n == 1:
                        if has_prev:
                            sp.wait_ge(x1_out, 16 * b)
                        sp.dma_start(xres[:, :, :], x[b].rearrange("(t p) d -> p t d", p=P)).then_inc(xres_in, 16)
                    sp.wait_ge(pr_freed, b * 12 + 2 * n + 2)
                    for j in range(4):
                        rows, slots = slice(DH * j, DH * j + DH), slice(2 * (n % 2), 2 * (n % 2) + 2)
                        hi, lo = qk_hi[rows, slots, :], qk_lo[rows, slots, :]
                        if n == 0:
                            dst, mid, last = ks[:, j:j + 5:4, :], hi, lo
                        else:
                            dst, mid, last = qs[:, 8 * (n - 1) + j:8 * (n - 1) + j + 5:4, :], lo, hi
                        for at, half in ((0, hi), (DH, mid), (2 * DH, last)):
                            sp.dma_start(dst[at:at + DH], half).then_inc(stacked[n % 2], 16)
                for g in range(NG):
                    sp.wait_ge(freed, b * FILLS + ND + fill_plan(has_next)["rows", g])
                    sp.dma_start(qs[3 * DH:3 * DH + 1, 4 * g:4 * g + 4, :], mrow[:, g % 2, :]).then_inc(ms_in[g % 2], 16)
                    if not (has_prev and has_next):
                        copy_toeplitz(sp, k_pad, toeplitz, toe_done, g + (NG if has_prev else 0))

            def store(b, mixes):
                sp.wait_ge(x1_done, mixes)
                sp.dma_start(x1[b].rearrange("(t p) d -> p t d", p=P), xres[:, :, :]).then_inc(x1_out, 16)

            loop_first_last(sp, nb, 1, batch)
            store(nb - 1, nb * NG)
            sp.wait_ge(x1_out, 16 * nb)

        @block.gpsimd
        def _(pool):
            nc.gpsimd.memset(ones[:, :], 1.0).then_inc(ready, 1)
            nc.gpsimd.memset(mhalf[:, :], -0.5).then_inc(ready, 1)
            pool.wait_ge(ready, 2)
            nc.gpsimd.memset(ks[3 * DH:3 * DH + 1, :, :], QK_S * QK_S).then_inc(ready, 1)
            pool.wait_ge(ready, 3)

            def norm_scale(n):
                pool.wait_ge(stats_done, n + 1)
                nc.gpsimd.tensor_tensor(rstd[:, :], veps[:, :], mhalf[:, :], ALU.pow).then_inc(rstd_done, 1)

            norm_scale(0)

            def add_mixed(g, banks):
                pool.wait_ge(freed, banks)
                part = xres[:, :, g * P:(g + 1) * P]
                nc.gpsimd.tensor_tensor(part, part, mixed[:, :].rearrange("p (s e) -> p s e", s=NS), ALU.add).then_inc(x1_done, 1)

            def batch(b, has_prev, has_next):
                at = fill_plan(has_next)
                if has_prev:
                    add_mixed(NG - 1, b * FILLS + ND)
                for t in range(8):
                    n = b * 8 + t
                    pool.wait_ge(elu_step, n + 1)
                    if t >= 4:
                        pool.wait_ge(filled, b * FILLS + ND + AT[f"am{t // 2 - 2}"])
                    elif has_prev:
                        pool.wait_ge(filled, b * FILLS + ND - (FILLS - AT[f"am{t // 2 + 2}"]))
                    nc.gpsimd.tensor_tensor(sq[:, t % 4, :], eq[:, t % 2, :], rq[:, t % 2, :], ALU.add).then_inc(sq_done, 1)
                for g in range(NG):
                    if g > 1:
                        add_mixed(g - 2, b * FILLS + ND + at["out", g - 2])
                    for t in (1, 2):
                        for pair in range(2):
                            n = 4 * g + 2 * t - 2 + pair
                            pool.wait_ge(exp_done, b * 64 + 2 * (4 * g + t) + pair + 1)
                            if t == 1:
                                pool.wait_ge(av_tick, b * 32 + 4 * g + 1)
                            else:
                                pool.wait_ge(added, b * 32 + n - 1)
                            heads = slice(2 * pair, 2 * pair + 2)
                            nc.gpsimd.tensor_tensor(base[:, g % 2, heads, :], base[:, g % 2, heads, :], block_of(g, t)[:, heads, :],
                                                    ALU.add).then_inc(added, 1)
                    if g == 3 and has_next:
                        norm_scale(b + 1)
                add_mixed(NG - 2, b * FILLS + ND + at["out", NG - 2])
                if not has_next:
                    add_mixed(NG - 1, b * FILLS + ND + at["out", NG - 1])

            loop_first_last(pool, nb, 1, batch)

        @block.tensor
        def _(pe):
            pe.wait_ge(const_in, 16 * 6)
            pe.wait_ge(ready, 3)
            for n in range(N_W):
                pe.wait_ge(w_in[n % 4], 16 * (n // 4 + 1))
                for c in range(2):
                    wait(pe, w_done, 2 * n + c - 1)
                    for k in range(4):
                        m = nc.tensor.transpose(misc[c][:, k * P:(k + 1) * P], xres[:, n % 4, (4 * c + k) * P:(4 * c + k + 1) * P], ident[:, :])
                    m.then_inc(w_filled, 1)
            pe.wait_ge(w_done, 2 * N_W)

            def fill(f):
                n = f.next()
                wait(pe, freed, n - 2)
                return misc[(f.start + f.n - 1) % 3]

            def xn_transposes(f, kk):
                bank = fill(f)
                for st in range(NS):
                    m = nc.tensor.transpose(bank[:, st * P:(st + 1) * P], xin[:, st, kk * P:(kk + 1) * P], ident[:, :])
                m.then_inc(filled, 1)

            def three(out, lhs_hi, lhs_lo, rhs_hi, rhs_lo, first, last):
                nc.tensor.matmul(out, lhs_hi, rhs_hi, start=first, stop=False)
                nc.tensor.matmul(out, lhs_hi, rhs_lo, start=False, stop=False)
                return nc.tensor.matmul(out, lhs_lo, rhs_hi, start=False, stop=last)

            f0 = Count(0)
            pe.wait_ge(norm_done, NS)
            for kk in range(ND):
                xn_transposes(f0, kk)

            def batch(b, has_prev, has_next):
                f = Count(b * FILLS + ND, ND)
                scored = {}
                pe.wait_ge(hi_done, (b + 1) * 8 + b * 10)
                pe.wait_ge(freed, b * FILLS + ND - TAIL if has_prev else ND)

                def score_max(g, chunk, c):
                    if chunk == 0 and c == 0:
                        if g == 0:
                            pe.wait_ge(stacked[0], stack_count(b, 0))
                        n = g // 2 + 1
                        pe.wait_ge(stacked[n % 2], stack_count(b, n))
                    bank = fill(f)
                    nc.tensor.matmul(bank[:, :], qs[0:3 * DH, 4 * g + chunk, c * P:(c + 1) * P], ks[0:3 * DH, (g % 2) * 4 + chunk, :],
                                     start=True, stop=True).then_inc(filled, 1)
                    scored[g] = f.n

                def mem_products(qq, st):
                    if st == 0:
                        pe.wait_ge(sq_done, b * 8 + 2 * qq + 2)
                    bank = fill(f)
                    for c in range(2):
                        m = nc.tensor.matmul(bank[:, 0:DKV + 1], sq[:, (2 * qq + c) % 4, st * P:(st + 1) * P], mem[:, c, :],
                                             start=(c == 0), stop=(c == 1))
                    m.then_inc(filled, 1)

                def max_rows(g):
                    pe.wait_ge(freed, f.base + scored[g])
                    bank = fill(f)
                    nc.tensor.matmul(bank[0:16, 0:P], maxima[:, g % 2, :, :].rearrange("p j s -> p (j s)"), ident[:, :],
                                     start=True, stop=True).then_inc(filled, 1)

                def out_transposes(n, copied, f, step=1):
                    pe.wait_ge(freed, copied)
                    bank = fill(f)
                    for st in range(NS):
                        m = nc.tensor.matmul(bank[:, 4 * st:4 * st + 4], sumT[:, st * P:(st + 1) * P], ident[:, 0:P:DH], start=True, stop=True)
                    m.then_inc(filled, 1)
                    pe.wait_ge(oT_done, n + 1)
                    bank = fill(f)
                    for st in range(NS):
                        m = nc.tensor.transpose(bank[:, st * P:(st + 1) * P], oT[:, st * P:(st + 1) * P], ident[:, :])
                    m.then_inc(filled, step)

                tile = Count(b * 12)

                def proj_bank():
                    wait(pe, pr_freed, tile.next() - 1)
                    return score[(tile.n - 1) % 2][:, 0, :]

                def side(job):
                    if job[0] == "max":
                        score_max(job[1] // 4, job[1] % 4, job[2])
                    elif job[0] == "mem":
                        mem_products(job[1], job[2])
                    else:
                        max_rows(0)

                for stage in PROJ:
                    i = int(stage[1])
                    jobs = side_jobs(stage)
                    bank = proj_bank()
                    for n in range(2 * ND):
                        if n % 2 == 0 and n // 2 < len(jobs):
                            side(jobs[n // 2])
                        if stage[0] == "v":
                            s, kk = n // ND, n % ND
                            rows = slice((2 * i + s) * P, (2 * i + s + 1) * P)
                            m = three(bank[:, s * DKV:(s + 1) * DKV], xT_hi[:, kk, rows], xT_lo[:, kk, rows],
                                      w_hi[:, kk, D + DKV:E_ALL], w_lo[:, kk, D + DKV:E_ALL], kk == 0, kk == ND - 1)
                        elif n % 2 == 0:
                            e0 = (D if stage[0] == "k" else 0) + i * P
                            kk = n // 2
                            m = three(bank, w_hi[:, kk, e0:e0 + P], w_lo[:, kk, e0:e0 + P], xT_hi[:, kk, :], xT_lo[:, kk, :],
                                      kk == 0, kk == ND - 1)
                    m.then_inc(pr_filled, 1)
                    if stage == "k0" and has_prev:
                        out_transposes(b * NG - 1, b * FILLS + ND - TAIL, Count(b * FILLS + ND - TAIL, ND - TAIL), 1 + SKIP)

                def scores(g, t, pair):
                    n = b * 64 + (g * 4 + t) * 2 + pair
                    wait(pe, exp_done, n - 1)
                    if (g, t, pair) == (0, 0, 0):
                        pe.wait_ge(pr_freed, (b + 1) * 12)
                    if t == 0 and pair == 0:
                        pe.wait_ge(ms_in[g % 2], 16 * (b * 4 + g // 2 + 1))
                    for i in range(2):
                        j = 2 * pair + i
                        m = nc.tensor.matmul(score[pair][:, i, :], ks[0:3 * DH + 1, (g % 2) * 4 + j, t * P:(t + 1) * P],
                                             qs[0:3 * DH + 1, 4 * g + j, :], start=True, stop=True)
                    m.then_inc(s2_filled, 1)

                def weighted(g, t):
                    pe.wait_ge(exp_done, b * 64 + 2 * (g * 4 + t) + 2)
                    if t == 0:
                        wait(pe, oT_done, b * NG + g)
                    for j in range(4):
                        rows = slice(DH * j, DH * j + DH)
                        head = (g % 2) * 4 + j
                        m = nc.tensor.matmul(ps_av[rows, :], v[:, t, head * DH:(head + 1) * DH], block_of(g, t)[:, j, :],
                                             start=(t == 0), stop=(t == NS - 1))
                    m.then_inc(av_tick, 1)

                def summed(g):
                    bank = fill(f)
                    for src, first in ((block_of(g, 3), True), (base[:, g % 2, :, :], False)):
                        if not first:
                            pe.wait_ge(added, b * 32 + 4 * g + 4)
                        for j in range(4):
                            m = nc.tensor.matmul(bank[DH * j:DH * j + DH, :], ones[:, :], src[:, j, :], start=first, stop=not first)
                    m.then_inc(filled, 1)

                for g in range(NG):
                    for t in range(NS):
                        more = g + 2 < NG
                        last = (g, t - 1) if t else (g - 1, 3)
                        if t == 1 and g + 1 < NG:
                            max_rows(g + 1)
                        if more:
                            score_max(g + 2, t, 0)
                        scores(g, t, 0)
                        if last[0] >= 0:
                            weighted(*last)
                        if more:
                            score_max(g + 2, t, 1)
                        scores(g, t, 1)
                        if g == NG - 1:
                            mem_products(3, t)
                        if more:
                            score_max(g + 2, t, 2)
                        if more:
                            score_max(g + 2, t, 3)
                        if has_next and (g, t) in XT_AT:
                            kk = XT_AT[g, t]
                            if kk == 0:
                                pe.wait_ge(norm_done, (b + 2) * NS)
                            xn_transposes(f, kk)
                        if t == 0 and g > 0:
                            summed(g - 1)
                            copied = f.now()
                        if t == 3 and g > 0:
                            out_transposes(b * NG + g - 1, copied, f)
                weighted(NG - 1, 3)
                summed(NG - 1)
                if not has_next:
                    out_transposes(b * NG + NG - 1, f.now(), f)

            loop_first_last(pe, nb, 1, batch)

        @block.scalar
        def _(act):
            act.wait_ge(const_in, 16 * 6)
            nc.scalar.activation(mixw[:, 1:2], mixw[:, 0:1], ACT.Exp, scale=-1.0).then_inc(mix_exp, 1)
            for n in range(2 * N_W):
                act.wait_ge(w_filled, n + 1)
                dst = w_hi[:, 4 * (n % 2):4 * (n % 2) + 4, (n // 2) * P:(n // 2 + 1) * P]
                nc.scalar.activation(dst, misc[n % 2][:, :].rearrange("p (k e) -> p k e", k=4), ACT.Copy, scale=W_S).then_inc(w_hi_done, 1)

            def xn_hi(n_fill, slot, kk):
                act.wait_ge(filled, n_fill + 1)
                nc.scalar.activation(xT_hi[:, kk, :], misc[slot][:, :], ACT.Copy, scale=XN_S).then_inc(hi_done, 1)

            for kk in range(ND):
                xn_hi(kk, kk % 3, kk)

            def batch(b, has_prev, has_next):
                f = Count(b * FILLS + ND, ND)
                for stage in PROJ:
                    f.n += len(side_jobs(stage))
                    if stage[0] in "kq":
                        tile = int(stage[1]) + (2 if stage[0] == "q" else 0)
                        bank = score[tile % 2][:, 0, :]
                        act.wait_ge(pr_filled, b * 12 + tile + 1)
                        if tile >= 4:
                            act.wait_ge(stacked[tile // 2 % 2], stack_count(b, tile // 2 - 2))
                        elif has_prev:
                            act.wait_ge(stacked[tile // 2], 16 * 12 * b * [3, 2][tile // 2])
                        nc.scalar.activation(qk_hi[:, tile % 4, :], bank, ACT.Copy, scale=QK_S / (XN_S * W_S)).then_inc(hi_done, 1)
                        if stage[0] == "q":
                            t = tile - 2
                            wait(act, sq_done, b * 8 + t - 1)
                            nc.scalar.activation(eq[:, t % 2, :], bank, ACT.Exp, scale=1.0 / (XN_S * W_S))
                            nc.scalar.activation(rq[:, t % 2, :], bank, ACT.Relu, scale=1.0 / (XN_S * W_S)).then_inc(eq_done, 1)
                def copy_weighted(g):
                    act.wait_ge(av_tick, b * 32 + 4 * g + 4)
                    if g > 0:
                        act.wait_ge(filled, out_end)
                    elif has_prev:
                        act.wait_ge(filled, b * FILLS + ND)
                    nc.scalar.activation(oT[:, :], ps_av[:, :], ACT.Copy).then_inc(oT_done, 1)

                for g in range(NG):
                    for t in range(NS):
                        back = 3 * g + t - 3
                        if t > 0 and (back >= 0 or has_prev):
                            if back % 3 == 2:
                                act.wait_ge(filled, sum_end if g > 0 else b * FILLS + ND - TAIL)
                            else:
                                act.wait_ge(av_tick, b * 32 + 4 * (back // 3) + back % 3 + 2)
                                act.wait_ge(added, b * 32 + 4 * (back // 3) + 2 * (back % 3) + 2)
                        for pair in range(2):
                            act.wait_ge(s2_filled, b * 64 + 2 * (4 * g + t) + pair + 1)
                            nc.scalar.activation(block_of(g, t)[:, 2 * pair:2 * pair + 2, :], score[pair][:, :, :], ACT.Exp,
                                                 scale=DH ** -0.5 / (QK_S * QK_S)).then_inc(exp_done, 1)
                        if t == 1 and g + 1 < NG:
                            f.n += 1
                        if g + 2 < NG:
                            f.n += 4
                        if g == NG - 1:
                            f.n += 1
                        if t == 0 and g > 0:
                            copy_weighted(g - 1)
                        if has_next and (g, t) in XT_AT:
                            n = f.next()
                            xn_hi(n, (ND + f.n - 1) % 3, XT_AT[g, t])
                        if t == 0 and g > 0:
                            f.n += 1
                            sum_end = f.now()
                        if t == 3 and g > 0:
                            f.n += 2
                            out_end = f.now()
                copy_weighted(NG - 1)

            loop_first_last(act, nb, 1, batch)

        @block.vector
        def _(dve):
            dve.wait_ge(mix_exp, 1)
            nc.vector.tensor_scalar(mixw[:, 2:3], mixw[:, 1:2], 1.0, None, ALU.add).then_inc(mix_step, 1)
            dve.wait_ge(mix_step, 1)
            nc.vector.reciprocal(mixw[:, 3:4], mixw[:, 2:3]).then_inc(mix_step, 1)
            dve.wait_ge(mix_step, 2)
            nc.vector.tensor_scalar(mixw[:, 4:5], mixw[:, 3:4], -1.0, 1.0, ALU.mult, ALU.add).then_inc(mix_step, 1)
            dve.wait_ge(mix_step, 3)
            for n in range(2 * N_W):
                dve.wait_ge(w_hi_done, n + 1)
                rows = (slice(None), slice(4 * (n % 2), 4 * (n % 2) + 4), slice((n // 2) * P, (n // 2 + 1) * P))
                nc.vector.scalar_tensor_tensor(out=w_lo[rows], in0=misc[n % 2][:, :].rearrange("p (k e) -> p k e", k=4), scalar=W_S,
                                               in1=w_hi[rows], op0=ALU.mult, op1=ALU.subtract).then_inc(w_done, 1)

            def bn(n, st):
                if st == 0:
                    dve.wait_ge(xin_in, 16 * (n + 1))
                for h in range(2):
                    nc.vector.bn_stats(out=stats[:, st, h, :], in_=xin[:, st, h * 512:(h + 1) * 512]).then_inc(bn_step, 1)
                wait_on_cell(nc, cell[:, :], dve, bn_step, n * 2 * NS + 2 * st + 2)
                nc.vector.bn_aggr(out=mv[:, st, :], in_=stats[:, st, :, :]).then_inc(aggr_step, 1)
                if st == NS - 1:
                    dve.wait_ge(aggr_step, n * NS + NS)
                    nc.vector.tensor_scalar(veps[:, :], mv[:, :, 1], LN_EPS, None, ALU.add).then_inc(stats_done, 1)

            def normalise(n, st):
                dve.wait_ge(rstd_done, n + 1)
                nc.vector.tensor_scalar(xin[:, st, :], xin[:, st, :], mv[:, st, 0:1], rstd[:, st:st + 1], ALU.subtract, ALU.mult).then_inc(norm_done, 1)

            def xn_lo(n_fill, n_hi, slot, kk):
                dve.wait_ge(hi_done, n_hi + 1)
                nc.vector.scalar_tensor_tensor(out=xT_lo[:, kk, :], in0=misc[slot][:, :], scalar=XN_S, in1=xT_hi[:, kk, :],
                                               op0=ALU.mult, op1=ALU.subtract).then_inc(freed, 1)

            for st in range(NS):
                bn(0, st)
            for st in range(NS):
                normalise(0, st)
            for kk in range(ND):
                xn_lo(kk, kk, kk % 3, kk)

            def batch(b, has_prev, has_next):
                f = Count(b * FILLS + ND, ND)
                his = Count(b * HIS + ND)

                def bank_ready(f=f):
                    n = f.next()
                    dve.wait_ge(filled, n + 1)
                    return misc[(f.start + f.n - 1) % 3]

                def maximum_of(g, chunk, c):
                    bank = bank_ready()
                    nc.vector.reduce_max(maxima[:, g % 2, chunk, c:c + 1], bank[:, :], AX_X).then_inc(freed, 1)

                def mem_mix(qq, st):
                    bank = bank_ready()
                    k = Count(b * 32 + (qq * 4 + st) * 2)
                    nc.vector.reciprocal(den[:, st % 2, 0:1], bank[:, DKV:DKV + 1]).then_inc(mem_step, 1)
                    dve.wait_ge(mem_step, k.next() + 1)
                    nc.vector.tensor_scalar(den[:, st % 2, 1:2], den[:, st % 2, 0:1], mixw[:, 3:4], None, ALU.mult).then_inc(mem_step, 1)
                    dve.wait_ge(mem_step, k.next() + 1)
                    part = xres[:, st, qq * DKV:(qq + 1) * DKV]
                    nc.vector.scalar_tensor_tensor(out=part, in0=bank[:, 0:DKV], scalar=den[:, st % 2, 1:2], in1=part,
                                                   op0=ALU.mult, op1=ALU.add).then_inc(freed, 1)

                def rows_out(g):
                    bank = bank_ready()
                    if g >= 2:
                        dve.wait_ge(ms_in[g % 2], 16 * (b * 4 + g // 2))
                    elif has_prev:
                        dve.wait_ge(ms_in[g % 2], 16 * (b * 4))
                    nc.vector.tensor_scalar(mrow[:, g % 2, :], bank[0:16, 0:P], -1.0 / (QK_S * QK_S), None, ALU.mult).then_inc(freed, 1)

                def attn_mix(g, n, f, step=1):
                    bank = bank_ready(f)
                    nc.vector.reciprocal(rsum[:, 0, :], bank[:, 0:4 * NS]).then_inc(freed, 1)
                    dve.wait_ge(freed, f.now())
                    nc.vector.tensor_scalar(rsum[:, 1, :], rsum[:, 0, :], mixw[:, 4:5], None, ALU.mult).then_inc(quot_step, 1)
                    dve.wait_ge(quot_step, n + 1)
                    bank = bank_ready(f)
                    wait(dve, x1_done, n)
                    nc.vector.tensor_tensor(mixed[:, :].rearrange("p (h d) -> p h d", d=DH), bank[:, :].rearrange("p (h d) -> p h d", d=DH),
                                            rsum[:, 1, :].unsqueeze(2).to_broadcast([P, 4 * NS, DH]), ALU.mult).then_inc(freed, step)

                def copy_sums():
                    bank = bank_ready()
                    nc.vector.tensor_copy(sumT[:, :], bank[:, :]).then_inc(freed, 1)

                for stage in PROJ:
                    i = int(stage[1])
                    for job in side_jobs(stage):
                        if job[0] == "max":
                            maximum_of(job[1] // 4, job[1] % 4, job[2])
                        elif job[0] == "mem":
                            if job == ("mem", 0, 0):
                                dve.wait_ge(xres_in, 16 * (b + 1))
                            mem_mix(job[1], job[2])
                        else:
                            rows_out(0)
                    if stage[0] in "kq":
                        tile = i + (2 if stage[0] == "q" else 0)
                        bank = score[tile % 2][:, 0, :]
                        dve.wait_ge(hi_done, his.next() + 1)
                        if stage[0] == "q":
                            dve.wait_ge(eq_done, b * 8 + tile - 1)
                        nc.vector.scalar_tensor_tensor(out=qk_lo[:, tile % 4, :], in0=bank, scalar=QK_S / (XN_S * W_S),
                                                       in1=qk_hi[:, tile % 4, :], op0=ALU.mult, op1=ALU.subtract).then_inc(pr_freed, 1)
                        if stage[0] == "q":
                            e = eq[:, tile % 2, :]
                            nc.vector.tensor_scalar(e, e, 1.0, 0.0, ALU.subtract, ALU.min).then_inc(elu_step, 1)
                    else:
                        dve.wait_ge(pr_filled, b * 12 + 10 + i + 1)
                        nc.vector.tensor_scalar(v[:, 2 * i:2 * i + 2, :], score[i][:, 0, :].rearrange("p (s e) -> p s e", s=2),
                                                1.0 / (XN_S * W_S), None, ALU.mult).then_inc(pr_freed, 1)
                    if stage == "k0" and has_prev:
                        attn_mix(NG - 1, b * NG - 1, Count(b * FILLS + ND - TAIL, ND - TAIL), 1 + SKIP)

                for g in range(NG):
                    for t in range(NS):
                        if t == 1 and g + 1 < NG:
                            rows_out(g + 1)
                        if g + 2 < NG:
                            for c in range(4):
                                maximum_of(g + 2, t, c)
                        if g == NG - 1:
                            mem_mix(3, t)
                        if has_next and g == 3:
                            bn(b + 1, t)
                        if has_next and g == 4:
                            normalise(b + 1, t)
                        if has_next and (g, t) in XT_AT:
                            n = f.next()
                            xn_lo(n, his.next(), (ND + f.n - 1) % 3, XT_AT[g, t])
                        if t == 0 and g > 0:
                            copy_sums()
                        if t == 3 and g > 0:
                            attn_mix(g - 1, b * NG + g - 1, f)
                copy_sums()
                if not has_next:
                    attn_mix(NG - 1, (b + 1) * NG - 1, f)

            loop_first_last(dve, nb, 1, batch)


def filter_phase(nc, k, k_pad):
    with (
        nc.sbuf_tensor("f_k", [NHC, P + D], F32) as kf,
        nc.sbuf_tensor("f_hi", [NHC, P + D], F16) as k_hi,
        nc.sbuf_tensor("f_lo", [NHC, P + D], F16) as k_lo,
        nc.semaphore("f_zero") as zeroed,
        nc.semaphore("f_in") as k_in,
        nc.semaphore("f_split") as split,
        nc.semaphore("f_out") as k_out,
        nc.Block() as block,
    ):
        @block.vector
        def _(dve):
            nc.vector.memset(kf[:, 0:P], 0.0).then_inc(zeroed, 1)
            dve.wait_ge(zeroed, 1)
            dve.wait_ge(k_in, 16)
            nc.vector.tensor_scalar(k_hi[:, :], kf[:, :], T_S, None, ALU.mult).then_inc(split, 1)
            dve.wait_ge(split, 1)
            nc.vector.scalar_tensor_tensor(out=k_lo[:, :], in0=kf[:, :], scalar=T_S, in1=k_hi[:, :],
                                           op0=ALU.mult, op1=ALU.subtract).then_inc(split, 1)

        @block.sync
        def _(sp):
            sp.dma_start(kf[:, P:P + D], k).then_inc(k_in, 16)
            sp.wait_ge(split, 2)
            sp.dma_start(k_pad[0], k_hi[:, :]).then_inc(k_out, 16)
            sp.dma_start(k_pad[1], k_lo[:, :]).then_inc(k_out, 16)
            sp.wait_ge(k_out, 32)


def copy_toeplitz(sp, k_pad, toeplitz, toe_done, part):
    h0 = part * NHC // TOE_PARTS
    for half in range(2):
        rows = k_pad[half, h0, P:]
        shifted = bass.AP(rows.tensor, rows.offset, [[P + D, NHC // TOE_PARTS], [-1, P], [1, D]])
        sp.dma_start(toeplitz[h0:h0 + NHC // TOE_PARTS, :, half, :], shifted).then_inc(toe_done, 16)


def conv_phase(nc, x1, ctx_in, toeplitz, toe_done, skip, ident_in, x2, absmax, moments, weight, w_rows, w_in, nh):
    NL = D // P
    NP = HX * P
    with ExitStack() as ctx:
        def sb(name, shape, dt=F32):
            return ctx.enter_context(nc.sbuf_tensor(name, shape, dt))

        def sem(name):
            return ctx.enter_context(nc.semaphore(name))

        ident = sb("c_ident", [P, P])
        xh = sb("c_xh", [P, 2, D])
        ch = sb("c_ch", [P, 2, D])
        xres = sb("c_xres", [P, 2, D])
        vh = sb("c_vh", [P, D])
        vT = sb("c_vT", [P, NL, P])
        uT = sb("c_uT", [P, 2, NL, P])
        gT = sb("c_gT", [P, 2, NL, P])
        toe = sb("c_toe", [P, 2, 2, D], F16)
        u = sb("c_u", [P, 3, NP])
        u_hi = sb("c_u_hi", [P, 2, NL, NP], F16)
        u_lo = sb("c_u_lo", [P, 2, NL, NP], F16)
        z = sb("c_z", [P, 2, NP])
        tree = sb("c_tree", [P, 2, NP // 2])
        skp = sb("c_skp", [P, NHC, HX])
        sterm = sb("c_sterm", [P, 2, NL, P])
        st1 = sb("c_st1", [P, NL, P])
        oT = sb("c_oT", [P, 2, NL, P])
        zn = sb("c_zn", [P, D])
        stats = sb("c_stats", [P, 2, 6])
        mv = sb("c_mv", [P, 2])
        rstd = sb("c_rstd", [P, 1])
        stats2 = sb("c_stats2", [P, 2, 6])
        veps = sb("c_veps", [P, 2])
        cell = sb("c_cell", [P, 1])
        mv2 = sb("c_mv2", [P, 2])
        mhalf = sb("c_mhalf", [P, 1])

        bankT = [ctx.enter_context(nc.psum_tensor(f"c_bt{i}", [P, 512], F32)) for i in range(4)]
        y = [ctx.enter_context(nc.psum_tensor(f"c_y{i}", [P, 2, 512], F32)) for i in range(2)]

        const_in = sem("c_const_in")
        ready = sem("c_ready")
        skp_done = sem("c_skp_done")
        x_in = [sem(f"c_x_in{i}") for i in range(2)]
        c_in = [sem(f"c_c_in{i}") for i in range(2)]
        t_in = [sem(f"c_t_in{i}") for i in range(2)]
        x2_out = [sem(f"c_x2_out{i}") for i in range(2)]
        bn_step = sem("c_bn_step")
        veps_done = sem("c_veps_done")
        rstd_done = sem("c_rstd_done")
        rstd2_done = sem("c_rstd2_done")
        vh_done = sem("c_vh_done")
        res_done = sem("c_res_done")
        tr_filled = sem("c_tr_filled")
        tr_read = sem("c_tr_read")
        bk_filled = sem("c_bk_filled")
        bk_read = sem("c_bk_read")
        u_done = sem("c_u_done")
        hi_done = sem("c_hi_done")
        lo_done = sem("c_lo_done")
        y_done = sem("c_y_done")
        z_done = sem("c_z_done")
        tree_step = sem("c_tree_step")
        o_done = sem("c_o_done")
        skip_step = sem("c_skip_step")
        bn2_step = sem("c_bn2_step")
        zn_done = sem("c_zn_done")
        veps2_done = sem("c_veps2_done")

        block = ctx.enter_context(nc.Block())

        rows_x1 = x1.rearrange("b (h i) d -> h b i d", i=HX)
        rows_c = ctx_in.rearrange("b (h i) d -> h b i d", i=HX)

        @block.sync
        def _(sp):
            sp.dma_start(ident[:, :], ident_in).then_inc(const_in, 16)
            sp.dma_start(skp[:, :, :], skip.rearrange("(a h i) -> a h i", a=1, i=HX).to_broadcast([P, NHC, HX])).then_inc(const_in, 16)

            def load_filter(h, q):
                sp.dma_start(toe[:, q, :, :], toeplitz[h]).then_inc(t_in[q], 16)

            def load_rows(h, q):
                sp.dma_start(xh[:, q, :], rows_x1[h]).then_inc(x_in[q], 16)
                sp.dma_start(ch[:, q, :], rows_c[h]).then_inc(c_in[q], 16)

            load_rows(0, 0)
            load_rows(1, 1)
            sp.wait_ge(toe_done, TOE_DONE)
            load_filter(0, 0)
            sp.dma_start(w_rows[:, :, :], weight.rearrange("(t p) d -> p t d", p=P)).then_inc(w_in, 16)

            def channel(h, pair, q, has_prev, has_next, ahead):
                if has_next:
                    if has_prev:
                        sp.wait_ge(y_done, h * NL)
                    load_filter(h + 1, 1 - q)
                if ahead:
                    sp.wait_ge(res_done, h + 1)
                    if not has_prev:
                        sp.wait_ge(tr_filled, 4)
                    load_rows(h + 2, q)
                if has_prev:
                    sp.wait_ge(bk_read, 2 * h)
                    sp.dma_start(x2[h - 1], xres[:, 1 - q, :]).then_inc(x2_out[1 - q], 16)

            channel_loop(sp, nh, channel)
            sp.wait_ge(bk_read, 2 * nh)
            sp.dma_start(x2[nh - 1], xres[:, (nh - 1) % 2, :]).then_inc(x2_out[(nh - 1) % 2], 16)
            for i in range(2):
                sp.wait_ge(x2_out[i], 16 * (nh // 2))

        @block.gpsimd
        def _(pool):
            nc.gpsimd.memset(mhalf[:, :], -0.5).then_inc(ready, 1)
            pool.wait_ge(const_in, 32)
            nc.gpsimd.tensor_scalar(skp[:, :, :], skp[:, :, :], T_S, None, ALU.mult).then_inc(skp_done, 1)
            pool.wait_ge(ready, 1)
            pool.wait_ge(skp_done, 1)

            def skip_share(h, q):
                pool.wait_ge(tr_read, 4 * (h + 1))
                n = Count(h * 6)
                nc.gpsimd.tensor_tensor(st1[:, :, :], vT[:, :, :], gT[:, q, :, :], ALU.mult).then_inc(skip_step, 1)
                pool.wait_ge(skip_step, n.next() + 1)
                s = st1[:, :, :].rearrange("p c (b i) -> p (c b) i", i=HX)
                w = skp[:, h, :].unsqueeze(1).to_broadcast([P, P, HX])
                nc.gpsimd.tensor_tensor(s, s, w, ALU.mult).then_inc(skip_step, 1)
                for width in (4, 2, 1):
                    pool.wait_ge(skip_step, n.next() + 1)
                    nc.gpsimd.tensor_tensor(s[:, :, 0:width], s[:, :, 0:width], s[:, :, width:2 * width], ALU.add).then_inc(skip_step, 1)
                pool.wait_ge(skip_step, n.next() + 1)
                nc.gpsimd.tensor_tensor(sterm[:, q, :, :].rearrange("p c (b j) -> p (c b) j", j=HX),
                                        uT[:, q, :, :].rearrange("p c (b j) -> p (c b) j", j=HX),
                                        s[:, :, 0:1].to_broadcast([P, P, HX]), ALU.mult).then_inc(skip_step, 1)
                n.next()

            def norm_scale1(h):
                pool.wait_ge(veps_done, h + 1)
                nc.gpsimd.tensor_tensor(rstd[:, :], veps[:, 0:1], mhalf[:, :], ALU.pow).then_inc(rstd_done, 1)

            def norm_scale2(h):
                pool.wait_ge(veps2_done, h + 1)
                nc.gpsimd.tensor_tensor(mv2[:, 1:2], veps[:, 1:2], mhalf[:, :], ALU.pow).then_inc(rstd2_done, 1)

            def sum_block(h, q, a):
                n = Count(h * NL * 3 + a * 3)
                pool.wait_ge(z_done, h * NL + a + 1)
                wait(pool, o_done, h * NL + a - 1)
                zz, tr = z[:, a % 2, :], tree[:, a % 2, :]
                nc.gpsimd.tensor_tensor(tr[:, 0:512], zz[:, 0:512], zz[:, 512:1024], ALU.add).then_inc(tree_step, 1)
                pool.wait_ge(tree_step, n.next() + 1)
                nc.gpsimd.tensor_tensor(tr[:, 0:256], tr[:, 0:256], tr[:, 256:512], ALU.add).then_inc(tree_step, 1)
                pool.wait_ge(tree_step, n.next() + 1)
                nc.gpsimd.tensor_tensor(tr[:, 0:128], tr[:, 0:128], tr[:, 128:256], ALU.add).then_inc(tree_step, 1)
                pool.wait_ge(tree_step, n.next() + 1)
                nc.gpsimd.tensor_tensor(oT[:, q, a, :], tr[:, 0:128], sterm[:, q, a, :], ALU.add).then_inc(o_done, 1)

            norm_scale1(0)
            skip_share(0, 0)

            norm_scale1(1)

            def channel(h, pair, q, has_prev, has_next, ahead):
                for a in range(NL):
                    if a == 2 and has_next:
                        skip_share(h + 1, 1 - q)
                    if a == 3 and has_prev:
                        norm_scale2(h - 1)
                    if a == 4 and ahead:
                        norm_scale1(h + 2)
                    sum_block(h, q, a)

            channel_loop(pool, nh, channel)
            norm_scale2(nh - 1)

        @block.tensor
        def _(pe):
            pe.wait_ge(const_in, 32)

            def forward(h, q):
                pe.wait_ge(vh_done, h + 1)
                for src in range(2):
                    if src:
                        pe.wait_ge(c_in[q], pair_count(h, q))
                    for c in range(2):
                        wait(pe, tr_read, 4 * h + 2 * src + c - 1)
                        for k in range(4):
                            cols = slice((4 * c + k) * P, (4 * c + k + 1) * P)
                            m = nc.tensor.transpose(bankT[c][:, k * P:(k + 1) * P], vh[:, cols] if src == 0 else ch[:, q, cols], ident[:, :])
                        m.then_inc(tr_filled, 1)

            def backward(h, q):
                for c in range(2):
                    pe.wait_ge(o_done, h * NL + 4 * c + 4)
                    wait(pe, bk_read, 2 * h + c - 1)
                    for k in range(4):
                        m = nc.tensor.transpose(bankT[2 + c][:, k * P:(k + 1) * P], oT[:, q, 4 * c + k, :], ident[:, :])
                    m.then_inc(bk_filled, 1)

            def conv(h, q, a):
                wait(pe, z_done, h * NL + a - 1)
                for c in range(a + 1):
                    wt_hi = toe[:, q, 0, (a - c) * P:(a - c + 1) * P]
                    wt_lo = toe[:, q, 1, (a - c) * P:(a - c + 1) * P]
                    if c == a:
                        pe.wait_ge(lo_done, h * NL + a + 1)
                    for wt, src, first, last in ((wt_hi, u_hi, True, False), (wt_hi, u_lo, False, False), (wt_lo, u_hi, False, True)):
                        for n in range(2):
                            m = nc.tensor.matmul(y[a % 2][:, n, :], wt, src[:, q, c, n * 512:(n + 1) * 512],
                                                 start=(first and c == 0), stop=(last and c == a))
                m.then_inc(y_done, 1)

            forward(0, 0)

            def channel(h, pair, q, has_prev, has_next, ahead):
                if has_next:
                    forward(h + 1, 1 - q)
                pe.wait_ge(t_in[q], pair_count(h, q))
                for a in range(NL):
                    if a == 3 and has_prev:
                        backward(h - 1, 1 - q)
                    conv(h, q, a)

            channel_loop(pe, nh, channel)
            backward(nh - 1, (nh - 1) % 2)

        @block.scalar
        def _(act):
            def evacuate(h, q):
                for n in range(4):
                    src, c = n // 2, n % 2
                    act.wait_ge(tr_filled, 4 * h + n + 1)
                    bank, blocks = bankT[c][:, :].rearrange("p (k e) -> p k e", k=4), slice(4 * c, 4 * c + 4)
                    if src == 0:
                        if n == 0:
                            wait(act, u_done, NL * h)
                            wait(act, skip_step, 6 * h)
                        nc.scalar.activation(vT[:, blocks, :], bank, ACT.Copy).then_inc(tr_read, 1)
                    else:
                        if n == 2:
                            wait(act, z_done, NL * (h - 1))
                        nc.scalar.activation(uT[:, q, blocks, :], bank, ACT.Copy, scale=U_S)
                        nc.scalar.activation(gT[:, q, blocks, :], bank, ACT.Copy, scale=1.0 / (T_S * U_S)).then_inc(tr_read, 1)

            def residual(h, q):
                act.wait_ge(x_in[q], pair_count(h, q))
                wait(act, x2_out[q], pair_count(h, q) - 16)
                wait(act, zn_done, h - 1)
                nc.scalar.activation(xres[:, q, :], xh[:, q, :], ACT.Copy).then_inc(res_done, 1)

            def high(h, q, c):
                act.wait_ge(u_done, h * NL + c + 1)
                if c == 0:
                    wait(act, y_done, NL * (h - 1))
                nc.scalar.activation(u_hi[:, q, c, :], u[:, c % 3, :], ACT.Copy).then_inc(hi_done, 1)

            residual(0, 0)
            evacuate(0, 0)
            for c in range(NL):
                high(0, 0, c)

            def channel(h, pair, q, has_prev, has_next, ahead):
                if has_next:
                    evacuate(h + 1, 1 - q)
                    for c in range(NL):
                        high(h + 1, 1 - q, c)
                    residual(h + 1, 1 - q)

            channel_loop(act, nh, channel)

        @block.vector
        def _(dve):
            def normalise(h, q):
                dve.wait_ge(x_in[q], pair_count(h, q))
                for c in range(2):
                    nc.vector.bn_stats(out=stats[:, c, :], in_=xh[:, q, c * 512:(c + 1) * 512]).then_inc(bn_step, 1)
                wait_on_cell(nc, cell[:, :], dve, bn_step, 3 * h + 2)
                nc.vector.bn_aggr(out=mv[:, :], in_=stats[:, :, :]).then_inc(bn_step, 1)
                dve.wait_ge(bn_step, 3 * h + 3)
                nc.vector.tensor_scalar(veps[:, 0:1], mv[:, 1:2], LN_EPS, None, ALU.add).then_inc(veps_done, 1)

            def normalise_end(h, q):
                dve.wait_ge(rstd_done, h + 1)
                wait(dve, tr_filled, 4 * h - 2)
                nc.vector.tensor_scalar(vh[:, :], xh[:, q, :], mv[:, 0:1], rstd[:, :], ALU.subtract, ALU.mult).then_inc(vh_done, 1)

            def product(h, q, c):
                if c == 0:
                    dve.wait_ge(tr_read, 4 * (h + 1))
                wait(dve, lo_done, h * NL + c - 2)
                n = nc.vector.tensor_tensor(u[:, c % 3, :].rearrange("p (i b j) -> p i b j", i=HX, j=HX),
                                            vT[:, c, :].rearrange("p (b i) -> p i b", i=HX).unsqueeze(3).to_broadcast([P, HX, B, HX]),
                                            uT[:, q, c, :].rearrange("p (b j) -> p b j", j=HX).unsqueeze(1).to_broadcast([P, HX, B, HX]),
                                            ALU.mult)
                n.then_inc(u_done, 1)

            def low(h, q, c):
                dve.wait_ge(hi_done, h * NL + c + 1)
                nc.vector.tensor_tensor(u_lo[:, q, c, :], u[:, c % 3, :], u_hi[:, q, c, :], ALU.subtract).then_inc(lo_done, 1)

            def gate(h, q, a):
                dve.wait_ge(y_done, h * NL + a + 1)
                wait(dve, tree_step, 3 * (h * NL + a - 1) - 2)
                nc.vector.tensor_tensor(z[:, a % 2, :].rearrange("p (i b j) -> p i b j", i=HX, j=HX),
                                        y[a % 2][:, :, :].rearrange("p n (i b j) -> p (n i) b j", i=HX // 2, j=HX),
                                        gT[:, q, a, :].rearrange("p (b i) -> p i b", i=HX).unsqueeze(3).to_broadcast([P, HX, B, HX]),
                                        ALU.mult).then_inc(z_done, 1)

            def add_result(h, q):
                dve.wait_ge(res_done, h + 1)
                for c in range(2):
                    dve.wait_ge(bk_filled, 2 * h + c + 1)
                    part = xres[:, q, c * 512:(c + 1) * 512]
                    nc.vector.tensor_tensor(part, part, bankT[2 + c][:, :], ALU.add).then_inc(bk_read, 1)
                for c in range(2):
                    dve.wait_ge(bk_read, 2 * h + c + 1)
                    nc.vector.bn_stats(out=stats2[:, c, :], in_=xres[:, q, c * 512:(c + 1) * 512]).then_inc(bn2_step, 1)
                wait_on_cell(nc, cell[:, :], dve, bn2_step, 3 * h + 2)
                nc.vector.bn_aggr(out=mv2[:, 0:2], in_=stats2[:, :, :]).then_inc(bn2_step, 1)
                dve.wait_ge(bn2_step, 3 * h + 3)
                nc.vector.tensor_scalar(veps[:, 1:2], mv2[:, 1:2], LN_EPS, None, ALU.add).then_inc(veps2_done, 1)

            def largest(h, q):
                dve.wait_ge(rstd2_done, h + 1)
                nc.vector.tensor_scalar(zn[:, :], xres[:, q, :], mv2[:, 0:1], mv2[:, 1:2], ALU.subtract, ALU.mult).then_inc(zn_done, 1)
                nc.vector.tensor_copy(moments[:, h, :], mv2[:, 0:2])
                dve.wait_ge(zn_done, h + 1)
                nc.vector.tensor_reduce(absmax[:, bass.ds(h, 1)], zn[:, :], axis=AX_X, op=ALU.max, apply_absolute_value=True)

            normalise(0, 0)
            normalise_end(0, 0)
            product(0, 0, 0)
            for c in range(NL):
                if c + 1 < NL:
                    product(0, 0, c + 1)
                low(0, 0, c)

            normalise(1, 1)
            normalise_end(1, 1)

            def channel(h, pair, q, has_prev, has_next, ahead):
                c = 0
                for a in range(NL):
                    if has_next and a >= 2:
                        for _ in range(2 if a in (4, 5) else 1):
                            product(h + 1, 1 - q, c)
                            if c:
                                low(h + 1, 1 - q, c - 1)
                            c += 1
                        if a == NL - 1:
                            low(h + 1, 1 - q, NL - 1)
                    if a == 3 and has_prev:
                        add_result(h - 1, 1 - q)
                    if a == 4 and ahead:
                        normalise(h + 2, q)
                    if a == 5 and has_prev:
                        largest(h - 1, 1 - q)
                    if a == 6 and ahead:
                        normalise_end(h + 2, q)
                    gate(h, q, a)

            channel_loop(dve, nh, channel)
            add_result(nh - 1, (nh - 1) % 2)
            largest(nh - 1, (nh - 1) % 2)


def channel_loop(eng, n, body):
    for q in range(2):
        body(q, 0, q, q > 0, True, True)
    if n > 4:
        with eng.Fori(1, n // 2 - 1) as pair:
            for q in range(2):
                body(pair * 2 + q, pair, q, True, True, True)
    for q in range(2):
        body(n - 2 + q, n // 2 - 1, q, True, q == 0, False)


def pair_count(h, q):
    return (h - q) * 8 + 16


def ffn_phase(nc, x2, w_rows, w_in, weight_scale, bias, ident_in, absmax, moments, out, nt):
    NT3 = 3
    with ExitStack() as ctx:
        def sb(name, shape, dt=F32):
            return ctx.enter_context(nc.sbuf_tensor(name, shape, dt))

        def sem(name):
            return ctx.enter_context(nc.semaphore(name))

        ident = sb("g_ident", [P, P])
        ident16 = sb("g_ident16", [P, P], F16)
        ones = sb("g_ones", [1, P])
        w_hi = sb("g_w_hi", [P, ND, D], F16)
        w_lo = sb("g_w_lo", [P, ND, D], F16)
        wscale = sb("g_wscale", [P, 2])
        bias_all = sb("g_bias", [P, D])
        top = sb("g_top", [P, 1])
        row = sb("g_row", [1, P + 4])
        inv = sb("g_inv", [P, 1])
        gain = sb("g_gain", [P, NHC])
        xt = sb("g_xt", [P, 4, D])
        xb = sb("g_xb", [P, 2, D])
        zt = sb("g_zt", [P, 2, D])
        power = sb("g_power", [P, 2, D])
        xq = sb("g_xq", [P, 2, D], F16)
        xqT = sb("g_xqT", [P, 2, ND, P], F16)
        res = sb("g_res", [P, 2, D])

        bank = [ctx.enter_context(nc.psum_tensor(f"g_b{i}", [P, 512], F32)) for i in range(2)]
        bankT = [ctx.enter_context(nc.psum_tensor(f"g_t{i}", [P, ND, P], F16)) for i in range(2)]
        acc = [ctx.enter_context(nc.psum_tensor(f"g_acc{i}", [P, 2, 512], F32)) for i in range(2)]

        const_in = sem("g_const_in")
        w_filled = sem("g_w_filled")
        w_hi_done = sem("g_w_hi_done")
        w_done = sem("g_w_done")
        id16_done = sem("g_id16_done")
        ones_done = sem("g_ones_done")
        ws_done = sem("g_ws_done")
        top_step = sem("g_top_step")
        top_T = sem("g_top_T")
        top_B = sem("g_top_B")
        x_in = [sem(f"g_x_in{i}") for i in range(4)]
        xb_done = sem("g_xb_done")
        z_step = sem("g_z_step")
        sum_step = sem("g_sum_step")
        xq_done = sem("g_xq_done")
        tr_done = sem("g_tr_done")
        xqT_done = sem("g_xqT_done")
        mm_done = sem("g_mm_done")
        res_done = sem("g_res_done")
        stored = [sem(f"g_stored{i}") for i in range(2)]

        block = ctx.enter_context(nc.Block())
        rows_out = out.rearrange("b (h i) d -> h b i d", i=HX)

        @block.sync
        def _(sp):
            sp.dma_start(ident[:, :], ident_in).then_inc(const_in, 16)
            sp.dma_start(wscale[:, 0:1], weight_scale.to_broadcast([P, 1])).then_inc(const_in, 16)
            sp.dma_start(bias_all[:, :], bias.rearrange("(a n) -> a n", a=1).to_broadcast([P, D])).then_inc(const_in, 16)
            for n in range(NT3):
                sp.dma_start(xt[:, n, :], x2[n]).then_inc(x_in[n], 16)

            def tile(n, quad, r):
                if n_static(n) is None or n + NT3 < nt:
                    wait(sp, xb_done, n)
                    wait(sp, xq_done, n)
                    sp.dma_start(xt[:, (r + NT3) % 4, :], x2[n + NT3]).then_inc(x_in[(r + NT3) % 4], 16)
                sp.wait_ge(res_done, n + 1)
                sp.dma_start(rows_out[n], res[:, r % 2, :]).then_inc(stored[r % 2], 16)

            quad_loop(sp, nt, tile)
            for i in range(2):
                sp.wait_ge(stored[i], 16 * (nt // 2))

        @block.gpsimd
        def _(pool):
            nc.gpsimd.memset(ones[:, :], 1.0).then_inc(ones_done, 1)
            pool.wait_ge(const_in, 48)

            def tile(n, quad, r):
                pool.wait_ge(x_in[r], 16 * (quad + 1))
                wait(pool, res_done, n - 1)
                nc.gpsimd.tensor_tensor(xb[:, r % 2, :], xt[:, r, :], bias_all[:, :], ALU.add).then_inc(xb_done, 1)

            quad_loop(pool, nt, tile)

        @block.tensor
        def _(pe):
            pe.wait_ge(const_in, 48)
            pe.wait_ge(w_in, 16)
            for n in range(ND):
                for c in range(2):
                    wait(pe, w_done, 2 * n + c - 1)
                    for k in range(4):
                        m = nc.tensor.transpose(bank[c][:, k * P:(k + 1) * P], w_rows[:, n, (4 * c + k) * P:(4 * c + k + 1) * P], ident[:, :])
                    m.then_inc(w_filled, 1)
            pe.wait_ge(w_done, 2 * ND)
            pe.wait_ge(top_step, 1)
            nc.tensor.matmul(bank[0][0:1, 0:P], top[:, :], ident[:, :], start=True, stop=True).then_inc(top_T, 1)
            pe.wait_ge(top_step, 4)
            pe.wait_ge(ones_done, 1)
            nc.tensor.matmul(bank[1][:, 0:1], ones[0:1, :], row[0:1, P + 2:P + 3], start=True, stop=True).then_inc(top_B, 1)
            pe.wait_ge(id16_done, 1)

            def transposes(n, r):
                pe.wait_ge(xq_done, n + 1)
                wait(pe, xqT_done, n - 1)
                for k in range(ND):
                    m = nc.tensor.transpose(bankT[r % 2][:, k, :], xq[:, r % 2, k * P:(k + 1) * P], ident16[:, :])
                m.then_inc(tr_done, 1)

            transposes(0, 0)

            def tile(n, quad, r):
                if n_static(n) is None or n + 1 < nt:
                    transposes(n + 1, r + 1)
                pe.wait_ge(xqT_done, n + 1)
                wait(pe, res_done, n - 1)
                for k in range(ND):
                    for w in (w_hi, w_lo):
                        for c in range(2):
                            m = nc.tensor.matmul(acc[r % 2][:, c, :], xqT[:, r % 2, k, :], w[:, k, c * 512:(c + 1) * 512],
                                                 start=(k == 0 and w is w_hi), stop=(k == ND - 1 and w is w_lo))
                m.then_inc(mm_done, 1)

            quad_loop(pe, nt, tile)

        @block.scalar
        def _(act):
            act.wait_ge(const_in, 48)
            nc.scalar.activation(wscale[:, 1:2], wscale[:, 0:1], ACT.Copy, scale=W_S).then_inc(ws_done, 1)
            nc.scalar.activation(ident16[:, :], ident[:, :], ACT.Copy).then_inc(id16_done, 1)
            act.wait_ge(ws_done, 1)
            for n in range(2 * ND):
                act.wait_ge(w_filled, n + 1)
                dst = w_hi[:, 4 * (n % 2):4 * (n % 2) + 4, (n // 2) * P:(n // 2 + 1) * P]
                nc.scalar.activation(dst, bank[n % 2][:, :].rearrange("p (k e) -> p k e", k=4), ACT.Copy, scale=wscale[:, 1:2]).then_inc(w_hi_done, 1)

            def tile(n, quad, r):
                act.wait_ge(tr_done, n + 1)
                wait(act, mm_done, n - 1)
                nc.scalar.activation(xqT[:, r % 2, :, :], bankT[r % 2][:, :, :], ACT.Copy).then_inc(xqT_done, 1)

            quad_loop(act, nt, tile)

        @block.vector
        def _(dve):
            for n in range(2 * ND):
                dve.wait_ge(w_hi_done, n + 1)
                part = (slice(None), slice(4 * (n % 2), 4 * (n % 2) + 4), slice((n // 2) * P, (n // 2 + 1) * P))
                nc.vector.scalar_tensor_tensor(out=w_lo[part], in0=bank[n % 2][:, :].rearrange("p (k e) -> p k e", k=4), scalar=wscale[:, 1:2],
                                               in1=w_hi[part], op0=ALU.mult, op1=ALU.subtract).then_inc(w_done, 1)
            nc.vector.reduce_max(top[:, :], absmax[:, 0:nt], AX_X).then_inc(top_step, 1)
            dve.wait_ge(top_T, 1)
            nc.vector.reduce_max(row[:, P:P + 1], bank[0][0:1, 0:P], AX_X).then_inc(top_step, 1)
            dve.wait_ge(top_step, 2)
            nc.vector.tensor_scalar(row[:, P + 1:P + 2], row[:, P:P + 1], 1.0 / 448.0, 1e-7, ALU.mult, ALU.max).then_inc(top_step, 1)
            dve.wait_ge(top_step, 3)
            nc.vector.reciprocal(row[:, P + 2:P + 3], row[:, P + 1:P + 2]).then_inc(top_step, 1)
            dve.wait_ge(top_B, 1)
            nc.vector.tensor_copy(inv[:, :], bank[1][:, 0:1]).then_inc(top_step, 1)
            dve.wait_ge(top_step, 5)
            nc.vector.tensor_scalar(gain[:, 0:nt], moments[:, 0:nt, 1], inv[:, :], None, ALU.mult).then_inc(top_step, 1)
            dve.wait_ge(top_step, 6)

            def quantise(n, quad, r):
                dve.wait_ge(x_in[r], 16 * (quad + 1))
                s = Count(n * 3)
                nc.vector.tensor_scalar(zt[:, r % 2, :], xt[:, r, :], moments[:, n, 0:1], gain[:, bass.ds(n, 1)], ALU.subtract, ALU.mult).then_inc(z_step, 1)
                dve.wait_ge(z_step, s.next() + 1)
                nc.vector.tensor_scalar(power[:, r % 2, :].bitcast(U32), zt[:, r % 2, :].bitcast(U32), 0x7F800000, None, ALU.bitwise_and).then_inc(z_step, 1)
                dve.wait_ge(z_step, s.next() + 1)
                nc.vector.tensor_scalar(power[:, r % 2, :], power[:, r % 2, :], 2.0 ** -6, 1.5 * 2.0 ** 20, ALU.max, ALU.mult).then_inc(z_step, 1)
                dve.wait_ge(z_step, s.next() + 1)
                nc.vector.tensor_tensor(zt[:, r % 2, :], zt[:, r % 2, :], power[:, r % 2, :], ALU.add).then_inc(sum_step, 1)
                dve.wait_ge(sum_step, n + 1)
                wait(dve, tr_done, n - 1)
                nc.vector.tensor_tensor(xq[:, r % 2, :], zt[:, r % 2, :], power[:, r % 2, :], ALU.subtract).then_inc(xq_done, 1)

            quantise(0, 0, 0)
            quantise(1, 0, 1)

            def tile(n, quad, r):
                if n_static(n) is None or n + 2 < nt:
                    quantise(n + 2, quad + (r + 2) // 4, (r + 2) % 4)
                dve.wait_ge(mm_done, n + 1)
                dve.wait_ge(xb_done, n + 1)
                wait(dve, stored[r % 2], 16 * (quad * 2 + r // 2))
                nc.vector.scalar_tensor_tensor(out=res[:, r % 2, :], in0=acc[r % 2][:, :, :].rearrange("p a n -> p (a n)"), scalar=1.0 / W_S,
                                               in1=xb[:, r % 2, :], op0=ALU.mult, op1=ALU.add).then_inc(res_done, 1)

            quad_loop(dve, nt, tile)


def n_static(n):
    return n if isinstance(n, int) else None


def quad_loop(eng, n, body):
    for r in range(4):
        body(r, 0, r)
    if n > 8:
        with eng.Fori(1, n // 4 - 1) as quad:
            for r in range(4):
                body(quad * 4 + r, quad, r)
    for r in range(4):
        body(n - 4 + r, n // 4 - 1, r)


def decoder_layer(nc, x, skip, context, Wq, Wk, Wv, memory, memory_norm, memory_weight, k, weight, weight_scale, bias, ident, out):
    x1 = nc.dram_tensor("x1_rows", [B, S, D], F32).ap()
    x2 = nc.dram_tensor("x2_rows", [NHC, P, D], F32).ap()
    k_pad = nc.dram_tensor("filter_halves", [2, NHC, P + D], F16).ap()
    toeplitz = nc.dram_tensor("toeplitz_halves", [NHC, P, 2, D], F16).ap()
    with (
        nc.sbuf_tensor("absmax", [P, NHC], F32) as absmax,
        nc.semaphore("toe_done") as toe_done,
        nc.sbuf_tensor("moments", [P, NHC, 2], F32) as moments,
    ):
        filter_phase(nc, k, k_pad)
        attention_phase(nc, x, Wq, Wk, Wv, memory, memory_norm, memory_weight, ident, k_pad, toeplitz, toe_done, x1, B)
        with (
            nc.sbuf_tensor("w_rows", [P, ND, D], F32) as w_rows,
            nc.semaphore("w_in") as w_in,
        ):
            conv_phase(nc, x1, context, toeplitz, toe_done, skip, ident, x2, absmax, moments, weight, w_rows, w_in, NHC)
            ffn_phase(nc, x2, w_rows, w_in, weight_scale, bias, ident, absmax, moments, out, NHC)


_INS = ['x', 'fside_S2_0', 'ctx_2048', 'L0_attn_Wq', 'L0_attn_Wk', 'L0_attn_Wv', 'L0_attn_memory', 'L0_attn_memory_norm',
        'L0_attn_memory_weight', 'L0_xattn_k', 'L0_ffn_weight', 'L0_ffn_weight_scale', 'L0_ffn_bias']


def kernel(**inputs):
    import numpy as np
    import concourse.bacc as bacc
    from concourse.bass_utils import run_bass_kernel_spmd

    nc = bacc.Bacc("TRN2", target_bir_lowering=False, num_devices=1)
    arrays, args = {}, []
    for name in _INS:
        a = np.ascontiguousarray(inputs[name])
        if a.ndim == 0:
            a = a.reshape(1, 1)
        arrays[f"in_{name}"] = a
        args.append(nc.dram_tensor(f"in_{name}", a.shape, mybir.dt.from_np(a.dtype), kind="ExternalInput").ap())
    ident = np.eye(P, dtype=np.float32)
    arrays["in_ident"] = ident
    args.append(nc.dram_tensor("in_ident", ident.shape, F32, kind="ExternalInput").ap())
    args.append(nc.dram_tensor("out_0", (B, S, D), F32, kind="ExternalOutput").ap())
    decoder_layer(nc, *args)
    r = run_bass_kernel_spmd(nc, [arrays], core_ids=[0])
    return r.results[0]["out_0"]
```
